# Optimizing a Trainium2 kernel written in Bass

```python
import numpy as np
import jax
import jax.numpy as jnp

def _softmax(x, axis=-1):
    return jax.nn.softmax(x, axis=axis)

def _gelu(x):
    return jax.nn.gelu(x, approximate=True)

def _silu(x):
    return jax.nn.silu(x)

def _sigmoid(x):
    return jax.nn.sigmoid(x)

def _layernorm(x, axis=-1, eps=1e-05):
    m = jnp.mean(x, axis=axis, keepdims=True)
    v = jnp.var(x, axis=axis, keepdims=True)
    return (x - m) / jnp.sqrt(v + eps)

def _scatter_add(tgt, idx, src, axis=0):
    return tgt.at[idx].add(src)

def _segment_sum(src, seg, n):
    return jax.ops.segment_sum(src, seg, n)
kernel_name = 'mk_vit_tower_cls_d1_tok_img256_r4_c904d2'

def setup_inputs(seed: int=0):
    np.random.seed(seed)
    _w = jnp.asarray

    def _rec_inputs():
        import jax
        import jax.numpy as jnp
        _rk = jax.random.key(seed)
        x = -0.0003702 + 0.999946 * jax.random.normal(jax.random.fold_in(_rk, 1), (32, 1, 64, 1000), jnp.float32)
        cls_tok = 0.02 * jax.random.normal(jax.random.fold_in(_rk, 5), (1, 1, 64), jnp.float32)
        return (x, cls_tok)
    x, cls_tok = _rec_inputs()

    def _L0_tok_setup():
        import jax, jax.numpy as jnp
        import numpy as np
        PH, PW = (64, 25)
        SH, SW = (64, 12)

        def _unfold(x, ph, pw, sh, sw):
            B, C, H, W = x.shape
            nh = (H - ph) // sh + 1
            nw = (W - pw) // sw + 1
            rows = jnp.arange(nh)[:, None] * sh + jnp.arange(ph)[None, :]
            cols = jnp.arange(nw)[:, None] * sw + jnp.arange(pw)[None, :]
            p = x[:, :, rows, :]
            p = p[:, :, :, :, cols]
            p = jnp.transpose(p, (0, 2, 4, 1, 3, 5))
            return p.reshape(B, nh * nw, C * ph * pw)
        key = jax.random.key(seed)
        kx, kw = jax.random.split(key, 2)
        x = jax.random.normal(kx, (64, 1, 64, 1000), dtype=jnp.float32)
        in_dim = 1 * PH * PW
        weight = jax.random.normal(kw, (in_dim, 64), dtype=jnp.float32) / np.sqrt(in_dim).astype(np.float32)
        bias = jnp.zeros((64,), dtype=jnp.float32)
        return {'x': x, 'weight': weight, 'bias': bias}
    _L0_tok_all = _L0_tok_setup()
    _L0_tok_in = {k: v for k, v in _L0_tok_all.items() if k in ('weight', 'bias')}
    del _L0_tok_all

    def _L0_attn_setup():
        import jax, jax.numpy as jnp
        import numpy as np
        B, N, C, H = (64, 75, 64, 8)
        STD = 0.02

        def _rel_indices(n):
            d = (jnp.arange(n)[None, :] - jnp.arange(n)[:, None]).astype(jnp.float32)
            return jnp.stack([d, jnp.zeros_like(d), d * d], axis=-1)
        key = jax.random.key(seed)
        ks = jax.random.split(key, 6)
        return {'x': jax.random.normal(ks[0], (B, N, C), jnp.float32), 'Wqk': jax.random.normal(ks[1], (2 * C, C), jnp.float32) * STD, 'Wv': jax.random.normal(ks[2], (C, C), jnp.float32) * STD, 'Wpos': jax.random.normal(ks[3], (H, 3), jnp.float32) * STD, 'bpos': jnp.zeros((H,), jnp.float32), 'Wproj': jax.random.normal(ks[4], (C, C), jnp.float32) * STD, 'bproj': jnp.zeros((C,), jnp.float32), 'gating': jnp.ones((H,), jnp.float32)}
    _L0_attn_all = _L0_attn_setup()
    _L0_attn_in = {k: v for k, v in _L0_attn_all.items() if k in ('Wqk', 'Wv', 'Wpos', 'bpos', 'Wproj', 'bproj', 'gating')}
    del _L0_attn_all

    def _L0_ffn_setup():
        import jax, jax.numpy as jnp
        import numpy as np
        B, T, C = (64, 96, 64)
        NH, NKV = (4, 2)
        HD = C // NH
        NREP = NH // NKV
        NE, TOPK = (8, 2)
        HID = int(8 / 3 * C)
        EPS_RMS = 1e-06

        def _rope_tables(t_len):
            inv_freq = 1.0 / 10000.0 ** (np.arange(0, HD, 2, dtype=np.float32) / HD)
            t = np.arange(t_len, dtype=np.float32)
            freqs = np.outer(t, inv_freq)
            emb = np.concatenate([freqs, freqs], axis=-1)
            return (jnp.asarray(np.cos(emb)), jnp.asarray(np.sin(emb)))

        def _rotate_half(x):
            h = x.shape[-1] // 2
            return jnp.concatenate([-x[..., h:], x[..., :h]], axis=-1)

        def _rmsnorm(v, w):
            return v * jax.lax.rsqrt(jnp.mean(v * v, axis=-1, keepdims=True) + EPS_RMS) * w
        key = jax.random.key(seed)
        ks = jax.random.split(key, 10)
        s = lambda k, shape: jax.random.normal(k, shape, jnp.float32) * 0.02
        return {'x': jax.random.normal(ks[0], (B, T, C), jnp.float32), 'ln1_w': jnp.ones((C,), jnp.float32), 'ln2_w': jnp.ones((C,), jnp.float32), 'wq': s(ks[1], (NH * HD, C)), 'wk': s(ks[2], (NKV * HD, C)), 'wv': s(ks[3], (NKV * HD, C)), 'wo': s(ks[4], (C, C)), 'router_w': s(ks[5], (NE, C)), 'w1': s(ks[6], (NE, HID, C)), 'w2': s(ks[7], (NE, C, HID)), 'w3': s(ks[8], (NE, HID, C))}
    _L0_ffn_all = _L0_ffn_setup()
    _L0_ffn_in = {k: v for k, v in _L0_ffn_all.items() if k in ('ln1_w', 'ln2_w', 'wq', 'wk', 'wv', 'wo', 'router_w', 'w1', 'w2', 'w3')}
    del _L0_ffn_all
    return {'x': x, 'cls_tok': cls_tok, 'L0_tok_weight': _L0_tok_in['weight'], 'L0_tok_bias': _L0_tok_in['bias'], 'L0_attn_Wqk': _L0_attn_in['Wqk'], 'L0_attn_Wv': _L0_attn_in['Wv'], 'L0_attn_Wpos': _L0_attn_in['Wpos'], 'L0_attn_bpos': _L0_attn_in['bpos'], 'L0_attn_Wproj': _L0_attn_in['Wproj'], 'L0_attn_bproj': _L0_attn_in['bproj'], 'L0_attn_gating': _L0_attn_in['gating'], 'L0_ffn_ln1_w': _L0_ffn_in['ln1_w'], 'L0_ffn_ln2_w': _L0_ffn_in['ln2_w'], 'L0_ffn_wq': _L0_ffn_in['wq'], 'L0_ffn_wk': _L0_ffn_in['wk'], 'L0_ffn_wv': _L0_ffn_in['wv'], 'L0_ffn_wo': _L0_ffn_in['wo'], 'L0_ffn_router_w': _L0_ffn_in['router_w'], 'L0_ffn_w1': _L0_ffn_in['w1'], 'L0_ffn_w2': _L0_ffn_in['w2'], 'L0_ffn_w3': _L0_ffn_in['w3']}

def reference(x, cls_tok, L0_tok_weight, L0_tok_bias, L0_attn_Wqk, L0_attn_Wv, L0_attn_Wpos, L0_attn_bpos, L0_attn_Wproj, L0_attn_bproj, L0_attn_gating, L0_ffn_ln1_w, L0_ffn_ln2_w, L0_ffn_wq, L0_ffn_wk, L0_ffn_wv, L0_ffn_wo, L0_ffn_router_w, L0_ffn_w1, L0_ffn_w2, L0_ffn_w3):
    import jax
    import jax.numpy as jnp

    def _L0_tok_ref(x, weight, bias):
        import jax, jax.numpy as jnp
        import numpy as np
        PH, PW = (64, 25)
        SH, SW = (64, 12)

        def _unfold(x, ph, pw, sh, sw):
            B, C, H, W = x.shape
            nh = (H - ph) // sh + 1
            nw = (W - pw) // sw + 1
            rows = jnp.arange(nh)[:, None] * sh + jnp.arange(ph)[None, :]
            cols = jnp.arange(nw)[:, None] * sw + jnp.arange(pw)[None, :]
            p = x[:, :, rows, :]
            p = p[:, :, :, :, cols]
            p = jnp.transpose(p, (0, 2, 4, 1, 3, 5))
            return p.reshape(B, nh * nw, C * ph * pw)
        p = _unfold(x, PH, PW, SH, SW)
        return jax.nn.gelu(jnp.einsum('bnk,kd->bnd', p, weight) + bias, approximate=False)

    def _L0_attn_ref(x, Wqk, Wv, Wpos, bpos, Wproj, bproj, gating):
        import jax, jax.numpy as jnp
        import numpy as np
        B, N, C, H = (64, 75, 64, 8)
        STD = 0.02

        def _rel_indices(n):
            d = (jnp.arange(n)[None, :] - jnp.arange(n)[:, None]).astype(jnp.float32)
            return jnp.stack([d, jnp.zeros_like(d), d * d], axis=-1)
        Bb, Nn, Cc = x.shape
        Hh = gating.shape[0]
        hd = Cc // Hh
        scale = hd ** (-0.5)
        qk = (x @ Wqk.T).reshape(Bb, Nn, 2, Hh, hd)
        q = qk[:, :, 0].transpose(0, 2, 1, 3)
        k = qk[:, :, 1].transpose(0, 2, 1, 3)
        patch_score = jax.nn.softmax(jnp.einsum('bhnd,bhmd->bhnm', q, k) * scale, axis=-1)
        rel = _rel_indices(Nn)
        pos_score = (rel @ Wpos.T + bpos).transpose(2, 0, 1)
        pos_score = jax.nn.softmax(pos_score, axis=-1)
        g = jax.nn.sigmoid(gating)[None, :, None, None]
        attn = (1.0 - g) * patch_score + g * pos_score[None]
        attn = attn / attn.sum(axis=-1, keepdims=True)
        v = (x @ Wv.T).reshape(Bb, Nn, Hh, hd).transpose(0, 2, 1, 3)
        out = jnp.einsum('bhnm,bhmd->bhnd', attn, v)
        out = out.transpose(0, 2, 1, 3).reshape(Bb, Nn, Cc)
        return out @ Wproj.T + bproj

    def _L0_ffn_ref(x, ln1_w, ln2_w, wq, wk, wv, wo, router_w, w1, w2, w3):
        import jax, jax.numpy as jnp
        import numpy as np
        B, T, C = (64, 96, 64)
        NH, NKV = (4, 2)
        HD = C // NH
        NREP = NH // NKV
        NE, TOPK = (8, 2)
        HID = int(8 / 3 * C)
        EPS_RMS = 1e-06

        def _rope_tables(t_len):
            inv_freq = 1.0 / 10000.0 ** (np.arange(0, HD, 2, dtype=np.float32) / HD)
            t = np.arange(t_len, dtype=np.float32)
            freqs = np.outer(t, inv_freq)
            emb = np.concatenate([freqs, freqs], axis=-1)
            return (jnp.asarray(np.cos(emb)), jnp.asarray(np.sin(emb)))

        def _rotate_half(x):
            h = x.shape[-1] // 2
            return jnp.concatenate([-x[..., h:], x[..., :h]], axis=-1)

        def _rmsnorm(v, w):
            return v * jax.lax.rsqrt(jnp.mean(v * v, axis=-1, keepdims=True) + EPS_RMS) * w
        Bx, Tx, Cx = x.shape
        h = _rmsnorm(x, ln1_w)
        q = (h @ wq.T).reshape(Bx, Tx, NH, HD).transpose(0, 2, 1, 3)
        k = (h @ wk.T).reshape(Bx, Tx, NKV, HD).transpose(0, 2, 1, 3)
        v = (h @ wv.T).reshape(Bx, Tx, NKV, HD).transpose(0, 2, 1, 3)
        cos, sin = _rope_tables(Tx)
        cos, sin = (cos[None, None], sin[None, None])
        q = q * cos + _rotate_half(q) * sin
        k = k * cos + _rotate_half(k) * sin
        k = jnp.repeat(k, NREP, axis=1)
        v = jnp.repeat(v, NREP, axis=1)
        scores = jnp.einsum('bhtd,bhsd->bhts', q, k) / jnp.sqrt(jnp.float32(HD))
        causal = jnp.tril(jnp.ones((Tx, Tx), dtype=bool))
        scores = jnp.where(causal[None, None], scores, jnp.float32(-1e+30))
        att = jax.nn.softmax(scores, axis=-1)
        y = jnp.einsum('bhts,bhsd->bhtd', att, v).transpose(0, 2, 1, 3).reshape(Bx, Tx, Cx)
        x = x + y @ wo.T
        flat = _rmsnorm(x, ln2_w).reshape(-1, Cx)
        probs = jax.nn.softmax(flat @ router_w.T, axis=-1)
        tp, ti = jax.lax.top_k(probs, TOPK)
        tp = tp / (jnp.sum(tp, axis=-1, keepdims=True) + 1e-09)
        weights = jnp.sum(tp[..., None] * jax.nn.one_hot(ti, NE, dtype=flat.dtype), axis=1)
        out = jnp.zeros_like(flat)
        for e in range(NE):
            hh = jax.nn.silu(flat @ w1[e].T) * (flat @ w3[e].T)
            out = out + weights[:, e:e + 1] * (hh @ w2[e].T)
        return x + out.reshape(Bx, Tx, Cx)
    h = _L0_tok_ref(x, L0_tok_weight, L0_tok_bias)
    h = jnp.concatenate([jnp.broadcast_to(cls_tok, (h.shape[0], 1, h.shape[2])), h], axis=1)
    h = h + _L0_attn_ref(_layernorm(h, axis=-1), L0_attn_Wqk, L0_attn_Wv, L0_attn_Wpos, L0_attn_bpos, L0_attn_Wproj, L0_attn_bproj, L0_attn_gating)
    h = h + _L0_ffn_ref(_layernorm(h, axis=-1), L0_ffn_ln1_w, L0_ffn_ln2_w, L0_ffn_wq, L0_ffn_wk, L0_ffn_wv, L0_ffn_wo, L0_ffn_router_w, L0_ffn_w1, L0_ffn_w2, L0_ffn_w3)
    return h

_drawn_inputs = setup_inputs


def setup_inputs(seed=0):
    import zlib

    import numpy as np

    out = dict(_drawn_inputs(seed))
    spreads = {'L0_tok_bias': (0.0, 0.1),
     'L0_attn_bpos': (0.0, 0.8),
     'L0_attn_bproj': (0.0, 0.1),
     'L0_attn_gating': (1.0, 0.6),
     'L0_ffn_ln1_w': (1.0, 0.6),
     'L0_ffn_ln2_w': (1.0, 0.6)}
    factors = {'L0_attn_Wqk': 8.0,
     'L0_ffn_wq': 8.0,
     'L0_ffn_wk': 8.0,
     'L0_ffn_wv': 8.0,
     'L0_ffn_wo': 8.0,
     'L0_ffn_router_w': 8.0,
     'L0_ffn_w1': 8.0,
     'L0_ffn_w2': 8.0,
     'L0_ffn_w3': 8.0}
    for name, (base, spread) in spreads.items():
        noise = np.random.default_rng([zlib.crc32(name.encode()), seed]).standard_normal(out[name].shape)
        drawn = base * np.exp(spread * noise) if base else spread * noise
        out[name] = jnp.asarray(drawn.astype(out[name].dtype))
    for name, factor in factors.items():
        out[name] = (out[name] * factor).astype(out[name].dtype)
    return out
```

```python
from contextlib import ExitStack

import numpy as np
import concourse.bass as bass
from concourse import mybir

B, HP, WX = 32, 64, 1000
PW, SW = 25, 12
NP = (WX - PW) // SW + 1
T = NP + 1
TP = T + 1
C = 64
G = 4
NCH = B // G
GT = G * TP
H1, D1 = 8, 8
H2, KV2, D2 = 4, 2, 16
NE, HID = 8, 170
NPAIR = NE // 2
TILES = 12
HT_ROWS = 114
BANK = 512

QK1, V1C, QKV2, ROT2, ROUT, W1C = 0, 512, 576, 704, 800, 808
NSPLIT = W1C + TILES * HT_ROWS
IDENT, FOLD, COSC, SINC, MROW, MCOL, TRI, DIST, HMASK, CEND = 0, 128, 192, 288, 384, 552, 720, 784, 1033, 1036
WPOS, BPOS, GATE, BPROJ, SEND = 0, 24, 32, 40, 104
BPATCH, CLS, LN1W, LN2W, PEND = 0, 1, 2, 3, 4
WPROJ, WOUT, W3C, FEND = 0, 128, 256, 256 + TILES * HT_ROWS

LN_EPS, RMS_EPS = 1e-5, 1e-6
MAGIC = 1597463007.0

EXPERTS_AFTER = {
    "patch": (0,), "tokens": (1,), "project": (2,), "a0": (3,), "a1": (4,), "a2": (5,), "a3": (6,),
    "a4": (7,), "mix": (8,), "project2": (9,), "c0": (10,), "c1": (11, "sum"),
}


def build_program(nc, x, w_patch, w_split, w_full, w2, consts, small, chan, out):
    F = mybir.dt.float32
    R = mybir.dt.float32r
    BF = mybir.dt.bfloat16
    I32 = mybir.dt.int32
    ALU = mybir.AluOpType
    ACT = mybir.ActivationFunctionType
    AX = mybir.AxisListType.X
    ctx = ExitStack()
    with ctx:
        def sb(name, shape, dt=F):
            return ctx.enter_context(nc.sbuf_tensor(name, shape, dt))

        def sem(name):
            return ctx.enter_context(nc.semaphore(name))

        wp = sb("wp", [128, PW, 128])
        ws = sb("ws", [128, NSPLIT])
        wh = sb("wh", [128, NSPLIT], R)
        wl = sb("wl", [128, NSPLIT], R)
        wf = sb("wf", [128, FEND])
        w2s = sb("w2s", [HT_ROWS, TILES, C])
        cs = sb("cs", [128, CEND])
        sm = sb("sm", [128, SEND])
        ch = sb("ch", [128, PEND])
        identb = sb("identb", [128, 128], BF)
        maskb = sb("maskb", [128, 2, 2 * TP], BF)
        ident = cs[:, IDENT:IDENT + 128]
        fold = cs[:, FOLD:FOLD + C]
        pos_a = sb("pos_a", [T, H1, T])
        pos_b = sb("pos_b", [T, H1, T])
        pos_s = sb("pos_s", [T, 6, H1])
        pos_t = sb("pos_t", [128, H1, T])
        one_g, pos_sum = pos_s[:, 4], pos_s[:, 5]
        xs = sb("xs", [128, 2, WX])
        emb = sb("emb", [128, 2, T])
        res = sb("res", [T, G, C])
        resb = sb("resb", [T, G, C])
        bst = sb("bst", [T, G, 6])
        bsum = sb("bsum", [T, G, 4])
        mv = sb("mv", [T, G, 2])
        rsv = sb("rsv", [T, 8])
        rsy = sb("rsy", [T, 8])
        rsa = sb("rsa", [T, 8])
        rsb = sb("rsb", [T, 8])
        yn = sb("yn", [T, G, C])
        ysp = sb("ysp", [T, G, 2, C], R)
        xt = sb("xt", [128, G, TP], R)
        hi = sb("hi", [128, 4, GT], R)
        qk = sb("qk", [128, 4, GT], R)
        qm = sb("qm", [128, 2, TP], R)
        v1 = sb("v1", [128, G, H1, 32])
        v2 = sb("v2", [128, G, KV2, 32])
        pv = sb("pv", [T, H1, G, D1])
        nm = sb("nm", [T, 8])
        mx1 = sb("mx1", [T, 2, 128], R)
        mx2 = sb("mx2", [T, 2, 128], R)
        ex = sb("ex", [128, 2, 2, 4 * TP])
        avt = sb("avt", [128, G, 2 * TP])
        den = sb("den", [T, 4, G, H1])
        y2 = sb("y2", [T, G, C])
        yt = sb("yt", [128, 2, TP])
        h1 = sb("h1", [T, G, C])
        zz = sb("zz", [T, G, C])
        x1 = sb("x1", [T, G, C])
        sq = sb("sq", [T, G, C])
        rr = sb("rr", [T, G, C])
        rp1 = sb("rp1", [T, G, 96])
        rp2 = sb("rp2", [T, G, 96])
        rp = sb("rp", [T, G, 96])
        rph = sb("rph", [T, G, 96], R)
        rs = sb("rs", [T, G, 6, 64], R)
        rt = sb("rt", [T, 8, G, NE])
        cmp1 = sb("cmp1", [T, G, NE, NE])
        cmp2 = sb("cmp2", [T, G, NE, NE])
        rsm = sb("rsm", [T, 4, G])
        fw = sb("fw", [T, G, NE, C])
        xt3 = sb("xt3", [128, G, TP], R)
        fwt = sb("fwt", [128, NPAIR, G, TP])
        th = sb("th", [HT_ROWS, GT])
        gb = sb("gb", [HT_ROWS, 2, GT])
        hid = sb("hid", [HT_ROWS, 4, GT])
        yd = sb("yd", [128, GT])
        ot = sb("ot", [T, G, C])
        pM = ctx.enter_context(nc.psum_tensor("pM", [128, BANK], F))
        pS = ctx.enter_context(nc.psum_tensor("pS", [128, 2, BANK], F))
        pT = ctx.enter_context(nc.psum_tensor("pT", [128, 2, BANK], F))
        pG = ctx.enter_context(nc.psum_tensor("pG", [128, BANK], F))
        pU = ctx.enter_context(nc.psum_tensor("pU", [128, BANK], F))
        pY = ctx.enter_context(nc.psum_tensor("pY", [128, BANK], F))
        quads = [pS[:, 0], pS[:, 1], pT[:, 0], pT[:, 1]]

        ld_w = [sem(f"ld_w{i}") for i in range(8)]
        ld_x = sem("ld_x")
        ot_free = sem("ot_free")
        w_split_done, w_low_done, w_half_done = sem("w_split_done"), sem("w_low_done"), sem("w_half_done")
        zeroed, zeroed_pool, casts = sem("zeroed"), sem("zeroed_pool"), sem("casts")
        pos_pool, pos_dve, pos_act, pos_pe = sem("pos_pool"), sem("pos_dve"), sem("pos_act"), sem("pos_pe")
        patch_done = sem("patch_done")
        emb_done = sem("emb_done")
        tok_done = sem("tok_done")
        res_done = sem("res_done")
        resb_done = sem("resb_done")
        stat = sem("stat")
        stat3 = sem("stat3")
        yn_done = sem("yn_done")
        yh_done, ysp_done = sem("yh_done"), sem("ysp_done")
        xt_ps = sem("xt_ps")
        xt_done = sem("xt_done")
        qk_ps = sem("qk_ps")
        hi_done = sem("hi_done")
        qk_done = sem("qk_done")
        v_ps, v1_done = sem("v_ps"), sem("v1_done")
        pv_ps, pv_done = sem("pv_ps"), sem("pv_done")
        s_ps = sem("s_ps")
        s_half, st_half = sem("s_half"), sem("st_half")
        nm_done = sem("nm_done")
        mh_done = sem("mh_done")
        mx_done = sem("mx_done")
        mt_ps = sem("mt_ps")
        qm_done = sem("qm_done")
        st_ps = sem("st_ps")
        ex_done = sem("ex_done")
        av_ps = sem("av_ps")
        avt_done = sem("avt_done")
        yt_ps = sem("yt_ps")
        mix = sem("mix")
        y2_done = sem("y2_done")
        ytt_ps, ytt_done = sem("ytt_ps"), sem("ytt_done")
        pr_ps = sem("pr_ps")
        h1_done = sem("h1_done")
        z_done = sem("z_done")
        p2_ps = sem("p2_ps")
        rope1 = sem("rope1")
        rope2 = sem("rope2")
        v2_done = sem("v2_done")
        rph_done = sem("rph_done")
        rs_act = sem("rs_act")
        rs_pool = sem("rs_pool")
        rst_ps, rst_done = sem("rst_ps"), sem("rst_done")
        x1_done = sem("x1_done")
        sq_done, rr_done = sem("sq_done"), sem("rr_done")
        lg_ps = sem("lg_ps")
        rt_dve, rt2, rt_exp = sem("rt_dve"), sem("rt2"), sem("rt_exp")
        wt_done = sem("wt_done")
        fw_done = sem("fw_done")
        fwt_ps, fwt_done = sem("fwt_ps"), sem("fwt_done")
        g_ps, u_ps = sem("g_ps"), sem("u_ps")
        th_done = sem("th_done")
        gb_done, hid_done = sem("gb_done"), sem("hid_done")
        down_done = sem("down_done")
        yd_done = sem("yd_done")
        o_ps = sem("o_ps")
        ot_done = sem("ot_done")

        STAT, STAT3, MIX, RT, RT2 = 32, 10, 8, 9, 4

        def bc(ap, shape):
            return ap.broadcast_to(shape)

        block = ctx.enter_context(nc.Block())

        @block.sync
        def _(sp):
            def load_images(c):
                src = x[bass.ds(c * G, G), 0].rearrange("(q b) h t -> (b h) q t", b=2)
                sp.dma_start(xs[:, :, :], src).then_inc(ld_x, 16)

            sp.dma_start(wp[:, :, :], w_patch).then_inc(ld_w[0], 16)
            load_images(0)
            sp.dma_start(cs[:, :], consts).then_inc(ld_w[1], 16)
            sp.dma_start(sm[:, :], small).then_inc(ld_w[2], 16)
            sp.dma_start(ch[:, :], chan).then_inc(ot_free, 16)
            sp.dma_start(ws[:, :], w_split).then_inc(ld_w[4], 16)
            sp.dma_start(wf[:, :], w_full).then_inc(ld_w[5], 16)
            sp.dma_start(w2s[:, :, :], w2).then_inc(ld_w[6], 16)
            sp.wait_ge(patch_done, 1)
            load_images(1)

            def store(c):
                sp.wait_ge(ot_done, c + 1)
                sp.dma_start(out[bass.ds(c * G, G)].rearrange("b t d -> t b d"), ot[:, :, :]).then_inc(ot_free, 16)

            with sp.Fori(1, NCH - 1) as c:
                sp.wait_ge(patch_done, c + 1)
                load_images(c + 1)
                store(c - 1)
            store(NCH - 2)
            store(NCH - 1)
            sp.wait_ge(ot_free, 16 * NCH + 16)

        @block.tensor
        def _(pe):
            def mm(o, l, r, start=True, stop=True):
                return nc.tensor.matmul(o, l, r, start=start, stop=stop)

            def split_mm(o, l, cols, r):
                mm(o, wh[:, cols], r, stop=False)
                return mm(o, wl[:, cols], r, start=False)

            def split_mm_t(o, stacked, cols):
                mm(o, stacked, wh[:, cols], stop=False)
                return mm(o, stacked, wl[:, cols], start=False)

            def to_channels(n, c):
                pe.wait_ge(ysp_done, c * 3 + n)
                for b in range(G):
                    last = nc.tensor.transpose(pM[:, b * TP:b * TP + T],
                                               ysp[:, b].rearrange("p a c -> p (a c)").bitcast(F), ident[0:T, 0:T])
                last.then_inc(xt_ps, 1)

            def project_out(n, c, w):
                pe.wait_ge(y2_done, c * 2 + n)
                for q in range(2):
                    last = nc.tensor.transpose(pM[:, q * TP:q * TP + T],
                                               y2[:, 2 * q:2 * q + 2].rearrange("p b c -> p (b c)"), ident[0:T, 0:T])
                last.then_inc(ytt_ps, 1)
                pe.wait_ge(ytt_done, c * 2 + n)
                for q in range(2):
                    last = mm(pM[0:T, q * 128:q * 128 + 128], yt[:, q, 0:T], wf[:, w:w + 128])
                last.then_inc(pr_ps, 1)

            def scores1(c, b, half):
                if half == 0:
                    pe.wait_ge(qk_done, c * 4 + 4)
                    if b > 0:
                        pe.wait_ge(nm_done, c * 8 + b)
                else:
                    pe.wait_ge(s_half, c * 4 + b + 1)
                for j in (2 * half, 2 * half + 1):
                    for t in range(2):
                        at = (j // 2 * 2 + t) * TP
                        last = mm(pS[0:T, j % 2, at:at + TP], qk[32 * j:32 * j + 32, t, b * TP:b * TP + T],
                                  qk[32 * j:32 * j + 32, 2 + t, b * TP:b * TP + TP])
                last.then_inc(s_ps if half else s_half, 1)

            def scores1_t(c, b, half):
                if half == 0:
                    pe.wait_ge(qm_done, c * 8 + b + 1)
                    if b > 0:
                        pe.wait_ge(ex_done, c * 8 + b)
                else:
                    pe.wait_ge(st_half, c * 4 + b + 1)
                for j in (2 * half, 2 * half + 1):
                    for t in range(2):
                        at = (j // 2 * 2 + t) * TP
                        last = mm(pT[0:T, j % 2, at:at + TP], qk[32 * j:32 * j + 32, 2 + t, b * TP:b * TP + T],
                                  qm[32 * j:32 * j + 32, t, :])
                last.then_inc(st_ps if half else st_half, 1)

            def maxima_t(c, n, mx):
                pe.wait_ge(mx_done, c * 8 + n + 1)
                for t in range(2):
                    last = nc.tensor.transpose(pM[:, t * TP:t * TP + T], mx[:, t].bitcast(F), ident[0:T, 0:T])
                last.then_inc(mt_ps, 1)

            def values1(c, b):
                pe.wait_ge(ex_done, c * 8 + b + 1)
                pe.wait_ge(qm_done, c * 8 + min(b + 2, G))
                for t in range(2):
                    for j in range(4):
                        at = (j // 2 * 2 + t) * TP
                        last = mm(pM[32 * j:32 * j + 32, t * TP:t * TP + TP], v1[:, b, 4 * t + j, :],
                                  ex[:, b % 2, j % 2, at:at + TP])
                last.then_inc(av_ps, 1)

            def scores2(c, b):
                if b == 0:
                    pe.wait_ge(rst_done, c * 3 + 3)
                else:
                    pe.wait_ge(nm_done, c * 8 + G + b)
                for i in range(2):
                    nc.tensor.matmul(pS[0:T, i, 0:2 * TP], identb[0:T, 0:T], maskb[0:T, 0, :], start=True, stop=False,
                                     skip_group_check=True)
                for i in range(2):
                    for t in range(2):
                        last = nc.tensor.matmul(pS[0:T, i, t * TP:t * TP + TP],
                                                qk[64 * i:64 * i + 64, t, b * TP:b * TP + T],
                                                qk[64 * i:64 * i + 64, 2, b * TP:b * TP + TP], start=False, stop=t == 1,
                                                skip_group_check=True)
                last.then_inc(s_ps, 1)

            def scores2_t(c, b):
                pe.wait_ge(qm_done, c * 8 + G + b + 1)
                if b > 0:
                    pe.wait_ge(ex_done, c * 8 + G + b)
                for i in range(2):
                    nc.tensor.matmul(pT[0:T, i, 0:2 * TP], identb[0:T, 0:T], maskb[0:T, 1, :], start=True, stop=False,
                                     skip_group_check=True)
                for i in range(2):
                    for t in range(2):
                        last = nc.tensor.matmul(pT[0:T, i, t * TP:t * TP + TP],
                                                qk[64 * i:64 * i + 64, 2, b * TP:b * TP + T],
                                                qm[64 * i:64 * i + 64, t, :], start=False, stop=t == 1,
                                                skip_group_check=True)
                last.then_inc(st_ps, 1)

            def values2(c, b):
                pe.wait_ge(ex_done, c * 8 + G + b + 1)
                pe.wait_ge(qm_done, c * 8 + G + min(b + 2, G))
                for h in range(H2):
                    i, t = h // 2, h % 2
                    last = mm(pM[32 * h:32 * h + 32, 0:TP], v2[:, b, i, :], ex[:, b % 2, i, t * TP:t * TP + TP])
                last.then_inc(av_ps, 1)

            def token_side(c, experts, first=False):
                if first:
                    pe.wait_ge(ld_w[0], 16)
                pe.wait_ge(ld_x, 16 * c + 16)
                for j in range(PW):
                    last = mm(pM[:, 0:2 * NP], wp[:, j, :], xs[:, :, j:j + SW * (NP - 1) + 1:SW], j == 0, j == PW - 1)
                last.then_inc(patch_done, 1)
                experts("patch")
                pe.wait_ge(emb_done, c + 1)
                if first:
                    pe.wait_ge(casts, 2)
                for q in range(2):
                    last = nc.tensor.transpose(pM[0:T, q * 128:q * 128 + 128], emb[:, q, :], ident)
                last.then_inc(tok_done, 1)
                if first:
                    pe.wait_ge(pos_dve, 7)
                    for h in range(H1):
                        last = nc.tensor.transpose(pS[0:T, h // 4, h % 4 * T:h % 4 * T + T], pos_b[:, h, :],
                                                   ident[0:T, 0:T])
                    last.then_inc(pos_pe, 1)
                experts("tokens")
                pe.wait_ge(res_done, c + 1)
                to_channels(1, c)
                pe.wait_ge(xt_done, c * 3 + 1)
                if first:
                    pe.wait_ge(w_low_done, 3)
                    pe.wait_ge(pos_act, 3)
                for t in range(4):
                    split_mm(quads[t][:, 0:GT], None, slice(QK1 + t * 128, QK1 + t * 128 + 128), 
                             xt[:, :, :].rearrange("p b t -> p (b t)")).then_inc(qk_ps, 1)
                for b in range(G):
                    last = split_mm_t(pM[0:T, b * C:b * C + C], xt[:, b, 0:T], slice(V1C, V1C + C))
                last.then_inc(v_ps, 1)
                experts("project")
                pe.wait_ge(v1_done, c + 1)
                for h in range(H1):
                    last = mm(pM[0:T, h * 32:h * 32 + 32], pos_t[:, h, :], v1[:, :, h, 0:D1])
                last.then_inc(pv_ps, 1)
                for b in range(G + 1):
                    for half in range(2):
                        if b < G:
                            scores1(c, b, half)
                        if b > 0:
                            scores1_t(c, b - 1, half)
                    experts(f"a{b}")
                    if b < G:
                        if b == 0:
                            pe.wait_ge(pv_done, c + 1)
                        elif b > 1:
                            pe.wait_ge(avt_done, c * 8 + b - 1)
                        maxima_t(c, b, mx1)
                    if b > 0:
                        if b == G:
                            pe.wait_ge(avt_done, c * 8 + b - 1)
                        values1(c, b - 1)
                pe.wait_ge(avt_done, c * 8 + G)
                for b in range(G):
                    for t in range(2):
                        last = nc.tensor.transpose(pS[0:T, b // 2, (b % 2) * 256 + t * 128:(b % 2) * 256 + t * 128 + 128],
                                                   avt[:, b, t * TP:t * TP + T], ident)
                last.then_inc(yt_ps, 1)
                experts("mix")
                if first:
                    pe.wait_ge(ld_w[5], 16)
                project_out(1, c, WPROJ)
                pe.wait_ge(h1_done, c + 1)
                to_channels(2, c)
                pe.wait_ge(xt_done, c * 3 + 2)
                for b in range(G):
                    last = split_mm_t(pS[0:T, 0, b * 128:b * 128 + 128], xt[:, b, 0:T], slice(QKV2, QKV2 + 128))
                last.then_inc(p2_ps, 1)
                for b in range(G):
                    last = split_mm_t(pS[0:T, 1, b * 96:b * 96 + 96], xt[:, b, 0:T], slice(ROT2, ROT2 + 96))
                last.then_inc(p2_ps, 1)
                experts("project2")
                pe.wait_ge(rs_act, c + 1)
                pe.wait_ge(rs_pool, c + 1)
                for t, o in enumerate((quads[2], quads[3], pM)):
                    for b in range(G):
                        last = nc.tensor.transpose(o[:, b * TP:b * TP + T],
                                                   rs[:, b, 2 * t:2 * t + 2].rearrange("p a c -> p (a c)").bitcast(F),
                                                   ident[0:T, 0:T])
                    last.then_inc(rst_ps, 1)
                for b in range(G + 1):
                    if b < G:
                        scores2(c, b)
                    if b > 0:
                        scores2_t(c, b - 1)
                    experts(f"c{b}")
                    if b < G:
                        if b > 1:
                            pe.wait_ge(avt_done, c * 8 + G + b - 1)
                        maxima_t(c, G + b, mx2)
                    if b > 0:
                        if b == G:
                            pe.wait_ge(avt_done, c * 8 + G + b - 1)
                        values2(c, b - 1)
                pe.wait_ge(avt_done, c * 8 + 2 * G)
                for b in range(G):
                    last = nc.tensor.transpose(pS[0:T, 0, b * 128:b * 128 + 128], avt[:, b, 0:T], ident)
                last.then_inc(yt_ps, 1)
                project_out(2, c, WOUT)
                pe.wait_ge(x1_done, c + 1)
                to_channels(3, c)
                pe.wait_ge(xt_done, c * 3 + 3)
                for b in range(G):
                    last = split_mm_t(pM[0:T, b * NE:b * NE + NE], xt3[:, b, 0:T], slice(ROUT, ROUT + NE))
                last.then_inc(lg_ps, 1)
                pe.wait_ge(fw_done, c + 1)
                for p in range(NPAIR):
                    for b in range(G):
                        last = nc.tensor.transpose(quads[p][:, b * TP:b * TP + T],
                                                   fw[:, b, 2 * p:2 * p + 2].rearrange("p e c -> p (e c)"),
                                                   ident[0:T, 0:T])
                    last.then_inc(fwt_ps, 1)

            def down(c, k, last_pair):
                pe.wait_ge(hid_done, c * TILES + k + 2)
                for n in (k, k + 1):
                    r0 = 64 * (n % 2)
                    last = nc.tensor.matmul(pY[r0:r0 + C, 0:GT], w2s[:, n, :], hid[:, n % 4, :],
                                            start=k == 0, stop=last_pair, skip_group_check=True)
                last.then_inc(down_done, 1)

            def expert_tile(c, k):
                if k == "sum":
                    down(c, TILES - 2, True)
                    pe.wait_ge(yd_done, c + 1)
                    for b in range(G):
                        last = mm(pG[0:T, b * C:b * C + C], yd[:, b * TP:b * TP + T], fold)
                    last.then_inc(o_ps, 1)
                    return
                if k == 0:
                    pe.wait_ge(fwt_done, c * 4 + 4)
                else:
                    pe.wait_ge(gb_done, c * TILES + k)
                cols = slice(W1C + k * HT_ROWS, W1C + k * HT_ROWS + HT_ROWS)
                split_mm(pG[0:HT_ROWS, 0:GT], None, cols,
                         xt3[:, :, :].rearrange("p b t -> p (b t)")).then_inc(g_ps, 1)
                if k > 0:
                    pe.wait_ge(hid_done, c * TILES + k)
                mm(pU[0:HT_ROWS, 0:GT], wf[:, W3C + k * HT_ROWS:W3C + k * HT_ROWS + HT_ROWS],
                   fwt[:, k // 3].rearrange("p b t -> p (b t)")).then_inc(u_ps, 1)
                if k >= 2 and k % 2 == 0:
                    down(c, k - 2, False)

            token_side(0, lambda step: None, first=True)
            pe.wait_ge(w_half_done, 2)
            with pe.Fori(1, NCH) as c:
                def experts(step):
                    for k in EXPERTS_AFTER.get(step, ()):
                        expert_tile(c - 1, k)
                token_side(c, experts)
            for k in (*range(TILES), "sum"):
                expert_tile(NCH - 1, k)

        @block.scalar
        def _(act):
            def copy(o, i):
                return nc.scalar.activation(o, i, ACT.Copy)

            def highs(n, c):
                act.wait_ge(yn_done, c * 3 + n)
                copy(ysp[:, :, 0], yn[:, :, :]).then_inc(yh_done, 1)

            def stacked(n, c, dst):
                act.wait_ge(xt_ps, c * 3 + n)
                copy(dst[:, :, 0:T], pM[:, 0:GT].rearrange("p (b t) -> p b t", b=G)[:, :, 0:T]).then_inc(xt_done, 1)

            def mixed(n, c):
                act.wait_ge(ytt_ps, c * 2 + n)
                copy(yt[:, :, 0:T], pM[:, 0:2 * TP].rearrange("p (q t) -> p q t", q=2)[:, :, 0:T]).then_inc(ytt_done, 1)

            def exps(c, n, width, scale):
                act.wait_ge(st_ps, c * 8 + n + 1)
                if n >= 2:
                    act.wait_ge(av_ps, c * 8 + n - 1)
                nc.scalar.activation(ex[0:T, n % 2, :, 0:width], pT[0:T, :, 0:width], ACT.Exp,
                                     scale=scale).then_inc(ex_done, 1)

            def values(c, n, width):
                act.wait_ge(av_ps, c * 8 + n + 1)
                copy(avt[:, n % G, 0:width], pM[:, 0:width]).then_inc(avt_done, 1)

            def token_side(c, experts, first=False):
                act.wait_ge(patch_done, c + 1)
                if first:
                    act.wait_ge(ot_free, 16)
                nc.scalar.activation(emb[:, :, 1:T], pM[:, 0:2 * NP].rearrange("p (q n) -> p q n", q=2), ACT.Gelu,
                                     bias=ch[:, BPATCH:BPATCH + 1]).then_inc(emb_done, 1)
                if first:
                    highs(1, c)
                    positional()
                experts("patch")
                if not first:
                    highs(1, c)
                experts("tokens")
                if first:
                    act.wait_ge(zeroed, 1)
                stacked(1, c, xt)
                for t in range(4):
                    act.wait_ge(qk_ps, c * 4 + t + 1)
                    nc.scalar.activation(hi[:, t], quads[t][:, 0:GT], ACT.Identity,
                                         bias=cs[:, HMASK + 2:HMASK + 3] if t >= 2 else 0.0).then_inc(hi_done, 1)
                experts("project")
                act.wait_ge(pv_ps, c + 1)
                copy(pv[:, :, :, :].rearrange("p h b d -> p (h b d)"), pM[0:T, 0:G * C]).then_inc(pv_done, 1)
                for b in range(G + 1):
                    if b > 0:
                        exps(c, b - 1, 4 * TP, D1 ** -0.5)
                    experts(f"a{b}")
                    if b > 0:
                        values(c, b - 1, 2 * TP)
                experts("mix")
                mixed(1, c)
                highs(2, c)
                stacked(2, c, xt)
                experts("project2")
                act.wait_ge(rope1, c * 2 + 2)
                copy(v2[0:T, :, :, 0:D2],
                     pS[0:T, 0].rearrange("p (b n) -> p b n", b=G)[:, :, 96:128]
                     .rearrange("p b (k d) -> p b k d", k=KV2)).then_inc(v2_done, 1)
                act.wait_ge(rope2, c + 1)
                heads = rp[:, :, :].rearrange("p b (h d) -> p b h d", d=D2)
                copy(rph[:, :, :], rp[:, :, :]).then_inc(rph_done, 1)
                copy(rs[:, :, :, 0:16], heads)
                copy(rs[:, :, 0:4, 32:48], heads[:, :, 0:4])
                copy(rs[:, :, 4:6, 16:32], heads[:, :, 4:6]).then_inc(rs_act, 1)
                for t, o in enumerate((quads[2], quads[3], pM)):
                    act.wait_ge(rst_ps, c * 3 + t + 1)
                    copy(qk[:, t].rearrange("p (b t) -> p b t", b=G)[:, :, 0:T],
                         o[:, 0:GT].rearrange("p (b t) -> p b t", b=G)[:, :, 0:T]).then_inc(rst_done, 1)
                for b in range(G + 1):
                    if b > 0:
                        exps(c, G + b - 1, 2 * TP, D2 ** -0.5)
                    experts(f"c{b}")
                    if b > 0:
                        values(c, G + b - 1, TP)
                mixed(2, c)
                highs(3, c)
                stacked(3, c, xt3)
                act.wait_ge(rt_dve, c * RT + 2)
                nc.scalar.activation(rt[:, 1], rt[:, 0], ACT.Exp).then_inc(rt_exp, 1)
                for p in range(NPAIR):
                    act.wait_ge(fwt_ps, c * 4 + p + 1)
                    copy(fwt[:, p, :, 0:T], quads[p][:, 0:GT].rearrange("p (b t) -> p b t", b=G)[:, :, 0:T])\
                        .then_inc(fwt_done, 1)

            def positional():
                act.wait_ge(ld_w[2], 16)
                nc.scalar.activation(pos_s[:, 3], sm[0:T, GATE:GATE + H1], ACT.Exp, scale=-1.0).then_inc(pos_act, 1)
                act.wait_ge(pos_pool, 7)
                nc.scalar.activation(pos_a[:, :, :], pos_b[:, :, :], ACT.Exp).then_inc(pos_act, 1)
                act.wait_ge(pos_pe, 1)
                act.wait_ge(zeroed, 1)
                copy(pos_t[0:T, :, :].rearrange("p (a h) t -> p a h t", a=2),
                     pS[0:T, :, 0:4 * T].rearrange("p a (h t) -> p a h t", h=4)).then_inc(pos_act, 1)

            def expert_tile(c, k):
                if k == "sum":
                    act.wait_ge(down_done, c * 6 + 6)
                    copy(yd[:, :], pY[:, 0:GT]).then_inc(yd_done, 1)
                    return
                act.wait_ge(g_ps, c * TILES + k + 1)
                if k > 0:
                    act.wait_ge(gb_done, c * TILES + k)
                nc.scalar.activation(th[:, :], pG[0:HT_ROWS, 0:GT], ACT.Tanh, scale=0.5).then_inc(th_done, 1)

            token_side(0, lambda step: None, first=True)
            with act.Fori(1, NCH) as c:
                def experts(step):
                    for k in EXPERTS_AFTER.get(step, ()):
                        expert_tile(c - 1, k)
                token_side(c, experts)
            for k in (*range(TILES), "sum"):
                expert_tile(NCH - 1, k)

        @block.vector
        def _(dve):
            V = nc.vector

            def moments(c, base, src):
                for b in range(G):
                    last = V.bn_stats(bst[:, b, :], src[:, b, :])
                last.then_inc(stat, 1)
                dve.wait_ge(stat, c * STAT + base + 1)
                V.tensor_tensor(bsum[:, :, 0:2], bst[:, :, 1:3], bst[:, :, 4:6], ALU.add)
                V.tensor_tensor(bsum[:, :, 2], bst[:, :, 1], bst[:, :, 4], ALU.subtract).then_inc(stat, 1)
                dve.wait_ge(stat, c * STAT + base + 2)
                V.scalar_tensor_tensor(bsum[:, :, 3], bsum[:, :, 2], 0.25, bsum[:, :, 2], ALU.mult, ALU.mult)
                V.tensor_scalar(mv[:, :, 0], bsum[:, :, 0], 0.5, None, ALU.mult).then_inc(stat, 1)
                dve.wait_ge(stat, c * STAT + base + 3)
                V.scalar_tensor_tensor(mv[:, :, 1], bsum[:, :, 1], 1.0 / C, bsum[:, :, 3], ALU.mult,
                                       ALU.add).then_inc(stat, 1)
                dve.wait_ge(stat, c * STAT + base + 4)

            def rsqrt(c, base, n):
                v, y, a, b = (t[:, 0:n] for t in (rsv, rsy, rsa, rsb))
                V.tensor_scalar(y.bitcast(I32), v.bitcast(I32), -0.5, MAGIC, ALU.mult, ALU.add).then_inc(stat, 1)
                dve.wait_ge(stat, c * STAT + base + 1)
                for i in range(3):
                    V.tensor_tensor(a, y, y, ALU.mult).then_inc(stat, 1)
                    dve.wait_ge(stat, c * STAT + base + 3 * i + 2)
                    V.scalar_tensor_tensor(b, a, -0.5, v, ALU.mult, ALU.mult).then_inc(stat, 1)
                    dve.wait_ge(stat, c * STAT + base + 3 * i + 3)
                    V.scalar_tensor_tensor(y, b, 1.5, y, ALU.add, ALU.mult).then_inc(stat, 1)
                    dve.wait_ge(stat, c * STAT + base + 3 * i + 4)

            def center(dst, src, rstd):
                for b in range(G):
                    last = V.tensor_scalar(dst[:, b, :], src[:, b, :], mv[:, b, 0:1], rstd[:, b:b + 1],
                                           ALU.subtract, ALU.mult)
                return last

            def maxima(c, n, scores, heads_hi, heads_lo, nh):
                dve.wait_ge(s_ps, c * 8 + n + 1)
                V.tensor_reduce(nm[:, 0:nh], scores, AX, ALU.max, negate=True).then_inc(nm_done, 1)
                dve.wait_ge(nm_done, c * 8 + n + 1)
                V.tensor_copy(heads_hi, nm[:, 0:nh].rearrange("p (a b t) -> p a b t", a=2, t=2)).then_inc(mh_done, 1)
                dve.wait_ge(mh_done, c * 8 + n + 1)
                V.tensor_tensor(heads_lo, nm[:, 0:nh].rearrange("p (a b t) -> p a b t", a=2, t=2),
                                heads_hi.bitcast(F), ALU.subtract).then_inc(mx_done, 1)

            def shifted(c, n, b):
                dve.wait_ge(mt_ps, c * 8 + n + 1)
                if n > 0:
                    dve.wait_ge(st_ps, c * 8 + n)
                V.tensor_tensor(qm[:, :, 0:T], pM[:, 0:2 * TP].rearrange("p (a t) -> p a t", a=2)[:, :, 0:T],
                                qk[:, 0:2, b * TP:b * TP + T].bitcast(F), ALU.add).then_inc(qm_done, 1)

            m1 = mx1[:, :, :].rearrange("p t (j2 bk r) -> p bk j2 t r", j2=2, bk=2)
            m2 = mx2[:, :, :].rearrange("p t (a i r) -> p i a t r", i=2, a=1)

            def token_side(c, experts, first=False):
                experts("patch")
                dve.wait_ge(tok_done, c + 1)
                V.tensor_copy(res[:, :, :].rearrange("p b c -> p (b c)"), pM[0:T, 0:G * C]).then_inc(res_done, 1)
                dve.wait_ge(res_done, c + 1)
                moments(c, 0, res)
                V.tensor_scalar(rsv[:, 0:G], mv[:, :, 1], LN_EPS, None, ALU.add).then_inc(stat, 1)
                dve.wait_ge(stat, c * STAT + 5)
                rsqrt(c, 5, G)
                center(yn, res, rsy).then_inc(yn_done, 1)
                experts("tokens")
                if first:
                    setup()
                for t in range(4):
                    dve.wait_ge(hi_done, c * 4 + t + 1)
                    mask = cs[:, HMASK + t // 2:HMASK + t // 2 + 1]
                    V.scalar_tensor_tensor(qk[:, t], hi[:, t].bitcast(F), mask, quads[t][:, 0:GT], ALU.mult,
                                           ALU.add).then_inc(qk_done, 1)
                dve.wait_ge(v_ps, c + 1)
                V.tensor_copy(v1[0:T, :, :, 0:D1],
                              pM[0:T, 0:G * C].rearrange("p (b h d) -> p b h d", b=G, h=H1)).then_inc(v1_done, 1)
                experts("project")
                for b in range(G + 1):
                    if b < G:
                        maxima(c, b, pS[0:T, :, 0:4 * TP].rearrange("p a (s t) -> p a s t", t=TP)[:, :, :, 0:T],
                               m1[:, :, :, :, 24], m1[:, :, :, :, 25], 8)
                    experts(f"a{b}")
                    if b < G:
                        shifted(c, b, b)
                dve.wait_ge(yt_ps, c * 2 + 1)
                tok = pS[0:T, :, :].rearrange("p a n -> p (a n)").rearrange("p (b h r) -> p b h r", b=G, h=H1)
                s = [den[:, i] for i in range(4)]
                k = c * MIX
                V.reciprocal(s[0], tok[:, :, :, D1]).then_inc(mix, 1)
                dve.wait_ge(mix, k + 1)
                V.tensor_tensor(s[1], s[0], bc(one_g.rearrange("p (a h) -> p a h", a=1), [T, G, H1]),
                                ALU.mult).then_inc(mix, 1)
                dve.wait_ge(mix, k + 2)
                V.tensor_tensor(s[2], tok[:, :, :, D1], s[1], ALU.mult).then_inc(mix, 1)
                V.tensor_tensor(y2[:, :, :].rearrange("p b (h d) -> p b h d", h=H1), tok[:, :, :, 0:D1],
                                bc(s[1].rearrange("p b (h d) -> p b h d", d=1), [T, G, H1, D1]), ALU.mult).then_inc(mix, 1)
                dve.wait_ge(mix, k + 4)
                V.tensor_tensor(s[3], s[2], bc(pos_sum.rearrange("p (a h) -> p a h", a=1), [T, G, H1]),
                                ALU.add).then_inc(mix, 1)
                dve.wait_ge(pv_done, c + 1)
                y2h = y2[:, :, :].rearrange("p b (h d) -> p b h d", h=H1)
                V.tensor_tensor(y2h, y2h, pv[:, :, :, :].rearrange("p h b d -> p b h d"), ALU.add).then_inc(mix, 1)
                dve.wait_ge(mix, k + 6)
                V.reciprocal(s[2], s[3]).then_inc(mix, 1)
                dve.wait_ge(mix, k + 7)
                V.tensor_tensor(y2h, y2h, bc(s[2].rearrange("p b (h d) -> p b h d", d=1), [T, G, H1, D1]),
                                ALU.mult).then_inc(y2_done, 1)
                experts("mix")
                dve.wait_ge(pr_ps, c * 2 + 1)
                dve.wait_ge(resb_done, c + 1)
                V.tensor_tensor(h1[:, :, :].rearrange("p b c -> p (b c)"), pM[0:T, 0:G * C],
                                resb[:, :, :].rearrange("p b c -> p (b c)"), ALU.add).then_inc(h1_done, 1)
                dve.wait_ge(h1_done, c + 1)
                moments(c, 15, h1)
                V.tensor_scalar(rsv[:, 0:G], mv[:, :, 1], LN_EPS, None, ALU.add)
                V.tensor_scalar(rsv[:, G:2 * G], mv[:, :, 1], 1.0 + RMS_EPS, RMS_EPS * LN_EPS, ALU.mult,
                                ALU.add).then_inc(stat, 1)
                dve.wait_ge(stat, c * STAT + 20)
                rsqrt(c, 20, 2 * G)
                center(yn, h1, rsy[:, G:2 * G]).then_inc(yn_done, 1)
                center(zz, h1, rsy[:, 0:G]).then_inc(z_done, 1)
                dve.wait_ge(p2_ps, c * 2 + 2)
                for src, tab, dst in ((pS[0:T, 0].rearrange("p (b n) -> p b n", b=G)[:, :, 0:96], COSC, rp1),
                                      (pS[0:T, 1, 0:G * 96].rearrange("p (b n) -> p b n", b=G), SINC, rp2)):
                    V.tensor_tensor(dst[:, :, :], src,
                                    bc(cs[0:T, tab:tab + 96].rearrange("p (a n) -> p a n", a=1), [T, G, 96]),
                                    ALU.mult).then_inc(rope1, 1)
                experts("project2")
                for b in range(G + 1):
                    if b < G:
                        maxima(c, G + b, pS[0:T, :, 0:2 * TP].rearrange("p a (s t) -> p a s t", t=TP)[:, :, :, 0:T],
                               m2[:, :, :, :, 48], m2[:, :, :, :, 49], 4)
                    experts(f"c{b}")
                    if b < G:
                        shifted(c, G + b, b)
                dve.wait_ge(yt_ps, c * 2 + 2)
                tok2 = pS[0:T, 0].rearrange("p (b h r) -> p b h r", b=G, h=H2)
                rden = den[:, 0, :, 0:H2]
                V.reciprocal(rden, tok2[:, :, :, D2]).then_inc(mix, 1)
                dve.wait_ge(mix, k + 8)
                V.tensor_tensor(y2[:, :, :].rearrange("p b (h d) -> p b h d", h=H2), tok2[:, :, :, 0:D2],
                                bc(rden.rearrange("p b (h d) -> p b h d", d=1), [T, G, H2, D2]),
                                ALU.mult).then_inc(y2_done, 1)
                dve.wait_ge(pr_ps, c * 2 + 2)
                dve.wait_ge(z_done, c + 1)
                V.tensor_tensor(x1[:, :, :].rearrange("p b c -> p (b c)"), pM[0:T, 0:G * C],
                                zz[:, :, :].rearrange("p b c -> p (b c)"), ALU.add).then_inc(x1_done, 1)
                dve.wait_ge(sq_done, c + 1)
                V.tensor_reduce(rsa[:, 0:G], sq[:, :, :], AX, ALU.add).then_inc(stat, 1)
                dve.wait_ge(stat, c * STAT + 31)
                V.tensor_scalar(rsv[:, 0:G], rsa[:, 0:G], 1.0 / C, RMS_EPS, ALU.mult, ALU.add).then_inc(stat, 1)
                dve.wait_ge(stat, c * STAT + 32)
                rsqrt_last(c)
                V.tensor_tensor(yn[:, :, :], x1[:, :, :], bc(rsy[:, 0:G].rearrange("p (b c) -> p b c", c=1), [T, G, C]),
                                ALU.mult).then_inc(yn_done, 1)
                lg = pM[0:T, 0:G * NE].rearrange("p (b e) -> p b e", b=G)
                k = c * RT
                one = lambda ap: ap.rearrange("p (b e) -> p b e", e=1)
                dve.wait_ge(lg_ps, c + 1)
                V.tensor_reduce(rsm[:, 0], lg, AX, ALU.max).then_inc(rt_dve, 1)
                dve.wait_ge(rt_dve, k + 1)
                V.tensor_tensor(rt[:, 0], lg, bc(one(rsm[:, 0]), [T, G, NE]), ALU.subtract).then_inc(rt_dve, 1)
                dve.wait_ge(rt_exp, c + 1)
                V.tensor_reduce(rsm[:, 1], rt[:, 1], AX, ALU.add).then_inc(rt_dve, 1)
                dve.wait_ge(rt_dve, k + 3)
                V.reciprocal(rsm[:, 2], rsm[:, 1]).then_inc(rt_dve, 1)
                dve.wait_ge(rt_dve, k + 4)
                V.tensor_tensor(rt[:, 2], rt[:, 1], bc(one(rsm[:, 2]), [T, G, NE]), ALU.mult).then_inc(rt_dve, 1)
                dve.wait_ge(rt_dve, k + 5)
                for b in range(G):
                    pe_ = bc(rt[:, 2, b].rearrange("p (e f) -> p e f", f=1), [T, NE, NE])
                    pf_ = bc(rt[:, 2, b].rearrange("p (e f) -> p e f", e=1), [T, NE, NE])
                    V.tensor_tensor(cmp1[:, b], pf_, pe_, ALU.is_gt)
                    last = V.tensor_tensor(cmp2[:, b], pf_, pe_, ALU.is_equal)
                last.then_inc(rt_dve, 1)
                dve.wait_ge(rt_dve, k + 6)
                ff = lambda t: t[:, :, :, :].rearrange("p b e f -> p b (e f)")
                V.tensor_tensor(ff(cmp2), ff(cmp2), bc(cs[0:T, TRI:TRI + 64].rearrange("p (b e) -> p b e", b=1),
                                                       [T, G, 64]), ALU.mult).then_inc(rt_dve, 1)
                dve.wait_ge(rt_dve, k + 7)
                V.tensor_tensor(ff(cmp1), ff(cmp1), ff(cmp2), ALU.add).then_inc(rt_dve, 1)
                dve.wait_ge(rt_dve, k + 8)
                V.tensor_reduce(rt[:, 3], cmp1[:, :, :, :], AX, ALU.add).then_inc(rt_dve, 1)
                dve.wait_ge(rt_dve, k + 9)
                V.scalar_tensor_tensor(rt[:, 4], rt[:, 3], 1.5, rt[:, 2], ALU.is_lt, ALU.mult).then_inc(rt2, 1)
                dve.wait_ge(rt2, c * RT2 + 1)
                V.tensor_reduce(rsm[:, 3], rt[:, 4], AX, ALU.add).then_inc(rt2, 1)
                dve.wait_ge(rt2, c * RT2 + 2)
                V.tensor_scalar(rsm[:, 0], rsm[:, 3], 1e-9, None, ALU.add).then_inc(rt2, 1)
                dve.wait_ge(rt2, c * RT2 + 3)
                V.reciprocal(rsm[:, 1], rsm[:, 0]).then_inc(rt2, 1)
                dve.wait_ge(rt2, c * RT2 + 4)
                V.tensor_tensor(rt[:, 5], rt[:, 4], bc(one(rsm[:, 1]), [T, G, NE]), ALU.mult).then_inc(wt_done, 1)

            def rsqrt_last(c):
                v, y, a, b = (t[:, 0:G] for t in (rsv, rsy, rsa, rsb))
                V.tensor_scalar(y.bitcast(I32), v.bitcast(I32), -0.5, MAGIC, ALU.mult, ALU.add).then_inc(stat3, 1)
                dve.wait_ge(stat3, c * STAT3 + 1)
                for i in range(3):
                    V.tensor_tensor(a, y, y, ALU.mult).then_inc(stat3, 1)
                    dve.wait_ge(stat3, c * STAT3 + 3 * i + 2)
                    V.scalar_tensor_tensor(b, a, -0.5, v, ALU.mult, ALU.mult).then_inc(stat3, 1)
                    dve.wait_ge(stat3, c * STAT3 + 3 * i + 3)
                    V.scalar_tensor_tensor(y, b, 1.5, y, ALU.add, ALU.mult).then_inc(stat3, 1)
                    dve.wait_ge(stat3, c * STAT3 + 3 * i + 4)

            def setup():
                dve.wait_ge(ld_w[4], 16)
                dve.wait_ge(ot_free, 16)
                for a, z, w in ((QK1, QKV2, None), (QKV2, ROUT, LN1W), (ROUT, NSPLIT, LN2W)):
                    scale = 1.0 if w is None else ch[:, w:w + 1]
                    last = V.tensor_scalar(wh[:, a:z], ws[:, a:z], scale, None, ALU.mult)
                last.then_inc(w_split_done, 1)
                dve.wait_ge(w_split_done, 1)
                for a, z, w in ((QK1, QKV2, None), (QKV2, ROUT, LN1W), (ROUT, NSPLIT, LN2W)):
                    scale = 1.0 if w is None else ch[:, w:w + 1]
                    V.scalar_tensor_tensor(wl[:, a:z], ws[:, a:z], scale, wh[:, a:z].bitcast(F), ALU.mult,
                                           ALU.subtract).then_inc(w_low_done, 1)
                dve.wait_ge(pos_act, 1)
                V.tensor_scalar(pos_s[:, 3], pos_s[:, 3], 1.0, None, ALU.add).then_inc(pos_dve, 1)
                dve.wait_ge(pos_dve, 1)
                V.reciprocal(pos_s[:, 3], pos_s[:, 3]).then_inc(pos_dve, 1)
                dve.wait_ge(pos_dve, 2)
                V.tensor_scalar(one_g, pos_s[:, 3], -1.0, 1.0, ALU.mult, ALU.add)
                dve.wait_ge(pos_pool, 6)
                V.tensor_reduce(pos_s[:, 0], pos_a[:, :, :], AX, ALU.max).then_inc(pos_dve, 1)
                dve.wait_ge(pos_act, 2)
                V.tensor_reduce(pos_s[:, 1], pos_a[:, :, :], AX, ALU.add).then_inc(pos_dve, 1)
                dve.wait_ge(pos_dve, 4)
                V.reciprocal(pos_s[:, 2], pos_s[:, 1]).then_inc(pos_dve, 1)
                dve.wait_ge(pos_dve, 5)
                V.tensor_tensor(pos_s[:, 2], pos_s[:, 2], pos_s[:, 3], ALU.mult).then_inc(pos_dve, 1)
                dve.wait_ge(pos_dve, 6)
                V.tensor_tensor(pos_b[:, :, :], pos_a[:, :, :],
                                bc(pos_s[:, 2].rearrange("p (h t) -> p h t", t=1), [T, H1, T]),
                                ALU.mult).then_inc(pos_dve, 1)
                dve.wait_ge(pos_dve, 7)
                V.tensor_reduce(pos_sum, pos_b[:, :, :], AX, ALU.add).then_inc(pos_dve, 1)
                dve.wait_ge(pos_dve, 8)
                dve.wait_ge(ld_w[5], 16)
                dve.wait_ge(ld_w[6], 16)
                V.tensor_scalar(w2s[:, :, :].rearrange("p k c -> p (k c)"), w2s[:, :, :].rearrange("p k c -> p (k c)"),
                                0.5, None, ALU.mult).then_inc(w_half_done, 1)
                V.tensor_scalar(wf[:, W3C:FEND], wf[:, W3C:FEND], ch[:, LN2W:LN2W + 1], None,
                                ALU.mult).then_inc(w_half_done, 1)

            def expert_tile(c, k):
                if k == "sum":
                    dve.wait_ge(o_ps, c + 1)
                    dve.wait_ge(rr_done, c + 1)
                    dve.wait_ge(ot_free, 16 * c + 16)
                    V.tensor_tensor(ot[:, :, :].rearrange("p b c -> p (b c)"), pG[0:T, 0:G * C],
                                    rr[:, :, :].rearrange("p b c -> p (b c)"), ALU.add).then_inc(ot_done, 1)
                    return
                dve.wait_ge(th_done, c * TILES + k + 1)
                V.scalar_tensor_tensor(gb[:, k % 2, :], th[:, :], 1.0, pG[0:HT_ROWS, 0:GT], ALU.add,
                                       ALU.mult).then_inc(gb_done, 1)
                dve.wait_ge(gb_done, c * TILES + k + 1)
                dve.wait_ge(u_ps, c * TILES + k + 1)
                if k >= 4:
                    dve.wait_ge(down_done, c * 6 + k // 2 - 1)
                V.tensor_tensor(hid[:, k % 4, :], gb[:, k % 2, :], pU[0:HT_ROWS, 0:GT], ALU.mult).then_inc(hid_done, 1)

            for t in (xt, xt3, qm):
                V.memset(t[:, :, T:TP].bitcast(F), 0.0)
            V.memset(qk[:, :, :].rearrange("p t (b s) -> p (t b) s", s=TP)[:, :, T:TP].bitcast(F), 0.0)
            V.memset(fwt[:, :, :, T:TP], 0.0)
            V.memset(pos_t[64:128, :, :], 0.0)
            V.memset(mx1[:, :, :].bitcast(F), 0.0)
            V.memset(mx2[:, :, :].bitcast(F), 0.0).then_inc(zeroed, 1)
            dve.wait_ge(zeroed, 1)
            dve.wait_ge(ld_w[1], 16)
            dve.wait_ge(ot_free, 16)
            V.tensor_copy(emb[:, :, 0:1], bc(ch[:, CLS:CLS + 1].rearrange("p (a b) -> p a b", a=1), [128, 2, 1]))
            V.tensor_copy(identb[:, :], ident).then_inc(casts, 1)
            V.tensor_copy(maskb[:, :, :], cs[:, MROW:MROW + 4 * TP].rearrange("p (a t) -> p a t", a=2)).then_inc(casts, 1)

            token_side(0, lambda step: None, first=True)
            with dve.Fori(1, NCH) as c:
                def experts(step):
                    for k in EXPERTS_AFTER.get(step, ()):
                        expert_tile(c - 1, k)
                token_side(c, experts)
            for k in (*range(TILES), "sum"):
                expert_tile(NCH - 1, k)

        @block.gpsimd
        def _(pool):
            P = nc.gpsimd

            def split(n, c):
                pool.wait_ge(yh_done, c * 3 + n)
                P.tensor_tensor(ysp[:, :, 1], yn[:, :, :], ysp[:, :, 0].bitcast(F), ALU.subtract).then_inc(ysp_done, 1)

            def token_side(c, first=False):
                pool.wait_ge(res_done, c + 1)
                P.tensor_tensor(resb[:, :, :], res[:, :, :],
                                bc(sm[0:T, BPROJ:BPROJ + C].rearrange("p (b c) -> p b c", b=1), [T, G, C]),
                                ALU.add).then_inc(resb_done, 1)
                split(1, c)
                split(2, c)
                pool.wait_ge(rope1, c * 2 + 2)
                P.tensor_tensor(rp[:, :, :], rp1[:, :, :], rp2[:, :, :], ALU.add).then_inc(rope2, 1)
                pool.wait_ge(rph_done, c + 1)
                heads = rp[:, :, :].rearrange("p b (h d) -> p b h d", d=D2)
                highs = rph[:, :, :].rearrange("p b (h d) -> p b h d", d=D2).bitcast(F)
                P.tensor_tensor(rs[:, :, 0:4, 16:32], heads[:, :, 0:4], highs[:, :, 0:4], ALU.subtract)
                P.tensor_tensor(rs[:, :, 4:6, 32:48], heads[:, :, 4:6], highs[:, :, 4:6],
                                ALU.subtract).then_inc(rs_pool, 1)
                pool.wait_ge(x1_done, c + 1)
                P.tensor_tensor(sq[:, :, :], x1[:, :, :], x1[:, :, :], ALU.mult).then_inc(sq_done, 1)
                if not first:
                    pool.wait_ge(ot_done, c)
                P.tensor_tensor(rr[:, :, :], x1[:, :, :], h1[:, :, :], ALU.add).then_inc(rr_done, 1)
                split(3, c)
                pool.wait_ge(wt_done, c + 1)
                for b in range(G):
                    last = P.tensor_tensor(fw[:, b], bc(yn[:, b].rearrange("p (e c) -> p e c", e=1), [T, NE, C]),
                                           bc(rt[:, 5, b].rearrange("p (e c) -> p e c", c=1), [T, NE, C]), ALU.mult)
                last.then_inc(fw_done, 1)

            for t in (v1, v2, ex):
                P.memset(t[:, :, :, :], 0.0)
            P.memset(rs[:, :, :, :].bitcast(F), 0.0).then_inc(zeroed_pool, 1)
            pool.wait_ge(zeroed_pool, 1)
            P.memset(v1[0:T, :, :, D1:D1 + 1], 1.0)
            P.memset(v2[0:T, :, :, D2:D2 + 1], 1.0)
            P.memset(rs[:, :, 4:6, 48:50].bitcast(F), 1.0).then_inc(zeroed_pool, 1)
            pool.wait_ge(ld_w[1], 16)
            pool.wait_ge(ld_w[2], 16)
            wpos = sm[0:T, WPOS:WPOS + 24].rearrange("p (h k) -> p h k", k=3)
            dist = cs[0:T, DIST:DIST + 3 * T].rearrange("p (k t) -> p k t", k=3)
            n = 0
            for k in range(3):
                dst = pos_a if k == 0 else pos_b
                P.tensor_tensor(dst[:, :, :], bc(dist[:, k:k + 1], [T, H1, T]), bc(wpos[:, :, k:k + 1], [T, H1, T]),
                                ALU.mult).then_inc(pos_pool, 1)
                n += 1
                pool.wait_ge(pos_pool, n)
                if k > 0:
                    P.tensor_tensor(pos_a[:, :, :], pos_a[:, :, :], pos_b[:, :, :], ALU.add).then_inc(pos_pool, 1)
                    n += 1
                    pool.wait_ge(pos_pool, n)
            P.tensor_tensor(pos_a[:, :, :], pos_a[:, :, :],
                            bc(sm[0:T, BPOS:BPOS + H1].rearrange("p (h t) -> p h t", t=1), [T, H1, T]),
                            ALU.add).then_inc(pos_pool, 1)
            pool.wait_ge(pos_dve, 3)
            P.tensor_tensor(pos_b[:, :, :], pos_a[:, :, :],
                            bc(pos_s[:, 0].rearrange("p (h t) -> p h t", t=1), [T, H1, T]),
                            ALU.subtract).then_inc(pos_pool, 1)
            token_side(0, first=True)
            with pool.Fori(1, NCH) as c:
                token_side(c)


def _split_weights(Wqk, Wv, wq, wk, wv, router_w, w1):
    w = np.zeros((C, NSPLIT), np.float32)
    for t in range(4):
        for j in range(4):
            rows = Wqk[(t // 2) * C + (4 * (t % 2) + j) * D1:][:D1]
            for r in range(3):
                at = QK1 + t * 128 + 32 * j + 8 * r
                w[:, at:at + D1] = rows.T
    w[:, V1C:V1C + C] = Wv.T
    order = (0, 2, 1, 3)
    heads = [wq[h * D2:h * D2 + D2] for h in order] + [wk[:D2], wk[D2:]]
    for n, rows in enumerate(heads):
        w[:, QKV2 + n * D2:QKV2 + n * D2 + D2] = rows.T
        w[:, ROT2 + n * D2:ROT2 + n * D2 + D2] = np.roll(rows, D2 // 2, axis=0).T
    w[:, QKV2 + 96:QKV2 + 128] = wv.T
    w[:, ROUT:ROUT + NE] = router_w.T
    for e in range(NE):
        at = W1C + e // 2 * 3 * HT_ROWS + e % 2 * HID
        w[:, at:at + HID] = w1[e].T
    return np.concatenate([w, w])


def _whole_weights(Wproj, wo, w3):
    f = np.zeros((128, FEND), np.float32)
    for n in range(2):
        f[n * C:n * C + C, WPROJ + n * C:WPROJ + n * C + C] = Wproj.T
        f[n * C:n * C + C, WOUT + n * C:WOUT + n * C + C] = wo.T
    for e in range(NE):
        at = W3C + e // 2 * 3 * HT_ROWS + e % 2 * HID
        f[e % 2 * C:e % 2 * C + C, at:at + HID] = w3[e].T
    return f


def _down_weights(w2):
    d = np.zeros((NPAIR, 3 * HT_ROWS, C), np.float32)
    for e in range(NE):
        d[e // 2, e % 2 * HID:e % 2 * HID + HID] = w2[e].T
    return np.ascontiguousarray(d.reshape(TILES, HT_ROWS, C).transpose(1, 0, 2))


def _patch_weights(weight):
    w = np.zeros((128, PW, 128), np.float32)
    taps = weight.reshape(HP, PW, C)
    for n in range(2):
        w[n * C:n * C + C, :, n * C:n * C + C] = taps
    return w


def _constants():
    k = np.zeros((128, CEND), np.float32)
    k[:, IDENT:IDENT + 128] = np.eye(128)
    k[:, FOLD:FOLD + C] = np.concatenate([np.eye(C)] * 2)
    inv = 1.0 / 10000.0 ** (np.arange(0, D2, 2, dtype=np.float32) / D2)
    freqs = np.outer(np.arange(T, dtype=np.float32), inv)
    cos, sin = np.cos(freqs), np.sin(freqs)
    k[:T, COSC:COSC + 96] = np.tile(np.concatenate([cos, cos], 1), 6)
    k[:T, SINC:SINC + 96] = np.tile(np.concatenate([-sin, sin], 1), 6)
    i = np.arange(TP)
    by_row = np.where(i[None, :] > i[:T, None], -1e30, 0.0)
    by_col = np.pad(np.where(i[None, :T] < i[:T, None], -1e30, 0.0), ((0, 0), (0, 1)))
    k[:T, MROW:MROW + 2 * TP] = np.tile(by_row, 2)
    k[:T, MCOL:MCOL + 2 * TP] = np.tile(by_col, 2)
    e = np.arange(NE)
    k[:, TRI:TRI + NE * NE] = (e[None, :] < e[:, None]).ravel()
    d = (np.arange(T)[None, :] - np.arange(T)[:, None]).astype(np.float32)
    k[:T, DIST:DIST + 3 * T] = np.concatenate([d, np.zeros_like(d), d * d], 1)
    r = np.arange(128) % 32
    k[:, HMASK] = -1.0 * ((r >= 8) & (r < 16))
    k[:, HMASK + 1] = -1.0 * ((r >= 16) & (r < 24)) + ((r == 24) | (r == 25))
    k[:, HMASK + 2] = (r == 24) | (r == 25)
    return k


def kernel(x, cls_tok, L0_tok_weight, L0_tok_bias, L0_attn_Wqk, L0_attn_Wv, L0_attn_Wpos, L0_attn_bpos,
           L0_attn_Wproj, L0_attn_bproj, L0_attn_gating, L0_ffn_ln1_w, L0_ffn_ln2_w, L0_ffn_wq, L0_ffn_wk,
           L0_ffn_wv, L0_ffn_wo, L0_ffn_router_w, L0_ffn_w1, L0_ffn_w2, L0_ffn_w3):
    import concourse.bacc as bacc
    from concourse.bass_utils import run_bass_kernel_spmd

    a = np.asarray
    small = np.concatenate([a(L0_attn_Wpos).ravel(), a(L0_attn_bpos), a(L0_attn_gating), a(L0_attn_bproj)])
    chan = np.stack([a(L0_tok_bias), a(cls_tok).ravel(), a(L0_ffn_ln1_w), a(L0_ffn_ln2_w)], 1)
    arrays = {
        "x": np.ascontiguousarray(a(x)),
        "w_patch": _patch_weights(a(L0_tok_weight)),
        "w_split": _split_weights(*map(a, (L0_attn_Wqk, L0_attn_Wv, L0_ffn_wq, L0_ffn_wk, L0_ffn_wv,
                                           L0_ffn_router_w, L0_ffn_w1))),
        "w_full": _whole_weights(a(L0_attn_Wproj), a(L0_ffn_wo), a(L0_ffn_w3)),
        "w2": _down_weights(a(L0_ffn_w2)),
        "consts": _constants(),
        "small": np.ascontiguousarray(np.broadcast_to(small, (128, SEND))),
        "chan": np.concatenate([chan, chan]),
    }
    nc = bacc.Bacc("TRN2", target_bir_lowering=False, num_devices=1)
    args = [nc.dram_tensor(f"in_{n}", v.shape, mybir.dt.from_np(v.dtype), kind="ExternalInput").ap()
            for n, v in arrays.items()]
    out = nc.dram_tensor("out_0", (B, T, C), mybir.dt.float32, kind="ExternalOutput").ap()
    build_program(nc, *args, out)
    r = run_bass_kernel_spmd(nc, [{f"in_{n}": v for n, v in arrays.items()}], core_ids=[0])
    return r.results[0]["out_0"]
```

```python
from contextlib import ExitStack

import numpy as np
import concourse.bass as bass
from concourse import mybir

B, HP, WX = 32, 64, 1000
PW, SW = 25, 12
NP = (WX - PW) // SW + 1
T = NP + 1
TP = T + 1
C = 64
G = 4
NCH = B // G
GT = G * TP
H1, D1 = 8, 8
H2, KV2, D2 = 4, 2, 16
NE, HID = 8, 170
NPAIR = NE // 2
TILES = 12
HT_ROWS = 114
BANK = 512

QK1, V1C, QKV2, ROT2, ROUT, W1C = 0, 512, 576, 704, 800, 808
NSPLIT = W1C + TILES * HT_ROWS
IDENT, FOLD, COSC, SINC, MROW, MCOL, TRI, DIST, HMASK, CEND = 0, 128, 192, 288, 384, 552, 720, 784, 1033, 1036
WPOS, BPOS, GATE, BPROJ, SEND = 0, 24, 32, 40, 104
BPATCH, CLS, LN1W, LN2W, PEND = 0, 1, 2, 3, 4
WPROJ, WOUT, W3C, FEND = 0, 128, 256, 256 + TILES * HT_ROWS

LN_EPS, RMS_EPS = 1e-5, 1e-6
MAGIC = 1597463007.0

ORDER = (
    ("queries", 0, 0), ("queries", 0, 1), ("values1", 0), ("queries", 0, 2), ("queries", 0, 3),
    ("tile", 3, 6), ("position", 0),
    ("s1", 0, 0, 0), ("s1", 0, 0, 1), ("proj2a", 2), ("tile", 3, 7), ("mt1", 0, 0), ("proj2b", 2),
    ("s1", 0, 1, 0), ("st1", 0, 0, 0), ("s1", 0, 1, 1), ("st1", 0, 0, 1),
    ("patch", -1, 0), ("rms", 2), ("patch", -1, 1), ("patch", -1, 2), ("mt1", 0, 1), ("av1", 0, 0),
    ("s1", 0, 2, 0), ("st1", 0, 1, 0), ("s1", 0, 2, 1), ("st1", 0, 1, 1),
    ("patch", -1, 3), ("patch", -1, 4), ("gelu", -1), ("tile", 3, 8), ("mt1", 0, 2), ("av1", 0, 1), ("tokens", -1),
    ("xt3", 2),
    ("s1", 0, 3, 0), ("st1", 0, 2, 0), ("s1", 0, 3, 1), ("st1", 0, 2, 1),
    ("logits", 2), ("tile", 3, 9), ("mt1", 0, 3), ("av1", 0, 2), ("ln1", -1),
    ("st1", 0, 3, 0), ("st1", 0, 3, 1), ("tile", 3, 10), ("av1", 0, 3),
    ("router", 2), ("tile", 3, 11), ("xt1", -1), ("sum", 3),
    ("rst", 1), ("yt1", 0), ("v2", 1), ("keep_sum", 2), ("keep_h1", 1), ("fwt", 2, 0), ("fwt", 2, 1),
    ("s2", 1, 0), ("proj1a", 0), ("mt2", 1, 0), ("proj1b", 0),
    ("s2", 1, 1), ("st2", 1, 0), ("tile", 2, 0), ("ln2", 0), ("mt2", 1, 1), ("av2", 1, 0),
    ("s2", 1, 2), ("st2", 1, 1), ("tile", 2, 1), ("fwt", 2, 2), ("mt2", 1, 2), ("av2", 1, 1), ("xt2", 0),
    ("s2", 1, 3), ("st2", 1, 2), ("tile", 2, 2), ("p2a", 0), ("mt2", 1, 3), ("av2", 1, 2), ("p2b", 0),
    ("st2", 1, 3), ("tile", 2, 3), ("av2", 1, 3), ("rope", 0), ("fwt", 2, 3),
    ("tile", 2, 4), ("yt2", 1), ("tile", 2, 5),
)
FIRST = min(lag for _, lag, *_ in ORDER)
LOOP_FROM = max(lag for _, lag, *_ in ORDER)
LOOP_TO, LAST = NCH + FIRST, NCH + LOOP_FROM

PM_BEFORE = {
    "patch": (("proj2b", -3), ("position", -1)),
    "tokens": (("patch", 0),),
    "xt1": (("logits", -3), ("tokens", 0)),
    "values1": (("fwt3", -3), ("p2b", -1), ("xt1", 0)),
    "position": (("values1", 0),),
    "proj1a": (("fwt1", -2), ("rst", -1), ("xt1", 1)),
    "proj1b": (("proj1a", 0),),
    "xt2": (("fwt2", -2), ("proj1b", 0)),
    "p2a": (("xt2", 0),),
    "p2b": (("p2a", 0),),
    "rst": (("xt1", 2), ("logits", -1)),
    "proj2a": (("position", 2), ("fwt3", -1)),
    "proj2b": (("proj2a", 0),),
    "xt3": (("tokens", 3), ("proj2b", 0)),
    "logits": (("xt3", 0),),
    "fwt0": (("rst", 1), ("logits", 0)),
    "fwt1": (("fwt0", 0),),
    "fwt2": (("proj1b", 2), ("fwt1", 0)),
    "fwt3": (("p2b", 2), ("fwt2", 0)),
}


def exists(c):
    return not isinstance(c, int) or 0 <= c < NCH


def later(c):
    return not isinstance(c, int) or c > 0


def run_steps(i, steps):
    for step, lag, *args in ORDER:
        if step in steps and exists(i - lag):
            steps[step](i - lag, *args)


def pipeline(engine, steps, setup=None):
    for i in range(FIRST, LOOP_FROM):
        run_steps(i, steps)
        if i == FIRST and setup is not None:
            setup()
    with engine.Fori(LOOP_FROM, LOOP_TO) as i:
        run_steps(i, steps)
    for i in range(LOOP_TO, LAST):
        run_steps(i, steps)


def build_program(nc, x, w_patch, w_split, w_full, w2, consts, small, chan, out):
    F = mybir.dt.float32
    R = mybir.dt.float32r
    BF = mybir.dt.bfloat16
    I32 = mybir.dt.int32
    ALU = mybir.AluOpType
    ACT = mybir.ActivationFunctionType
    AX = mybir.AxisListType.X
    ctx = ExitStack()
    with ctx:
        def sb(name, shape, dt=F):
            return ctx.enter_context(nc.sbuf_tensor(name, shape, dt))

        def sem(name):
            return ctx.enter_context(nc.semaphore(name))

        wp = sb("wp", [128, PW, 128])
        ws = sb("ws", [128, NSPLIT])
        wh = sb("wh", [128, NSPLIT], R)
        wl = sb("wl", [128, NSPLIT], R)
        wf = sb("wf", [128, FEND])
        w2s = sb("w2s", [HT_ROWS, TILES, C])
        cs = sb("cs", [128, CEND])
        sm = sb("sm", [128, SEND])
        ch = sb("ch", [128, PEND])
        identb = sb("identb", [128, 128], BF)
        maskb = sb("maskb", [128, 2, 2 * TP], BF)
        ident = cs[:, IDENT:IDENT + 128]
        fold = cs[:, FOLD:FOLD + C]
        pos_a = sb("pos_a", [T, H1, T])
        pos_b = sb("pos_b", [T, H1, T])
        pos_s = sb("pos_s", [T, 6, H1])
        pos_t = sb("pos_t", [128, H1, T])
        one_g, pos_sum = pos_s[:, 4], pos_s[:, 5]
        xs = sb("xs", [128, 2, WX])
        emb = sb("emb", [128, 2, T])
        res = sb("res", [T, G, C])
        resb = sb("resb", [T, G, C])
        xt1 = sb("xt1", [128, G, TP], R)

        def norm_tiles(name, n):
            return dict(bst=sb(name + "_bst", [T, G, 6]), bsum=sb(name + "_bsum", [T, G, 4]),
                        mv=sb(name + "_mv", [T, G, 2]), v=sb(name + "_v", [T, n]), y=sb(name + "_y", [T, n]),
                        a=sb(name + "_a", [T, n]), b=sb(name + "_b", [T, n]), yn=sb(name + "_yn", [T, G, C]),
                        ysp=sb(name + "_ysp", [T, G, 2, C], R))

        n1, n2, n3 = norm_tiles("ln1", G), norm_tiles("ln2", 2 * G), norm_tiles("rms", G)
        hi = sb("hi", [128, 4, GT], R)
        qk1 = sb("qk1", [128, 4, GT], R)
        qm1 = sb("qm1", [128, 2, TP], R)
        v1 = sb("v1", [128, G, H1, 32])
        pv = sb("pv", [T, H1, G, D1])
        nm1 = sb("nm1", [T, 8])
        mx1 = sb("mx1", [T, 2, 128], R)
        ex1 = sb("ex1", [128, 2, 2, 4 * TP])
        avt1 = sb("avt1", [128, G, 2 * TP])
        den1 = sb("den1", [T, 4, G, H1])
        y2a = sb("y2a", [T, G, C])
        yta = sb("yta", [128, 2, TP])
        h1 = sb("h1", [T, G, C])
        zz = sb("zz", [T, G, C])
        xt2 = sb("xt2", [128, G, TP], R)
        rp1 = sb("rp1", [T, G, 96])
        rp2 = sb("rp2", [T, G, 96])
        rp = sb("rp", [T, G, 96])
        rph = sb("rph", [T, G, 96], R)
        rs = sb("rs", [T, G, 6, 64], R)
        v2n = sb("v2n", [T, G, KV2, D2])
        qk2 = sb("qk2", [128, 3, GT], R)
        qm2 = sb("qm2", [128, 2, TP], R)
        v2 = sb("v2", [128, G, KV2, 32])
        nm2 = sb("nm2", [T, 4])
        mx2 = sb("mx2", [T, 2, 128], R)
        ex2 = sb("ex2", [128, 2, 2, 2 * TP])
        avt2 = sb("avt2", [128, G, TP])
        den2 = sb("den2", [T, G, H2])
        y2b = sb("y2b", [T, G, C])
        ytb = sb("ytb", [128, 2, TP])
        h1k = sb("h1k", [T, G, C])
        zzk = sb("zzk", [T, G, C])
        zero = sb("zero", [T, 1, 1])
        x1 = sb("x1", [T, G, C])
        sq = sb("sq", [T, G, C])
        rr = sb("rr", [T, G, C])
        xt3 = sb("xt3", [128, G, TP], R)
        rt = sb("rt", [T, 8, G, NE])
        cmp1 = sb("cmp1", [T, G, NE, NE])
        cmp2 = sb("cmp2", [T, G, NE, NE])
        rsm = sb("rsm", [T, 4, G])
        fw = sb("fw", [T, G, NE, C])
        xte = sb("xte", [128, G, TP], R)
        fwt = sb("fwt", [128, NPAIR, G, TP])
        th = sb("th", [HT_ROWS, GT])
        gb = sb("gb", [HT_ROWS, 2, GT])
        hid = sb("hid", [HT_ROWS, 4, GT])
        yd = sb("yd", [128, GT])
        ot = sb("ot", [T, G, C])
        pM = ctx.enter_context(nc.psum_tensor("pM", [128, BANK], F))
        pS = ctx.enter_context(nc.psum_tensor("pS", [128, 2, BANK], F))
        pT = ctx.enter_context(nc.psum_tensor("pT", [128, 2, BANK], F))
        pG = ctx.enter_context(nc.psum_tensor("pG", [128, BANK], F))
        pU = ctx.enter_context(nc.psum_tensor("pU", [128, BANK], F))
        pY = ctx.enter_context(nc.psum_tensor("pY", [128, BANK], F))
        quads = [pS[:, 0], pS[:, 1], pT[:, 0], pT[:, 1]]

        ld_w = [sem(f"ld_w{i}") for i in range(8)]
        ld_x = sem("ld_x")
        stored = sem("stored")
        w_split_done, w_low_done, w_half_done = sem("w_split_done"), sem("w_low_done"), sem("w_half_done")
        zeroed, zeroed_pool, casts = sem("zeroed"), sem("zeroed_pool"), sem("casts")
        pos_pool, pos_dve, pos_act, pos_pe = sem("pos_pool"), sem("pos_dve"), sem("pos_act"), sem("pos_pe")
        patch_ps, emb_done = sem("patch_ps"), sem("emb_done")
        tok_ps, res_done = sem("tok_ps"), sem("res_done")
        resb_done = sem("resb_done")
        for n, name, steps in ((n1, "ln1", 15), (n2, "ln2", 15), (n3, "rms", 12)):
            n.update(stat=sem(name + "_stat"), per=steps, yn_done=sem(name + "_yn_done"),
                     yh_done=sem(name + "_yh_done"), ysp_done=sem(name + "_ysp_done"),
                     xt_ps=sem(name + "_xt_ps"), xt_done=sem(name + "_xt_done"))
        qk1_ps, hi_done, qk1_done = sem("qk1_ps"), sem("hi_done"), sem("qk1_done")
        v1_ps, v1_done = sem("v1_ps"), sem("v1_done")
        pv_ps, pv_done = sem("pv_ps"), sem("pv_done")
        s1_half, st1_half = sem("s1_half"), sem("st1_half")

        def attention_semaphores(a):
            return {name: sem(f"{name}{a}") for name in
                    ("s_ps", "nm_done", "mh_done", "mx_done", "mt_ps", "qm_done", "st_ps", "ex_done", "av_ps",
                     "avt_done")}

        a1, a2 = attention_semaphores(1), attention_semaphores(2)
        yt1_ps, mix, y2a_done = sem("yt1_ps"), sem("mix"), sem("y2a_done")
        yta_ps, yta_done = sem("yta_ps"), sem("yta_done")
        pra_ps, h1_done = sem("pra_ps"), sem("h1_done")
        zz_done = sem("zz_done")
        p2a_ps, p2b_ps = sem("p2a_ps"), sem("p2b_ps")
        v2n_done, rpa_done, rpb_done = sem("v2n_done"), sem("rpa_done"), sem("rpb_done")
        rp_done, rph_done = sem("rp_done"), sem("rph_done")
        rs_act, rs_pool = sem("rs_act"), sem("rs_pool")
        rst_ps, rst_done = sem("rst_ps"), sem("rst_done")
        v2_done = sem("v2_done")
        yt2_ps, den2_done, y2b_done = sem("yt2_ps"), sem("den2_done"), sem("y2b_done")
        ytb_ps, ytb_done = sem("ytb_ps"), sem("ytb_done")
        prb_ps, x1_done = sem("prb_ps"), sem("x1_done")
        kept, h1_kept = sem("kept"), sem("h1_kept")
        sq_done, rr_done = sem("sq_done"), sem("rr_done")
        lg_ps = sem("lg_ps")
        rt_dve, rt_exp = sem("rt_dve"), sem("rt_exp")
        wt_done = sem("wt_done")
        fw_done = sem("fw_done")
        fwt_ps, fwt_done = sem("fwt_ps"), sem("fwt_done")
        g_ps, u_ps = sem("g_ps"), sem("u_ps")
        th_done = sem("th_done")
        gb_done, hid_done = sem("gb_done"), sem("hid_done")
        down_done = sem("down_done")
        yd_done = sem("yd_done")
        o_ps = sem("o_ps")
        ot_done = sem("ot_done")

        RT, MIX = 13, 7

        def bc(ap, shape):
            return ap.broadcast_to(shape)

        block = ctx.enter_context(nc.Block())

        @block.sync
        def _(sp):
            def load_images(c):
                src = x[bass.ds(c * G, G), 0].rearrange("(q b) h t -> (b h) q t", b=2)
                sp.dma_start(xs[:, :, :], src).then_inc(ld_x, 16)

            def patch(c, part):
                if part == 0 and later(c):
                    sp.wait_ge(patch_ps, c)
                    load_images(c)

            def store(c):
                sp.wait_ge(ot_done, c + 1)
                sp.dma_start(out[bass.ds(c * G, G)].rearrange("b t d -> t b d"), ot[:, :, :]).then_inc(stored, 16)

            sp.dma_start(cs[:, :], consts).then_inc(ld_w[1], 16)
            sp.dma_start(sm[:, :], small).then_inc(ld_w[2], 16)
            sp.dma_start(ch[:, :], chan).then_inc(ld_w[3], 16)
            sp.dma_start(wp[:, :, :], w_patch).then_inc(ld_w[0], 16)
            load_images(0)
            sp.dma_start(ws[:, :], w_split).then_inc(ld_w[4], 16)
            sp.dma_start(wf[:, :], w_full).then_inc(ld_w[5], 16)
            sp.dma_start(w2s[:, :, :], w2).then_inc(ld_w[6], 16)
            pipeline(sp, {"patch": patch, "sum": store})
            sp.wait_ge(stored, 16 * NCH)

        @block.tensor
        def _(pe):
            def mm(o, l, r, start=True, stop=True):
                return nc.tensor.matmul(o, l, r, start=start, stop=stop)

            def split_mm(o, cols, r):
                mm(o, wh[:, cols], r, stop=False)
                return mm(o, wl[:, cols], r, start=False)

            def split_mm_t(o, stacked, cols):
                mm(o, stacked, wh[:, cols], stop=False)
                return mm(o, stacked, wl[:, cols], start=False)

            pm_readers = {
                "values1": (v1_done, 1, 1), "position": (pv_done, 1, 1), "patch": (emb_done, 1, 1),
                "tokens": (res_done, 1, 1), "xt1": (n1["xt_done"], 1, 1), "proj1a": (yta_done, 1, 1),
                "proj1b": (h1_done, 1, 1), "xt2": (n2["xt_done"], 1, 1), "p2a": (v2n_done, 1, 1),
                "p2b": (rpb_done, 1, 1), "rst": (rst_done, 3, 3), "proj2a": (ytb_done, 1, 1),
                "proj2b": (x1_done, 1, 1), "xt3": (n3["xt_done"], 1, 1), "logits": (rt_dve, RT, 2),
                "fwt0": (fwt_done, 4, 1), "fwt1": (fwt_done, 4, 2), "fwt2": (fwt_done, 4, 3),
                "fwt3": (fwt_done, 4, 4),
            }

            def pm_free(use, c):
                for before, other in PM_BEFORE[use]:
                    if exists(c + other):
                        signal, per, n = pm_readers[before]
                        pe.wait_ge(signal, (c + other) * per + n)
                        return

            def patch(c, part):
                if part == 0:
                    if isinstance(c, int) and c == 0:
                        pe.wait_ge(ld_w[0], 16)
                    pe.wait_ge(ld_x, 16 * c + 16)
                    pm_free("patch", c)
                for j in range(5 * part, 5 * part + 5):
                    last = mm(pM[:, 0:2 * NP], wp[:, j, :], xs[:, :, j:j + SW * (NP - 1) + 1:SW], j == 0, j == PW - 1)
                if part == 4:
                    last.then_inc(patch_ps, 1)

            def tokens(c):
                pe.wait_ge(emb_done, c + 1)
                for q in range(2):
                    last = nc.tensor.transpose(pM[0:T, q * 128:q * 128 + 128], emb[:, q, :], ident)
                last.then_inc(tok_ps, 1)

            def to_channels(name, n):
                def step(c):
                    pm_free(name, c)
                    pe.wait_ge(n["ysp_done"], c + 1)
                    for b in range(G):
                        last = nc.tensor.transpose(pM[:, b * TP:b * TP + T],
                                                   n["ysp"][:, b].rearrange("p a c -> p (a c)").bitcast(F),
                                                   ident[0:T, 0:T])
                    last.then_inc(n["xt_ps"], 1)
                return step

            def queries(c, t):
                pe.wait_ge(n1["xt_done"], c + 1)
                if t < 2:
                    if not isinstance(c, int) or c > 1:
                        pe.wait_ge(y2b_done, c - 1)
                    elif c == 1:
                        pe.wait_ge(y2a_done, c)
                else:
                    if not isinstance(c, int) or c > 1:
                        pe.wait_ge(a2["avt_done"], (c - 1) * G)
                    elif c == 1:
                        pe.wait_ge(a1["avt_done"], G)
                split_mm(quads[t][:, 0:GT], slice(QK1 + t * 128, QK1 + t * 128 + 128),
                         xt1[:, :, :].rearrange("p b t -> p (b t)")).then_inc(qk1_ps, 1)

            def values1(c):
                pm_free("values1", c)
                for b in range(G):
                    last = split_mm_t(pM[0:T, b * C:b * C + C], xt1[:, b, 0:T], slice(V1C, V1C + C))
                last.then_inc(v1_ps, 1)

            def position(c):
                pm_free("position", c)
                pe.wait_ge(v1_done, c + 1)
                for h in range(H1):
                    last = mm(pM[0:T, h * 32:h * 32 + 32], pos_t[:, h, :], v1[:, :, h, 0:D1])
                last.then_inc(pv_ps, 1)

            def s1(c, b, half):
                if half == 0:
                    if b == 0:
                        pe.wait_ge(qk1_done, c * 4 + 4)
                    else:
                        pe.wait_ge(a1["qm_done"], c * G + b)
                else:
                    pe.wait_ge(s1_half, c * G + b + 1)
                for j in (2 * half, 2 * half + 1):
                    for t in range(2):
                        at = (j // 2 * 2 + t) * TP
                        last = mm(pS[0:T, j % 2, at:at + TP], qk1[32 * j:32 * j + 32, t, b * TP:b * TP + T],
                                  qk1[32 * j:32 * j + 32, 2 + t, b * TP:b * TP + TP])
                last.then_inc(a1["s_ps"] if half else s1_half, 1)

            def st1(c, b, half):
                if half == 0:
                    pe.wait_ge(a1["qm_done"], c * G + b + 1)
                    if b > 0:
                        pe.wait_ge(a1["avt_done"], c * G + b)
                else:
                    pe.wait_ge(st1_half, c * G + b + 1)
                for j in (2 * half, 2 * half + 1):
                    for t in range(2):
                        at = (j // 2 * 2 + t) * TP
                        last = mm(pT[0:T, j % 2, at:at + TP], qk1[32 * j:32 * j + 32, 2 + t, b * TP:b * TP + T],
                                  qm1[32 * j:32 * j + 32, t, :])
                last.then_inc(a1["st_ps"] if half else st1_half, 1)

            def maxima_t(a, mx):
                def step(c, b):
                    pe.wait_ge(a["mx_done"], c * G + b + 1)
                    for t in range(2):
                        last = nc.tensor.transpose(pS[:, 0, t * TP:t * TP + T], mx[:, t].bitcast(F), ident[0:T, 0:T])
                    last.then_inc(a["mt_ps"], 1)
                return step

            def av1(c, b):
                pe.wait_ge(a1["ex_done"], c * G + b + 1)
                for t in range(2):
                    for j in range(4):
                        at = (j // 2 * 2 + t) * TP
                        last = mm(pT[32 * j:32 * j + 32, 0, t * TP:t * TP + TP], v1[:, b, 4 * t + j, :],
                                  ex1[:, b % 2, j % 2, at:at + TP])
                last.then_inc(a1["av_ps"], 1)

            def yt1(c):
                pe.wait_ge(a1["avt_done"], c * G + G)
                for b in range(G):
                    for t in range(2):
                        at = (b % 2) * 256 + t * 128
                        last = nc.tensor.transpose(pS[0:T, b // 2, at:at + 128], avt1[:, b, t * TP:t * TP + T], ident)
                last.then_inc(yt1_ps, 1)

            def projection(name, y_done, y, yt_ps, yt, yt_done, pr_ps, w):
                def to_rows(c):
                    pm_free(name + "a", c)
                    pe.wait_ge(y_done, c + 1)
                    for q in range(2):
                        last = nc.tensor.transpose(pM[:, q * TP:q * TP + T],
                                                   y[:, 2 * q:2 * q + 2].rearrange("p b c -> p (b c)"), ident[0:T, 0:T])
                    last.then_inc(yt_ps, 1)

                def project(c):
                    pe.wait_ge(yt_done, c + 1)
                    if isinstance(c, int) and c == 0:
                        pe.wait_ge(ld_w[5], 16)
                    for q in range(2):
                        last = mm(pM[0:T, q * 128:q * 128 + 128], yt[:, q, 0:T], wf[:, w:w + 128])
                    last.then_inc(pr_ps, 1)
                return to_rows, project

            proj1a, proj1b = projection("proj1", y2a_done, y2a, yta_ps, yta, yta_done, pra_ps, WPROJ)
            proj2a, proj2b = projection("proj2", y2b_done, y2b, ytb_ps, ytb, ytb_done, prb_ps, WOUT)

            def p2a(c):
                pe.wait_ge(n2["xt_done"], c + 1)
                pm_free("p2a", c)
                for b in range(G):
                    last = split_mm_t(pM[0:T, b * 128:b * 128 + 128], xt2[:, b, 0:T], slice(QKV2, QKV2 + 128))
                last.then_inc(p2a_ps, 1)

            def p2b(c):
                pm_free("p2b", c)
                for b in range(G):
                    last = split_mm_t(pM[0:T, b * 96:b * 96 + 96], xt2[:, b, 0:T], slice(ROT2, ROT2 + 96))
                last.then_inc(p2b_ps, 1)

            def rst(c):
                pe.wait_ge(rs_act, c + 1)
                pe.wait_ge(rs_pool, c + 1)
                if exists(c + 1):
                    pe.wait_ge(a1["avt_done"], (c + 1) * G + G)
                else:
                    pe.wait_ge(a2["avt_done"], c * G)
                for t, o in enumerate((quads[2], quads[3], pM)):
                    if t == 2:
                        pm_free("rst", c)
                    for b in range(G):
                        last = nc.tensor.transpose(o[:, b * TP:b * TP + T],
                                                   rs[:, b, 2 * t:2 * t + 2].rearrange("p a c -> p (a c)").bitcast(F),
                                                   ident[0:T, 0:T])
                    last.then_inc(rst_ps, 1)

            def s2(c, b):
                if b == 0:
                    pe.wait_ge(rst_done, c * 3 + 3)
                    if exists(c + 1):
                        pe.wait_ge(y2a_done, c + 2)
                    else:
                        pe.wait_ge(y2b_done, c)
                else:
                    pe.wait_ge(a2["qm_done"], c * G + b)
                for i in range(2):
                    nc.tensor.matmul(pS[0:T, i, 0:2 * TP], identb[0:T, 0:T], maskb[0:T, 0, :], start=True, stop=False,
                                     skip_group_check=True)
                for i in range(2):
                    for t in range(2):
                        last = nc.tensor.matmul(pS[0:T, i, t * TP:t * TP + TP],
                                                qk2[64 * i:64 * i + 64, t, b * TP:b * TP + T],
                                                qk2[64 * i:64 * i + 64, 2, b * TP:b * TP + TP], start=False,
                                                stop=t == 1, skip_group_check=True)
                last.then_inc(a2["s_ps"], 1)

            def st2(c, b):
                pe.wait_ge(a2["qm_done"], c * G + b + 1)
                if b > 0:
                    pe.wait_ge(a2["avt_done"], c * G + b)
                for i in range(2):
                    nc.tensor.matmul(pT[0:T, i, 0:2 * TP], identb[0:T, 0:T], maskb[0:T, 1, :], start=True, stop=False,
                                     skip_group_check=True)
                for i in range(2):
                    for t in range(2):
                        last = nc.tensor.matmul(pT[0:T, i, t * TP:t * TP + TP],
                                                qk2[64 * i:64 * i + 64, 2, b * TP:b * TP + T],
                                                qm2[64 * i:64 * i + 64, t, :], start=False, stop=t == 1,
                                                skip_group_check=True)
                last.then_inc(a2["st_ps"], 1)

            def av2(c, b):
                pe.wait_ge(a2["ex_done"], c * G + b + 1)
                if b == 0:
                    pe.wait_ge(v2_done, c + 1)
                for h in range(H2):
                    i, t = h // 2, h % 2
                    last = mm(pT[32 * h:32 * h + 32, 0, 0:TP], v2[:, b, i, :], ex2[:, b % 2, i, t * TP:t * TP + TP])
                last.then_inc(a2["av_ps"], 1)

            def yt2(c):
                pe.wait_ge(a2["avt_done"], c * G + G)
                for b in range(G):
                    last = nc.tensor.transpose(pS[0:T, 0, b * 128:b * 128 + 128], avt2[:, b, 0:T], ident)
                last.then_inc(yt2_ps, 1)

            def logits(c):
                pe.wait_ge(n3["xt_done"], c + 1)
                for b in range(G):
                    last = split_mm_t(pM[0:T, b * NE:b * NE + NE], xt3[:, b, 0:T], slice(ROUT, ROUT + NE))
                last.then_inc(lg_ps, 1)

            def fwt_step(c, p):
                pm_free(f"fwt{p}", c)
                pe.wait_ge(fw_done, c + 1)
                for b in range(G):
                    last = nc.tensor.transpose(pM[:, b * TP:b * TP + T],
                                               fw[:, b, 2 * p:2 * p + 2].rearrange("p e c -> p (e c)"), ident[0:T, 0:T])
                last.then_inc(fwt_ps, 1)

            def down(c, k, last_pair):
                pe.wait_ge(hid_done, c * TILES + k + 2)
                if k == 0 and later(c):
                    pe.wait_ge(yd_done, c)
                for n in (k, k + 1):
                    r0 = 64 * (n % 2)
                    last = nc.tensor.matmul(pY[r0:r0 + C, 0:GT], w2s[:, n, :], hid[:, n % 4, :],
                                            start=k == 0, stop=last_pair, skip_group_check=True)
                last.then_inc(down_done, 1)

            def tile(c, k):
                if k == 0:
                    pe.wait_ge(kept, c + 1)
                    if later(c):
                        pe.wait_ge(ot_done, c)
                    else:
                        pe.wait_ge(w_half_done, 2)
                else:
                    pe.wait_ge(gb_done, c * TILES + k)
                cols = slice(W1C + k * HT_ROWS, W1C + k * HT_ROWS + HT_ROWS)
                split_mm(pG[0:HT_ROWS, 0:GT], cols, xte[:, :, :].rearrange("p b t -> p (b t)")).then_inc(g_ps, 1)
                if k % 3 == 0:
                    pe.wait_ge(fwt_done, c * 4 + k // 3 + 1)
                if k > 0 or later(c):
                    pe.wait_ge(hid_done, c * TILES + k)
                mm(pU[0:HT_ROWS, 0:GT], wf[:, W3C + k * HT_ROWS:W3C + k * HT_ROWS + HT_ROWS],
                   fwt[:, k // 3].rearrange("p b t -> p (b t)")).then_inc(u_ps, 1)
                if k >= 2 and k % 2 == 0:
                    down(c, k - 2, False)

            def expert_sum(c):
                down(c, TILES - 2, True)
                pe.wait_ge(yd_done, c + 1)
                for b in range(G):
                    last = mm(pG[0:T, b * C:b * C + C], yd[:, b * TP:b * TP + T], fold)
                last.then_inc(o_ps, 1)

            pe.wait_ge(ld_w[1], 16)
            pe.wait_ge(pos_dve, 7)
            for h in range(H1):
                last = nc.tensor.transpose(pS[0:T, h // 4, h % 4 * T:h % 4 * T + T], pos_b[:, h, :], ident[0:T, 0:T])
            last.then_inc(pos_pe, 1)

            def start():
                pe.wait_ge(w_low_done, 3)
                pe.wait_ge(pos_act, 3)

            pe.wait_ge(casts, 1)

            pipeline(pe, {
                "patch": patch, "tokens": tokens, "xt1": to_channels("xt1", n1), "queries": queries,
                "values1": values1, "position": position, "s1": s1, "st1": st1, "mt1": maxima_t(a1, mx1),
                "av1": av1, "yt1": yt1, "proj1a": proj1a, "proj1b": proj1b, "xt2": to_channels("xt2", n2),
                "p2a": p2a, "p2b": p2b, "rst": rst, "s2": s2, "st2": st2, "mt2": maxima_t(a2, mx2), "av2": av2,
                "yt2": yt2, "proj2a": proj2a, "proj2b": proj2b, "xt3": to_channels("xt3", n3), "logits": logits,
                "fwt": fwt_step, "tile": tile, "sum": expert_sum}, start)

        @block.scalar
        def _(act):
            def copy(o, i):
                return nc.scalar.activation(o, i, ACT.Copy)

            def gelu(c):
                act.wait_ge(patch_ps, c + 1)
                nc.scalar.activation(emb[:, :, 1:T], pM[:, 0:2 * NP].rearrange("p (q n) -> p q n", q=2), ACT.Gelu,
                                     bias=ch[:, BPATCH:BPATCH + 1]).then_inc(emb_done, 1)

            def highs(n):
                def step(c):
                    act.wait_ge(n["yn_done"], c + 1)
                    copy(n["ysp"][:, :, 0], n["yn"][:, :, :]).then_inc(n["yh_done"], 1)
                return step

            def stacked(n, dst):
                def step(c):
                    act.wait_ge(n["xt_ps"], c + 1)
                    if dst is xt3 and later(c):
                        act.wait_ge(kept, c)
                    copy(dst[:, :, 0:T],
                         pM[:, 0:GT].rearrange("p (b t) -> p b t", b=G)[:, :, 0:T]).then_inc(n["xt_done"], 1)
                return step

            def queries(c, t):
                act.wait_ge(qk1_ps, c * 4 + t + 1)
                nc.scalar.activation(hi[:, t], quads[t][:, 0:GT], ACT.Identity,
                                     bias=cs[:, HMASK + 2:HMASK + 3] if t >= 2 else 0.0).then_inc(hi_done, 1)

            def position(c):
                act.wait_ge(pv_ps, c + 1)
                copy(pv[:, :, :, :].rearrange("p h b d -> p (h b d)"), pM[0:T, 0:G * C]).then_inc(pv_done, 1)

            def exps(a, ex, width, scale, c, b):
                act.wait_ge(a["st_ps"], c * G + b + 1)
                if b >= 2 or later(c):
                    act.wait_ge(a["av_ps"], c * G + b - 1)
                nc.scalar.activation(ex[0:T, b % 2, :, 0:width], pT[0:T, :, 0:width], ACT.Exp,
                                     scale=scale).then_inc(a["ex_done"], 1)

            def exps1(c, b, half):
                if half == 1:
                    exps(a1, ex1, 4 * TP, D1 ** -0.5, c, b)

            def exps2(c, b):
                exps(a2, ex2, 2 * TP, D2 ** -0.5, c, b)

            def values(a, avt, width):
                def step(c, b):
                    act.wait_ge(a["av_ps"], c * G + b + 1)
                    copy(avt[:, b, 0:width], pT[:, 0, 0:width]).then_inc(a["avt_done"], 1)
                return step

            def mixed(ps, yt, done):
                def step(c):
                    act.wait_ge(ps, c + 1)
                    copy(yt[:, :, 0:T], pM[:, 0:2 * TP].rearrange("p (q t) -> p q t", q=2)[:, :, 0:T]).then_inc(done, 1)
                return step

            def p2a(c):
                act.wait_ge(rpa_done, c + 1)
                copy(v2n[:, :, :, :], pM[0:T].rearrange("p (b n) -> p b n", b=G)[:, :, 96:128]
                     .rearrange("p b (k d) -> p b k d", k=KV2)).then_inc(v2n_done, 1)

            def rope(c):
                act.wait_ge(rp_done, c + 1)
                if later(c):
                    act.wait_ge(rst_ps, c * 3)
                heads = rp[:, :, :].rearrange("p b (h d) -> p b h d", d=D2)
                copy(rph[:, :, :], rp[:, :, :]).then_inc(rph_done, 1)
                copy(rs[:, :, :, 0:16], heads)
                copy(rs[:, :, 0:4, 32:48], heads[:, :, 0:4])
                copy(rs[:, :, 4:6, 16:32], heads[:, :, 4:6]).then_inc(rs_act, 1)

            def v2_step(c):
                act.wait_ge(v2n_done, c + 1)
                copy(v2[0:T, :, :, 0:D2], v2n[:, :, :, :]).then_inc(v2_done, 1)

            def rst(c):
                for t, o in enumerate((quads[2], quads[3], pM)):
                    act.wait_ge(rst_ps, c * 3 + t + 1)
                    copy(qk2[:, t].rearrange("p (b t) -> p b t", b=G)[:, :, 0:T],
                         o[:, 0:GT].rearrange("p (b t) -> p b t", b=G)[:, :, 0:T]).then_inc(rst_done, 1)

            def router(c):
                act.wait_ge(rt_dve, c * RT + 2)
                nc.scalar.activation(rt[:, 1], rt[:, 0], ACT.Exp).then_inc(rt_exp, 1)

            def fwt_step(c, p):
                act.wait_ge(fwt_ps, c * 4 + p + 1)
                copy(fwt[:, p, :, 0:T],
                     pM[:, 0:GT].rearrange("p (b t) -> p b t", b=G)[:, :, 0:T]).then_inc(fwt_done, 1)

            def tile(c, k):
                act.wait_ge(g_ps, c * TILES + k + 1)
                if k > 0 or later(c):
                    act.wait_ge(gb_done, c * TILES + k)
                nc.scalar.activation(th[:, :], pG[0:HT_ROWS, 0:GT], ACT.Tanh, scale=0.5).then_inc(th_done, 1)

            def expert_sum(c):
                act.wait_ge(down_done, c * 6 + 6)
                copy(yd[:, :], pY[:, 0:GT]).then_inc(yd_done, 1)

            act.wait_ge(ld_w[2], 16)
            nc.scalar.activation(pos_s[:, 3], sm[0:T, GATE:GATE + H1], ACT.Exp, scale=-1.0).then_inc(pos_act, 1)
            act.wait_ge(pos_pool, 7)
            nc.scalar.activation(pos_a[:, :, :], pos_b[:, :, :], ACT.Exp).then_inc(pos_act, 1)
            act.wait_ge(pos_pe, 1)
            act.wait_ge(zeroed, 1)
            act.wait_ge(ld_w[1], 16)
            act.wait_ge(ld_w[3], 16)
            copy(pos_t[0:T, :, :].rearrange("p (a h) t -> p a h t", a=2),
                 pS[0:T, :, 0:4 * T].rearrange("p a (h t) -> p a h t", h=4)).then_inc(pos_act, 1)

            pipeline(act, {
                "gelu": gelu, "ln1": highs(n1), "xt1": stacked(n1, xt1), "queries": queries, "position": position,
                "st1": exps1, "av1": values(a1, avt1, 2 * TP), "proj1a": mixed(yta_ps, yta, yta_done),
                "ln2": highs(n2), "xt2": stacked(n2, xt2), "p2a": p2a, "rope": rope, "v2": v2_step, "rst": rst,
                "st2": exps2, "av2": values(a2, avt2, TP), "proj2a": mixed(ytb_ps, ytb, ytb_done),
                "rms": highs(n3), "xt3": stacked(n3, xt3), "router": router, "fwt": fwt_step, "tile": tile,
                "sum": expert_sum})

        @block.vector
        def _(dve):
            V = nc.vector

            def moments(n, c, src):
                bst, bsum, mv, stat, at = n["bst"], n["bsum"], n["mv"], n["stat"], c * n["per"]
                for b in range(G):
                    last = V.bn_stats(bst[:, b, :], src[:, b, :])
                last.then_inc(stat, 1)
                dve.wait_ge(stat, at + 1)
                V.tensor_tensor(bsum[:, :, 0:2], bst[:, :, 1:3], bst[:, :, 4:6], ALU.add)
                V.tensor_tensor(bsum[:, :, 2], bst[:, :, 1], bst[:, :, 4], ALU.subtract).then_inc(stat, 1)
                dve.wait_ge(stat, at + 2)
                V.scalar_tensor_tensor(bsum[:, :, 3], bsum[:, :, 2], 0.25, bsum[:, :, 2], ALU.mult, ALU.mult)
                V.tensor_scalar(mv[:, :, 0], bsum[:, :, 0], 0.5, None, ALU.mult).then_inc(stat, 1)
                dve.wait_ge(stat, at + 3)
                V.scalar_tensor_tensor(mv[:, :, 1], bsum[:, :, 1], 1.0 / C, bsum[:, :, 3], ALU.mult,
                                       ALU.add).then_inc(stat, 1)
                dve.wait_ge(stat, at + 4)

            def rsqrt(n, at):
                stat, (v, y, a, b) = n["stat"], (n[t][:, :] for t in "vyab")
                V.tensor_scalar(y.bitcast(I32), v.bitcast(I32), -0.5, MAGIC, ALU.mult, ALU.add).then_inc(stat, 1)
                dve.wait_ge(stat, at + 1)
                for i in range(3):
                    V.tensor_tensor(a, y, y, ALU.mult).then_inc(stat, 1)
                    dve.wait_ge(stat, at + 3 * i + 2)
                    V.scalar_tensor_tensor(b, a, -0.5, v, ALU.mult, ALU.mult).then_inc(stat, 1)
                    dve.wait_ge(stat, at + 3 * i + 3)
                    V.scalar_tensor_tensor(y, b, 1.5, y, ALU.add, ALU.mult).then_inc(stat, 1)
                    dve.wait_ge(stat, at + 3 * i + 4)

            def center(dst, src, mv, rstd):
                for b in range(G):
                    last = V.tensor_scalar(dst[:, b, :], src[:, b, :], mv[:, b, 0:1], rstd[:, b:b + 1],
                                           ALU.subtract, ALU.mult)
                return last

            def tokens(c):
                dve.wait_ge(tok_ps, c + 1)
                if later(c):
                    dve.wait_ge(resb_done, c)
                V.tensor_copy(res[:, :, :].rearrange("p b c -> p (b c)"), pM[0:T, 0:G * C]).then_inc(res_done, 1)

            def ln1(c):
                dve.wait_ge(res_done, c + 1)
                moments(n1, c, res)
                V.tensor_scalar(n1["v"][:, :], n1["mv"][:, :, 1], LN_EPS, None, ALU.add).then_inc(n1["stat"], 1)
                dve.wait_ge(n1["stat"], c * n1["per"] + 5)
                rsqrt(n1, c * n1["per"] + 5)
                center(n1["yn"], res, n1["mv"], n1["y"]).then_inc(n1["yn_done"], 1)

            def queries(c, t):
                dve.wait_ge(hi_done, c * 4 + t + 1)
                V.scalar_tensor_tensor(qk1[:, t], hi[:, t].bitcast(F), cs[:, HMASK + t // 2:HMASK + t // 2 + 1],
                                       quads[t][:, 0:GT], ALU.mult, ALU.add).then_inc(qk1_done, 1)

            def values1(c):
                dve.wait_ge(v1_ps, c + 1)
                V.tensor_copy(v1[0:T, :, :, 0:D1],
                              pM[0:T, 0:G * C].rearrange("p (b h d) -> p b h d", b=G, h=H1)).then_inc(v1_done, 1)

            def maxima(a, c, b, nm, scores, heads_hi, heads_lo):
                dve.wait_ge(a["s_ps"], c * G + b + 1)
                V.tensor_reduce(nm[:, :], scores, AX, ALU.max, negate=True).then_inc(a["nm_done"], 1)
                dve.wait_ge(a["nm_done"], c * G + b + 1)
                V.tensor_copy(heads_hi, nm[:, :].rearrange("p (a b t) -> p a b t", a=2, t=2)).then_inc(a["mh_done"], 1)
                dve.wait_ge(a["mh_done"], c * G + b + 1)
                V.tensor_tensor(heads_lo, nm[:, :].rearrange("p (a b t) -> p a b t", a=2, t=2),
                                heads_hi.bitcast(F), ALU.subtract).then_inc(a["mx_done"], 1)

            m1 = mx1[:, :, :].rearrange("p t (j2 bk r) -> p bk j2 t r", j2=2, bk=2)
            m2 = mx2[:, :, :].rearrange("p t (a i r) -> p i a t r", i=2, a=1)

            def s1(c, b, half):
                if half == 1:
                    maxima(a1, c, b, nm1, pS[0:T, :, 0:4 * TP].rearrange("p a (s t) -> p a s t", t=TP)[:, :, :, 0:T],
                           m1[:, :, :, :, 24], m1[:, :, :, :, 25])

            def s2(c, b):
                maxima(a2, c, b, nm2, pS[0:T, :, 0:2 * TP].rearrange("p a (s t) -> p a s t", t=TP)[:, :, :, 0:T],
                       m2[:, :, :, :, 48], m2[:, :, :, :, 49])

            def shifted(a, qm, qk):
                def step(c, b):
                    dve.wait_ge(a["mt_ps"], c * G + b + 1)
                    if b > 0 or later(c):
                        dve.wait_ge(a["st_ps"], c * G + b)
                    V.tensor_tensor(qm[:, :, 0:T], pS[:, 0, 0:2 * TP].rearrange("p (a t) -> p a t", a=2)[:, :, 0:T],
                                    qk[:, 0:2, b * TP:b * TP + T].bitcast(F), ALU.add).then_inc(a["qm_done"], 1)
                return step

            def yt1(c):
                dve.wait_ge(yt1_ps, c + 1)
                tok = pS[0:T, :, :].rearrange("p a n -> p (a n)").rearrange("p (b h r) -> p b h r", b=G, h=H1)
                s = [den1[:, i] for i in range(4)]
                k = c * MIX
                y2h = y2a[:, :, :].rearrange("p b (h d) -> p b h d", h=H1)
                V.reciprocal(s[0], tok[:, :, :, D1]).then_inc(mix, 1)
                dve.wait_ge(mix, k + 1)
                V.tensor_tensor(s[1], s[0], bc(one_g.rearrange("p (a h) -> p a h", a=1), [T, G, H1]),
                                ALU.mult).then_inc(mix, 1)
                dve.wait_ge(mix, k + 2)
                V.tensor_tensor(s[2], tok[:, :, :, D1], s[1], ALU.mult).then_inc(mix, 1)
                V.tensor_tensor(y2h, tok[:, :, :, 0:D1], bc(s[1].rearrange("p b (h d) -> p b h d", d=1), [T, G, H1, D1]),
                                ALU.mult).then_inc(mix, 1)
                dve.wait_ge(mix, k + 4)
                V.tensor_tensor(s[3], s[2], bc(pos_sum.rearrange("p (a h) -> p a h", a=1), [T, G, H1]),
                                ALU.add).then_inc(mix, 1)
                dve.wait_ge(pv_done, c + 1)
                V.tensor_tensor(y2h, y2h, pv[:, :, :, :].rearrange("p h b d -> p b h d"), ALU.add).then_inc(mix, 1)
                dve.wait_ge(mix, k + 6)
                V.reciprocal(s[2], s[3]).then_inc(mix, 1)
                dve.wait_ge(mix, k + 7)
                V.tensor_tensor(y2h, y2h, bc(s[2].rearrange("p b (h d) -> p b h d", d=1), [T, G, H1, D1]),
                                ALU.mult).then_inc(y2a_done, 1)

            def proj1b(c):
                dve.wait_ge(pra_ps, c + 1)
                dve.wait_ge(resb_done, c + 1)
                if later(c):
                    dve.wait_ge(h1_kept, c)
                V.tensor_tensor(h1[:, :, :].rearrange("p b c -> p (b c)"), pM[0:T, 0:G * C],
                                resb[:, :, :].rearrange("p b c -> p (b c)"), ALU.add).then_inc(h1_done, 1)

            def ln2(c):
                dve.wait_ge(h1_done, c + 1)
                moments(n2, c, h1)
                mv, v = n2["mv"], n2["v"]
                V.tensor_scalar(v[:, 0:G], mv[:, :, 1], LN_EPS, None, ALU.add)
                V.tensor_scalar(v[:, G:2 * G], mv[:, :, 1], 1.0 + RMS_EPS, RMS_EPS * LN_EPS, ALU.mult,
                                ALU.add).then_inc(n2["stat"], 1)
                dve.wait_ge(n2["stat"], c * n2["per"] + 5)
                rsqrt(n2, c * n2["per"] + 5)
                center(n2["yn"], h1, mv, n2["y"][:, G:2 * G]).then_inc(n2["yn_done"], 1)
                center(zz, h1, mv, n2["y"][:, 0:G]).then_inc(zz_done, 1)

            def rotate(ps, width, tab, dst, done):
                def step(c):
                    dve.wait_ge(ps, c + 1)
                    V.tensor_tensor(dst[:, :, :], pM[0:T, 0:G * width].rearrange("p (b n) -> p b n", b=G)[:, :, 0:96],
                                    bc(cs[0:T, tab:tab + 96].rearrange("p (a n) -> p a n", a=1), [T, G, 96]),
                                    ALU.mult).then_inc(done, 1)
                return step

            def yt2(c):
                dve.wait_ge(yt2_ps, c + 1)
                tok2 = pS[0:T, 0].rearrange("p (b h r) -> p b h r", b=G, h=H2)
                V.reciprocal(den2[:, :, :], tok2[:, :, :, D2]).then_inc(den2_done, 1)
                dve.wait_ge(den2_done, c + 1)
                V.tensor_tensor(y2b[:, :, :].rearrange("p b (h d) -> p b h d", h=H2), tok2[:, :, :, 0:D2],
                                bc(den2[:, :, :].rearrange("p b (h d) -> p b h d", d=1), [T, G, H2, D2]),
                                ALU.mult).then_inc(y2b_done, 1)

            def proj2b(c):
                dve.wait_ge(prb_ps, c + 1)
                dve.wait_ge(h1_kept, c + 1)
                V.tensor_tensor(x1[:, :, :].rearrange("p b c -> p (b c)"), pM[0:T, 0:G * C],
                                zzk[:, :, :].rearrange("p b c -> p (b c)"), ALU.add).then_inc(x1_done, 1)

            def rms(c):
                stat, at = n3["stat"], c * n3["per"]
                dve.wait_ge(sq_done, c + 1)
                V.tensor_reduce(n3["a"][:, :], sq[:, :, :], AX, ALU.add).then_inc(stat, 1)
                dve.wait_ge(stat, at + 1)
                V.tensor_scalar(n3["v"][:, :], n3["a"][:, :], 1.0 / C, RMS_EPS, ALU.mult, ALU.add).then_inc(stat, 1)
                dve.wait_ge(stat, at + 2)
                rsqrt(n3, at + 2)
                V.tensor_tensor(n3["yn"][:, :, :], x1[:, :, :],
                                bc(n3["y"][:, :].rearrange("p (b c) -> p b c", c=1), [T, G, C]),
                                ALU.mult).then_inc(n3["yn_done"], 1)

            def one(ap):
                return ap.rearrange("p (b e) -> p b e", e=1)

            def logits(c):
                lg = pM[0:T, 0:G * NE].rearrange("p (b e) -> p b e", b=G)
                dve.wait_ge(lg_ps, c + 1)
                V.tensor_reduce(rsm[:, 0], lg, AX, ALU.max).then_inc(rt_dve, 1)
                dve.wait_ge(rt_dve, c * RT + 1)
                V.tensor_tensor(rt[:, 0], lg, bc(one(rsm[:, 0]), [T, G, NE]), ALU.subtract).then_inc(rt_dve, 1)

            def router(c):
                k = c * RT
                dve.wait_ge(rt_exp, c + 1)
                V.tensor_reduce(rsm[:, 1], rt[:, 1], AX, ALU.add).then_inc(rt_dve, 1)
                dve.wait_ge(rt_dve, k + 3)
                V.reciprocal(rsm[:, 2], rsm[:, 1]).then_inc(rt_dve, 1)
                dve.wait_ge(rt_dve, k + 4)
                V.tensor_tensor(rt[:, 2], rt[:, 1], bc(one(rsm[:, 2]), [T, G, NE]), ALU.mult).then_inc(rt_dve, 1)
                dve.wait_ge(rt_dve, k + 5)
                for b in range(G):
                    pe_ = bc(rt[:, 2, b].rearrange("p (e f) -> p e f", f=1), [T, NE, NE])
                    pf_ = bc(rt[:, 2, b].rearrange("p (e f) -> p e f", e=1), [T, NE, NE])
                    V.tensor_tensor(cmp1[:, b], pf_, pe_, ALU.is_gt)
                    last = V.tensor_tensor(cmp2[:, b], pf_, pe_, ALU.is_equal)
                last.then_inc(rt_dve, 1)
                dve.wait_ge(rt_dve, k + 6)
                ff = lambda t: t[:, :, :, :].rearrange("p b e f -> p b (e f)")
                V.tensor_tensor(ff(cmp2), ff(cmp2), bc(cs[0:T, TRI:TRI + 64].rearrange("p (b e) -> p b e", b=1),
                                                       [T, G, 64]), ALU.mult).then_inc(rt_dve, 1)
                dve.wait_ge(rt_dve, k + 7)
                V.tensor_tensor(ff(cmp1), ff(cmp1), ff(cmp2), ALU.add).then_inc(rt_dve, 1)
                dve.wait_ge(rt_dve, k + 8)
                V.tensor_reduce(rt[:, 3], cmp1[:, :, :, :], AX, ALU.add).then_inc(rt_dve, 1)
                dve.wait_ge(rt_dve, k + 9)
                V.scalar_tensor_tensor(rt[:, 4], rt[:, 3], 1.5, rt[:, 2], ALU.is_lt, ALU.mult).then_inc(rt_dve, 1)
                dve.wait_ge(rt_dve, k + 10)
                V.tensor_reduce(rsm[:, 3], rt[:, 4], AX, ALU.add).then_inc(rt_dve, 1)
                dve.wait_ge(rt_dve, k + 11)
                V.tensor_scalar(rsm[:, 0], rsm[:, 3], 1e-9, None, ALU.add).then_inc(rt_dve, 1)
                dve.wait_ge(rt_dve, k + 12)
                V.reciprocal(rsm[:, 1], rsm[:, 0]).then_inc(rt_dve, 1)
                dve.wait_ge(rt_dve, k + 13)
                V.tensor_tensor(rt[:, 5], rt[:, 4], bc(one(rsm[:, 1]), [T, G, NE]), ALU.mult).then_inc(wt_done, 1)

            def tile(c, k):
                dve.wait_ge(th_done, c * TILES + k + 1)
                V.scalar_tensor_tensor(gb[:, k % 2, :], th[:, :], 1.0, pG[0:HT_ROWS, 0:GT], ALU.add,
                                       ALU.mult).then_inc(gb_done, 1)
                dve.wait_ge(gb_done, c * TILES + k + 1)
                dve.wait_ge(u_ps, c * TILES + k + 1)
                if k >= 4 or later(c):
                    dve.wait_ge(down_done, c * 6 + k // 2 - 1)
                V.tensor_tensor(hid[:, k % 4, :], gb[:, k % 2, :], pU[0:HT_ROWS, 0:GT], ALU.mult).then_inc(hid_done, 1)

            def expert_sum(c):
                dve.wait_ge(o_ps, c + 1)
                dve.wait_ge(rr_done, c + 1)
                if later(c):
                    dve.wait_ge(stored, 16 * c)
                V.tensor_tensor(ot[:, :, :].rearrange("p b c -> p (b c)"), pG[0:T, 0:G * C],
                                rr[:, :, :].rearrange("p b c -> p (b c)"), ALU.add).then_inc(ot_done, 1)

            for t in (xt1, xt2, xt3, qm1, qm2):
                V.memset(t[:, :, T:TP].bitcast(F), 0.0)
            for t in (qk1, qk2):
                V.memset(t[:, :, :].rearrange("p t (b s) -> p (t b) s", s=TP)[:, :, T:TP].bitcast(F), 0.0)
            V.memset(fwt[:, :, :, T:TP], 0.0)
            V.memset(pos_t[64:128, :, :], 0.0)
            V.memset(mx1[:, :, :].bitcast(F), 0.0)
            V.memset(mx2[:, :, :].bitcast(F), 0.0).then_inc(zeroed, 1)
            dve.wait_ge(zeroed, 1)
            dve.wait_ge(pos_act, 1)
            V.tensor_scalar(pos_s[:, 3], pos_s[:, 3], 1.0, None, ALU.add).then_inc(pos_dve, 1)
            dve.wait_ge(pos_dve, 1)
            V.reciprocal(pos_s[:, 3], pos_s[:, 3]).then_inc(pos_dve, 1)
            dve.wait_ge(pos_dve, 2)
            V.tensor_scalar(one_g, pos_s[:, 3], -1.0, 1.0, ALU.mult, ALU.add)
            dve.wait_ge(pos_pool, 6)
            V.tensor_reduce(pos_s[:, 0], pos_a[:, :, :], AX, ALU.max).then_inc(pos_dve, 1)
            dve.wait_ge(pos_act, 2)
            V.tensor_reduce(pos_s[:, 1], pos_a[:, :, :], AX, ALU.add).then_inc(pos_dve, 1)
            dve.wait_ge(pos_dve, 4)
            V.reciprocal(pos_s[:, 2], pos_s[:, 1]).then_inc(pos_dve, 1)
            dve.wait_ge(pos_dve, 5)
            V.tensor_tensor(pos_s[:, 2], pos_s[:, 2], pos_s[:, 3], ALU.mult).then_inc(pos_dve, 1)
            dve.wait_ge(pos_dve, 6)
            V.tensor_tensor(pos_b[:, :, :], pos_a[:, :, :],
                            bc(pos_s[:, 2].rearrange("p (h t) -> p h t", t=1), [T, H1, T]),
                            ALU.mult).then_inc(pos_dve, 1)
            dve.wait_ge(pos_dve, 7)
            V.tensor_reduce(pos_sum, pos_b[:, :, :], AX, ALU.add).then_inc(pos_dve, 1)
            dve.wait_ge(pos_dve, 8)
            dve.wait_ge(ld_w[1], 16)
            dve.wait_ge(ld_w[3], 16)
            V.tensor_copy(emb[:, :, 0:1], bc(ch[:, CLS:CLS + 1].rearrange("p (a b) -> p a b", a=1), [128, 2, 1]))
            V.tensor_copy(identb[:, :], ident)
            V.tensor_copy(maskb[:, :, :], cs[:, MROW:MROW + 4 * TP].rearrange("p (a t) -> p a t", a=2)).then_inc(casts, 1)
            dve.wait_ge(ld_w[4], 16)
            for a, z, w in ((QK1, QKV2, None), (QKV2, ROUT, LN1W), (ROUT, NSPLIT, LN2W)):
                scale = 1.0 if w is None else ch[:, w:w + 1]
                last = V.tensor_scalar(wh[:, a:z], ws[:, a:z], scale, None, ALU.mult)
            last.then_inc(w_split_done, 1)
            dve.wait_ge(w_split_done, 1)
            for a, z, w in ((QK1, QKV2, None), (QKV2, ROUT, LN1W), (ROUT, NSPLIT, LN2W)):
                scale = 1.0 if w is None else ch[:, w:w + 1]
                V.scalar_tensor_tensor(wl[:, a:z], ws[:, a:z], scale, wh[:, a:z].bitcast(F), ALU.mult,
                                       ALU.subtract).then_inc(w_low_done, 1)

            def start():
                dve.wait_ge(ld_w[5], 16)
                dve.wait_ge(ld_w[6], 16)
                V.tensor_scalar(w2s[:, :, :].rearrange("p k c -> p (k c)"), w2s[:, :, :].rearrange("p k c -> p (k c)"),
                                0.5, None, ALU.mult).then_inc(w_half_done, 1)
                V.tensor_scalar(wf[:, W3C:FEND], wf[:, W3C:FEND], ch[:, LN2W:LN2W + 1], None,
                                ALU.mult).then_inc(w_half_done, 1)

            pipeline(dve, {
                "tokens": tokens, "ln1": ln1, "queries": queries, "values1": values1, "s1": s1,
                "mt1": shifted(a1, qm1, qk1), "yt1": yt1, "proj1b": proj1b, "ln2": ln2,
                "p2a": rotate(p2a_ps, 128, COSC, rp1, rpa_done), "p2b": rotate(p2b_ps, 96, SINC, rp2, rpb_done),
                "s2": s2, "mt2": shifted(a2, qm2, qk2), "yt2": yt2, "proj2b": proj2b, "rms": rms,
                "logits": logits, "router": router, "tile": tile, "sum": expert_sum}, start)

        @block.gpsimd
        def _(pool):
            P = nc.gpsimd

            def lows(n):
                def step(c):
                    pool.wait_ge(n["yh_done"], c + 1)
                    P.tensor_tensor(n["ysp"][:, :, 1], n["yn"][:, :, :], n["ysp"][:, :, 0].bitcast(F),
                                    ALU.subtract).then_inc(n["ysp_done"], 1)
                return step

            def residual(c):
                pool.wait_ge(res_done, c + 1)
                if later(c):
                    pool.wait_ge(h1_done, c)
                P.tensor_tensor(resb[:, :, :], res[:, :, :],
                                bc(sm[0:T, BPROJ:BPROJ + C].rearrange("p (b c) -> p b c", b=1), [T, G, C]),
                                ALU.add).then_inc(resb_done, 1)

            def rope(c):
                pool.wait_ge(rpb_done, c + 1)
                P.tensor_tensor(rp[:, :, :], rp1[:, :, :], rp2[:, :, :], ALU.add).then_inc(rp_done, 1)
                pool.wait_ge(rph_done, c + 1)
                heads = rp[:, :, :].rearrange("p b (h d) -> p b h d", d=D2)
                highs = rph[:, :, :].rearrange("p b (h d) -> p b h d", d=D2).bitcast(F)
                P.tensor_tensor(rs[:, :, 0:4, 16:32], heads[:, :, 0:4], highs[:, :, 0:4], ALU.subtract)
                P.tensor_tensor(rs[:, :, 4:6, 32:48], heads[:, :, 4:6], highs[:, :, 4:6],
                                ALU.subtract).then_inc(rs_pool, 1)

            def squares(c):
                pool.wait_ge(x1_done, c + 1)
                P.tensor_tensor(sq[:, :, :], x1[:, :, :], x1[:, :, :], ALU.mult).then_inc(sq_done, 1)
                lows(n3)(c)

            def router(c):
                pool.wait_ge(wt_done, c + 1)
                for b in range(G):
                    last = P.tensor_tensor(fw[:, b], bc(n3["yn"][:, b].rearrange("p (e c) -> p e c", e=1), [T, NE, C]),
                                           bc(rt[:, 5, b].rearrange("p (e c) -> p e c", c=1), [T, NE, C]), ALU.mult)
                last.then_inc(fw_done, 1)

            def keep_sum(c):
                if later(c):
                    pool.wait_ge(ot_done, c)
                P.tensor_tensor(rr[:, :, :], x1[:, :, :], h1k[:, :, :], ALU.add).then_inc(rr_done, 1)
                P.tensor_copy(xte[:, :, :], xt3[:, :, :].bitcast(F)).then_inc(kept, 1)

            def keep_h1(c):
                pool.wait_ge(zz_done, c + 1)
                if later(c):
                    pool.wait_ge(x1_done, c)
                    pool.wait_ge(rr_done, c)
                P.tensor_tensor(zzk[:, :, :], zz[:, :, :], bc(zero[:, :, :], [T, G, C]), ALU.add)
                P.tensor_copy(h1k[:, :, :], h1[:, :, :]).then_inc(h1_kept, 1)

            for t in (v1, v2, ex1, ex2):
                P.memset(t[:, :, :, :], 0.0)
            P.memset(zero[:, :, :], 0.0)
            P.memset(rs[:, :, :, :].bitcast(F), 0.0).then_inc(zeroed_pool, 1)
            pool.wait_ge(zeroed_pool, 1)
            P.memset(v1[0:T, :, :, D1:D1 + 1], 1.0)
            P.memset(v2[0:T, :, :, D2:D2 + 1], 1.0)
            P.memset(rs[:, :, 4:6, 48:50].bitcast(F), 1.0).then_inc(zeroed_pool, 1)
            pool.wait_ge(ld_w[1], 16)
            pool.wait_ge(ld_w[2], 16)
            wpos = sm[0:T, WPOS:WPOS + 24].rearrange("p (h k) -> p h k", k=3)
            dist = cs[0:T, DIST:DIST + 3 * T].rearrange("p (k t) -> p k t", k=3)
            n = 0
            for k in range(3):
                dst = pos_a if k == 0 else pos_b
                P.tensor_tensor(dst[:, :, :], bc(dist[:, k:k + 1], [T, H1, T]), bc(wpos[:, :, k:k + 1], [T, H1, T]),
                                ALU.mult).then_inc(pos_pool, 1)
                n += 1
                pool.wait_ge(pos_pool, n)
                if k > 0:
                    P.tensor_tensor(pos_a[:, :, :], pos_a[:, :, :], pos_b[:, :, :], ALU.add).then_inc(pos_pool, 1)
                    n += 1
                    pool.wait_ge(pos_pool, n)
            P.tensor_tensor(pos_a[:, :, :], pos_a[:, :, :],
                            bc(sm[0:T, BPOS:BPOS + H1].rearrange("p (h t) -> p h t", t=1), [T, H1, T]),
                            ALU.add).then_inc(pos_pool, 1)
            pool.wait_ge(pos_dve, 3)
            P.tensor_tensor(pos_b[:, :, :], pos_a[:, :, :],
                            bc(pos_s[:, 0].rearrange("p (h t) -> p h t", t=1), [T, H1, T]),
                            ALU.subtract).then_inc(pos_pool, 1)

            pipeline(pool, {"ln1": lows(n1), "position": residual, "ln2": lows(n2), "rope": rope, "rms": squares,
                            "router": router, "keep_sum": keep_sum, "keep_h1": keep_h1})

def _split_weights(Wqk, Wv, wq, wk, wv, router_w, w1):
    w = np.zeros((C, NSPLIT), np.float32)
    for t in range(4):
        for j in range(4):
            rows = Wqk[(t // 2) * C + (4 * (t % 2) + j) * D1:][:D1]
            for r in range(3):
                at = QK1 + t * 128 + 32 * j + 8 * r
                w[:, at:at + D1] = rows.T
    w[:, V1C:V1C + C] = Wv.T
    order = (0, 2, 1, 3)
    heads = [wq[h * D2:h * D2 + D2] for h in order] + [wk[:D2], wk[D2:]]
    for n, rows in enumerate(heads):
        w[:, QKV2 + n * D2:QKV2 + n * D2 + D2] = rows.T
        w[:, ROT2 + n * D2:ROT2 + n * D2 + D2] = np.roll(rows, D2 // 2, axis=0).T
    w[:, QKV2 + 96:QKV2 + 128] = wv.T
    w[:, ROUT:ROUT + NE] = router_w.T
    for e in range(NE):
        at = W1C + e // 2 * 3 * HT_ROWS + e % 2 * HID
        w[:, at:at + HID] = w1[e].T
    return np.concatenate([w, w])


def _whole_weights(Wproj, wo, w3):
    f = np.zeros((128, FEND), np.float32)
    for n in range(2):
        f[n * C:n * C + C, WPROJ + n * C:WPROJ + n * C + C] = Wproj.T
        f[n * C:n * C + C, WOUT + n * C:WOUT + n * C + C] = wo.T
    for e in range(NE):
        at = W3C + e // 2 * 3 * HT_ROWS + e % 2 * HID
        f[e % 2 * C:e % 2 * C + C, at:at + HID] = w3[e].T
    return f


def _down_weights(w2):
    d = np.zeros((NPAIR, 3 * HT_ROWS, C), np.float32)
    for e in range(NE):
        d[e // 2, e % 2 * HID:e % 2 * HID + HID] = w2[e].T
    return np.ascontiguousarray(d.reshape(TILES, HT_ROWS, C).transpose(1, 0, 2))


def _patch_weights(weight):
    w = np.zeros((128, PW, 128), np.float32)
    taps = weight.reshape(HP, PW, C)
    for n in range(2):
        w[n * C:n * C + C, :, n * C:n * C + C] = taps
    return w


def _constants():
    k = np.zeros((128, CEND), np.float32)
    k[:, IDENT:IDENT + 128] = np.eye(128)
    k[:, FOLD:FOLD + C] = np.concatenate([np.eye(C)] * 2)
    inv = 1.0 / 10000.0 ** (np.arange(0, D2, 2, dtype=np.float32) / D2)
    freqs = np.outer(np.arange(T, dtype=np.float32), inv)
    cos, sin = np.cos(freqs), np.sin(freqs)
    k[:T, COSC:COSC + 96] = np.tile(np.concatenate([cos, cos], 1), 6)
    k[:T, SINC:SINC + 96] = np.tile(np.concatenate([-sin, sin], 1), 6)
    i = np.arange(TP)
    by_row = np.where(i[None, :] > i[:T, None], -1e30, 0.0)
    by_col = np.pad(np.where(i[None, :T] < i[:T, None], -1e30, 0.0), ((0, 0), (0, 1)))
    k[:T, MROW:MROW + 2 * TP] = np.tile(by_row, 2)
    k[:T, MCOL:MCOL + 2 * TP] = np.tile(by_col, 2)
    e = np.arange(NE)
    k[:, TRI:TRI + NE * NE] = (e[None, :] < e[:, None]).ravel()
    d = (np.arange(T)[None, :] - np.arange(T)[:, None]).astype(np.float32)
    k[:T, DIST:DIST + 3 * T] = np.concatenate([d, np.zeros_like(d), d * d], 1)
    r = np.arange(128) % 32
    k[:, HMASK] = -1.0 * ((r >= 8) & (r < 16))
    k[:, HMASK + 1] = -1.0 * ((r >= 16) & (r < 24)) + ((r == 24) | (r == 25))
    k[:, HMASK + 2] = (r == 24) | (r == 25)
    return k


def kernel(x, cls_tok, L0_tok_weight, L0_tok_bias, L0_attn_Wqk, L0_attn_Wv, L0_attn_Wpos, L0_attn_bpos,
           L0_attn_Wproj, L0_attn_bproj, L0_attn_gating, L0_ffn_ln1_w, L0_ffn_ln2_w, L0_ffn_wq, L0_ffn_wk,
           L0_ffn_wv, L0_ffn_wo, L0_ffn_router_w, L0_ffn_w1, L0_ffn_w2, L0_ffn_w3):
    import concourse.bacc as bacc
    from concourse.bass_utils import run_bass_kernel_spmd

    a = np.asarray
    small = np.concatenate([a(L0_attn_Wpos).ravel(), a(L0_attn_bpos), a(L0_attn_gating), a(L0_attn_bproj)])
    chan = np.stack([a(L0_tok_bias), a(cls_tok).ravel(), a(L0_ffn_ln1_w), a(L0_ffn_ln2_w)], 1)
    arrays = {
        "x": np.ascontiguousarray(a(x)),
        "w_patch": _patch_weights(a(L0_tok_weight)),
        "w_split": _split_weights(*map(a, (L0_attn_Wqk, L0_attn_Wv, L0_ffn_wq, L0_ffn_wk, L0_ffn_wv,
                                           L0_ffn_router_w, L0_ffn_w1))),
        "w_full": _whole_weights(a(L0_attn_Wproj), a(L0_ffn_wo), a(L0_ffn_w3)),
        "w2": _down_weights(a(L0_ffn_w2)),
        "consts": _constants(),
        "small": np.ascontiguousarray(np.broadcast_to(small, (128, SEND))),
        "chan": np.concatenate([chan, chan]),
    }
    nc = bacc.Bacc("TRN2", target_bir_lowering=False, num_devices=1)
    args = [nc.dram_tensor(f"in_{n}", v.shape, mybir.dt.from_np(v.dtype), kind="ExternalInput").ap()
            for n, v in arrays.items()]
    out = nc.dram_tensor("out_0", (B, T, C), mybir.dt.float32, kind="ExternalOutput").ap()
    build_program(nc, *args, out)
    r = run_bass_kernel_spmd(nc, [{f"in_{n}": v for n, v in arrays.items()}], core_ids=[0])
    return r.results[0]["out_0"]
```

```python
from contextlib import ExitStack

import numpy as np
import concourse.bass as bass
from concourse import mybir

B, HP, WX = 32, 64, 1000
PW, SW = 25, 12
NP = (WX - PW) // SW + 1
PAIRS = (PW + 1) // 2
T = NP + 1
TP = T + 1
C = 64
G = 4
NCH = B // G
GT = G * TP
H1, D1 = 8, 8
H2, KV2, D2 = 4, 2, 16
NE, HID = 8, 170
NPAIR = NE // 2
TILES = 12
HT_ROWS = 114
BANK = 512

QK1, V1C, QKV2, ROT2, ROUT, W1C = 0, 512, 576, 704, 800, 808
NSPLIT = W1C + TILES * HT_ROWS
IDENT, FOLD, COSC, SINC, MROW, MCOL, TRI, DIST, HMASK, CEND = 0, 128, 192, 288, 384, 552, 720, 784, 1033, 1036
WPOS, BPOS, GATE, BPROJ, CLS, SEND = 0, 24, 32, 40, 104, 168
BPATCH, LN1W, LN2W, PEND = 0, 1, 2, 3
WPROJ, WOUT, W3C, FEND = 0, 128, 256, 256 + TILES * HT_ROWS

LN_EPS, RMS_EPS = 1e-5, 1e-6
MAGIC = 1597463007.0

TENSOR_ORDER = (
    ("queries", 0, 0), ("proj1a", 1), ("queries", 0, 1), ("mt2", 2, 2), ("proj1b", 1), ("queries", 0, 2),
    ("queries", 0, 3), ("st2", 2, 2), ("fwt", 3, 0), ("av2", 2, 2), ("s1", 0, 0, 0), ("fwt", 3, 1), ("s1", 0, 0, 1),
    ("gate", 3, 0), ("up", 3, 0), ("values1", 0), ("mt1", 0, 0), ("s2", 2, 3), ("gate", 3, 1), ("st1", 0, 0, 0),
    ("fwt", 3, 2), ("st1", 0, 0, 1), ("up", 3, 1), ("gate", 3, 2), ("av1", 0, 0), ("fwt", 3, 3), ("s1", 0, 1, 0),
    ("s1", 0, 1, 1), ("up", 3, 2), ("down", 3, 0), ("gate", 3, 3), ("mt1", 0, 1), ("mt2", 2, 3), ("up", 3, 3),
    ("st1", 0, 1, 0), ("st2", 2, 3), ("st1", 0, 1, 1), ("position", 0), ("av1", 0, 1), ("gate", 3, 4), ("av2", 2, 3),
    ("s1", 0, 2, 0), ("s1", 0, 2, 1), ("xt2", 1), ("up", 3, 4), ("gate", 3, 5), ("p2a", 1), ("mt1", 0, 2), ("yt2", 2),
    ("up", 3, 5), ("st1", 0, 2, 0), ("gate", 3, 6), ("st1", 0, 2, 1), ("p2b", 1), ("down", 3, 2), ("av1", 0, 2),
    ("proj2a", 2), ("up", 3, 6), ("s1", 0, 3, 0), ("proj2b", 2), ("s1", 0, 3, 1), ("gate", 3, 7), ("up", 3, 7),
    ("patch", -1, 0), ("rst", 1, 0), ("mt1", 0, 3), ("patch", -1, 1), ("rst", 1, 1), ("st1", 0, 3, 0), ("rst", 1, 2),
    ("st1", 0, 3, 1), ("gate", 3, 8), ("patch", -1, 2), ("s2", 1, 0), ("patch", -1, 3), ("av1", 0, 3), ("down", 3, 4),
    ("gate", 3, 9), ("tokens", -1), ("up", 3, 8), ("yt1", 0), ("mt2", 1, 0), ("down", 3, 6), ("st2", 1, 0),
    ("up", 3, 9), ("av2", 1, 0), ("xt3", 2), ("gate", 3, 10), ("s2", 1, 1), ("logits", 2), ("up", 3, 10),
    ("gate", 3, 11), ("mt2", 1, 1), ("up", 3, 11), ("st2", 1, 1), ("down", 3, 8), ("down", 3, 10), ("av2", 1, 1),
    ("xt1", -1), ("s2", 1, 2), ("sum", 3),
)
SCALAR_ORDER = (
    ("xt1", 0), ("queries", 0, 0), ("proj1a", 1), ("queries", 0, 1), ("queries", 0, 2), ("queries", 0, 3),
    ("st2", 2, 2), ("fwt", 3, 0), ("fwt", 3, 1), ("av2", 2, 2), ("tile", 3, 0), ("values1", 0), ("tile", 3, 1),
    ("st1", 0, 0), ("fwt", 3, 2), ("tile", 3, 2), ("av1", 0, 0), ("fwt", 3, 3), ("ln2_out", 1), ("tile", 3, 3),
    ("st2", 2, 3), ("st1", 0, 1), ("av1", 0, 1), ("tile", 3, 4), ("position", 0), ("av2", 2, 3), ("xt2", 1),
    ("tile", 3, 5), ("zz", 1), ("p2a", 1), ("tile", 3, 6), ("st1", 0, 2), ("av1", 0, 2), ("proj2a", 2), ("rope", 1),
    ("tile", 3, 7), ("rst", 1, 0), ("v2", 1), ("rst", 1, 1), ("rst", 1, 2), ("st1", 0, 3), ("tile", 3, 8),
    ("embed", -1), ("av1", 0, 3), ("tile", 3, 9), ("rms_out", 2), ("tokens", -1), ("st2", 1, 0), ("av2", 1, 0),
    ("xt3", 2), ("tile", 3, 10), ("router", 2), ("tile", 3, 11), ("ln1_out", -1), ("st2", 1, 1), ("sum", 3),
    ("av2", 1, 1),
)
VECTOR_ORDER = (
    ("mx2", 2, 2), ("queries", 0, 0), ("queries", 0, 1), ("mt2", 2, 2), ("proj1b", 1), ("queries", 0, 2),
    ("queries", 0, 3), ("ln2", 1), ("s1", 0, 0), ("mx1", 0, 0), ("gated", 3, 0), ("mt1", 0, 0), ("hidden", 3, 0),
    ("gated", 3, 1), ("hidden", 3, 1), ("s2", 2, 3), ("mx2", 2, 3), ("gated", 3, 2), ("s1", 0, 1), ("mx1", 0, 1),
    ("hidden", 3, 2), ("mt1", 0, 1), ("mt2", 2, 3), ("gated", 3, 3), ("hidden", 3, 3), ("gated", 3, 4), ("s1", 0, 2),
    ("mx1", 0, 2), ("hidden", 3, 4), ("gated", 3, 5), ("mt1", 0, 2), ("p2a", 1), ("yt2", 2), ("hidden", 3, 5),
    ("p2b", 1), ("gated", 3, 6), ("hidden", 3, 6), ("proj2b", 2), ("s1", 0, 3), ("mx1", 0, 3), ("gated", 3, 7),
    ("mt1", 0, 3), ("rms", 2), ("hidden", 3, 7), ("s2", 1, 0), ("mx2", 1, 0), ("gated", 3, 8), ("hidden", 3, 8),
    ("gated", 3, 9), ("mt2", 1, 0), ("yt1", 0), ("mixture", 0), ("hidden", 3, 9), ("ln1", -1), ("s2", 1, 1),
    ("logits", 2), ("gated", 3, 10), ("mx2", 1, 1), ("hidden", 3, 10), ("probabilities", 2), ("gated", 3, 11),
    ("mt2", 1, 1), ("hidden", 3, 11), ("compare", 2), ("top2", 2), ("s2", 1, 2), ("sum", 3),
)
GPSIMD_ORDER = (
    ("rope", 1), ("proj2b", 2), ("position", 0), ("rms", 2), ("rms_out", 2), ("ln1", -1), ("keep_h1", 1),
    ("ln1_out", -1), ("router", 2), ("keep_sum", 2), ("ln2", 0), ("ln2_out", 0),
)
SYNC_ORDER = (
    ("load", -1), ("store", 3),
)
LAGS = [step[1] for order in (TENSOR_ORDER, SCALAR_ORDER, VECTOR_ORDER, GPSIMD_ORDER, SYNC_ORDER) for step in order]
FIRST, LOOP_FROM = min(LAGS), max(LAGS) + 1
LOOP_TO, LAST = NCH + FIRST, NCH + max(LAGS)
PM_BEFORE = {
    "patch": (("proj2b", -3), ("p2b", -2), ("position", -1)),
    "tokens": (("patch", 0),),
    "xt1": (("logits", -3), ("tokens", 0)),
    "values1": (("fwt1", -3), ("proj1b", -1), ("xt1", 0)),
    "position": (("fwt3", -3), ("values1", 0)),
    "proj1a": (("xt1", 1), ("logits", -2)),
    "proj1b": (("proj1a", 0),),
    "xt2": (("position", 1), ("fwt3", -2)),
    "p2a": (("xt2", 0),),
    "p2b": (("p2a", 0),),
    "proj2a": (("p2b", 1), ("fwt3", -1)),
    "proj2b": (("proj2a", 0),),
    "xt3": (("tokens", 3), ("proj2b", 0)),
    "logits": (("xt3", 0),),
    "fwt0": (("proj1b", 2), ("logits", 0)),
    "fwt1": (("fwt0", 0),),
    "fwt2": (("values1", 3), ("fwt1", 0)),
    "fwt3": (("fwt2", 0),),
}


def exists(c):
    return not isinstance(c, int) or 0 <= c < NCH


def later(c):
    return not isinstance(c, int) or c > 0


def iteration(i, order, steps):
    for step, lag, *args in order:
        if exists(i - lag):
            steps[step](i - lag, *args)


def pipeline(engine, order, steps, setup=None):
    for i in range(FIRST, LOOP_FROM):
        iteration(i, order, steps)
        if i == FIRST and setup is not None:
            setup()
    with engine.Fori(LOOP_FROM, LOOP_TO) as i:
        iteration(i, order, steps)
    for i in range(LOOP_TO, LAST):
        iteration(i, order, steps)


def build_program(nc, x, w_patch, w_split, w_full, w2, consts, small, chan, out):
    F = mybir.dt.float32
    R = mybir.dt.float32r
    BF = mybir.dt.bfloat16
    I32 = mybir.dt.int32
    ALU = mybir.AluOpType
    ACT = mybir.ActivationFunctionType
    AX = mybir.AxisListType.X
    ctx = ExitStack()
    with ctx:
        def sb(name, shape, dt=F):
            return ctx.enter_context(nc.sbuf_tensor(name, shape, dt))

        def sem(name):
            return ctx.enter_context(nc.semaphore(name))

        wp = sb("wp", [128, PAIRS, C])
        ws = sb("ws", [128, NSPLIT])
        wh = sb("wh", [128, NSPLIT], R)
        wl = sb("wl", [128, NSPLIT], R)
        wf = sb("wf", [128, FEND])
        w2s = sb("w2s", [HT_ROWS, TILES, C])
        cs = sb("cs", [128, CEND])
        sm = sb("sm", [128, SEND])
        ch = sb("ch", [128, PEND])
        identb = sb("identb", [128, 128], BF)
        maskb = sb("maskb", [128, 2, 2 * TP], BF)
        ident = cs[:, IDENT:IDENT + 128]
        fold = cs[:, FOLD:FOLD + C]
        pos_a = sb("pos_a", [T, H1, T])
        pos_b = sb("pos_b", [T, H1, T])
        pos_s = sb("pos_s", [T, 6, H1])
        pos_t = sb("pos_t", [128, H1, T])
        one_g, pos_sum = pos_s[:, 4], pos_s[:, 5]
        xs = sb("xs", [128, G, WX])
        emb = sb("emb", [128, G, T])
        res = sb("res", [T, G, C])
        resb = sb("resb", [T, G, C])
        xt1 = sb("xt1", [128, G, TP], R)

        def norm_tiles(name, n):
            return dict(bst=sb(name + "_bst", [T, G, 6]), bsum=sb(name + "_bsum", [T, G, 4]),
                        mv=sb(name + "_mv", [T, G, 2]), v=sb(name + "_v", [T, n]), y=sb(name + "_y", [T, n]),
                        a=sb(name + "_a", [T, n]), b=sb(name + "_b", [T, n]), w=sb(name + "_w", [T, n]),
                        nb=sb(name + "_nb", [T, n]), yn=sb(name + "_yn", [T, G, C]),
                        ysp=sb(name + "_ysp", [T, G, 2, C], R))

        n1, n2, n3 = norm_tiles("ln1", G), norm_tiles("ln2", 2 * G), norm_tiles("rms", G)
        hi = sb("hi", [128, 4, GT], R)
        qk1 = sb("qk1", [128, 4, GT], R)
        qm1 = sb("qm1", [128, 2, TP], R)
        v1 = sb("v1", [128, G, H1, 32])
        pv = sb("pv", [T, H1, G, D1])
        nm1 = sb("nm1", [T, 8])
        mx1 = sb("mx1", [T, 2, 128], R)
        ex1 = sb("ex1", [128, 2, 2, 4 * TP])
        avt1 = sb("avt1", [128, G, 2 * TP])
        den1 = sb("den1", [T, 4, G, H1])
        y2a = sb("y2a", [T, G, C])
        yta = sb("yta", [128, 2, TP])
        h1 = sb("h1", [T, G, C])
        zz = sb("zz", [T, G, C])
        xt2 = sb("xt2", [128, G, TP], R)
        rp1 = sb("rp1", [T, G, 96])
        rp2 = sb("rp2", [T, G, 96])
        rp = sb("rp", [T, G, 96])
        rph = sb("rph", [T, G, 96], R)
        rs = sb("rs", [T, G, 6, 64], R)
        v2n = sb("v2n", [T, G, KV2, D2])
        qk2 = sb("qk2", [128, 3, GT], R)
        qm2 = sb("qm2", [128, 2, TP], R)
        v2 = sb("v2", [128, G, KV2, 32])
        nm2 = sb("nm2", [T, 4])
        mx2 = sb("mx2", [T, 2, 128], R)
        ex2 = sb("ex2", [128, 2, 2, 2 * TP])
        avt2 = sb("avt2", [128, G, TP])
        den2 = sb("den2", [T, G, H2])
        y2b = sb("y2b", [T, G, C])
        ytb = sb("ytb", [128, 2, TP])
        h1k = sb("h1k", [T, G, C])
        zzk = sb("zzk", [T, G, C])
        zero, three_halves = sb("zero", [T, 1, 1]), sb("three_halves", [T, 1])
        x1 = sb("x1", [T, G, C])
        sq = sb("sq", [T, G, C])
        xh = sb("xh", [T, G, C])
        rr = sb("rr", [T, G, C])
        xt3 = sb("xt3", [128, G, TP], R)
        rt = sb("rt", [T, 8, G, NE])
        cmp1 = sb("cmp1", [T, G, NE, NE])
        cmp2 = sb("cmp2", [T, G, NE, NE])
        rsm = sb("rsm", [T, 4, G])
        fw = sb("fw", [T, G, NE, C])
        xte = sb("xte", [128, G, TP], R)
        fwt = sb("fwt", [128, NPAIR, G, TP])
        th = sb("th", [HT_ROWS, GT])
        gb = sb("gb", [HT_ROWS, 2, GT])
        hid = sb("hid", [HT_ROWS, 4, GT])
        yd = sb("yd", [128, GT])
        ot = sb("ot", [T, G, C])
        pM = ctx.enter_context(nc.psum_tensor("pM", [128, BANK], F))
        pS = ctx.enter_context(nc.psum_tensor("pS", [128, 2, BANK], F))
        pT = ctx.enter_context(nc.psum_tensor("pT", [128, 2, BANK], F))
        pG = ctx.enter_context(nc.psum_tensor("pG", [128, BANK], F))
        pU = ctx.enter_context(nc.psum_tensor("pU", [128, BANK], F))
        pY = ctx.enter_context(nc.psum_tensor("pY", [128, BANK], F))

        ld_w = [sem(f"ld_w{i}") for i in range(7)]
        ld_x = sem("ld_x")
        stored = sem("stored")
        w_split_done, w_low_done, w_half_done = sem("w_split_done"), sem("w_low_done"), sem("w_half_done")
        zeroed, zeroed_pool, casts = sem("zeroed"), sem("zeroed_pool"), sem("casts")
        pos_pool, pos_dve, pos_act, pos_pe = sem("pos_pool"), sem("pos_dve"), sem("pos_act"), sem("pos_pe")
        patch_ps, emb_done = sem("patch_ps"), sem("emb_done")
        tok_ps, res_done = sem("tok_ps"), sem("res_done")
        gelu_done = sem("gelu_done")
        resb_done = sem("resb_done")
        for n, name, steps in ((n1, "ln1", 6), (n2, "ln2", 6), (n3, "rms", 3)):
            n.update(stat=sem(name + "_stat"), per=steps, root=sem(name + "_root"), roots=12 if n is n3 else 13,
                     yn_done=sem(name + "_yn_done"),
                     yh_done=sem(name + "_yh_done"), ysp_done=sem(name + "_ysp_done"),
                     xt_ps=sem(name + "_xt_ps"), xt_done=sem(name + "_xt_done"))
        qk1_ps, hi_done, qk1_done = sem("qk1_ps"), sem("hi_done"), sem("qk1_done")
        v1_ps, v1_done = sem("v1_ps"), sem("v1_done")
        pv_ps, pv_done = sem("pv_ps"), sem("pv_done")
        s1_half, st1_half = sem("s1_half"), sem("st1_half")

        def attention_semaphores(a):
            return {name: sem(f"{name}{a}") for name in
                    ("s_ps", "nm_done", "mh_done", "mx_done", "mt_ps", "qm_done", "st_ps", "ex_done", "av_ps",
                     "avt_done")}

        a1, a2 = attention_semaphores(1), attention_semaphores(2)
        yt1_ps, mix, y2a_done = sem("yt1_ps"), sem("mix"), sem("y2a_done")
        yta_ps, yta_done = sem("yta_ps"), sem("yta_done")
        pra_ps, h1_done = sem("pra_ps"), sem("h1_done")
        zz_done = sem("zz_done")
        p2a_ps, p2b_ps = sem("p2a_ps"), sem("p2b_ps")
        v2n_done, rpa_done, rpb_done = sem("v2n_done"), sem("rpa_done"), sem("rpb_done")
        rp_done, rph_done = sem("rp_done"), sem("rph_done")
        rs_act, rs_pool = sem("rs_act"), sem("rs_pool")
        rst_ps, rst_done = sem("rst_ps"), sem("rst_done")
        v2_done = sem("v2_done")
        yt2_ps, den2_done, y2b_done = sem("yt2_ps"), sem("den2_done"), sem("y2b_done")
        ytb_ps, ytb_done = sem("ytb_ps"), sem("ytb_done")
        prb_ps, x1_done = sem("prb_ps"), sem("x1_done")
        kept, h1_kept = sem("kept"), sem("h1_kept")
        sq_done, xh_done, rr_done = sem("sq_done"), sem("xh_done"), sem("rr_done")
        lg_ps = sem("lg_ps")
        rt_dve, rt_exp = sem("rt_dve"), sem("rt_exp")
        wt_done = sem("wt_done")
        fw_done = sem("fw_done")
        fwt_ps, fwt_done = sem("fwt_ps"), sem("fwt_done")
        g_ps, u_ps = sem("g_ps"), sem("u_ps")
        th_done = sem("th_done")
        gb_done, hid_done = sem("gb_done"), sem("hid_done")
        down_done = sem("down_done")
        yd_done = sem("yd_done")
        o_ps = sem("o_ps")
        ot_done = sem("ot_done")

        RT, MIX = 13, 7

        def bc(ap, shape):
            return ap.broadcast_to(shape)

        block = ctx.enter_context(nc.Block())

        @block.sync
        def _(sp):
            def load_images(c):
                src = x[bass.ds(c * G, G), 0].rearrange("b h t -> h b t")
                sp.dma_start(xs[0:HP, :, :], src).then_inc(ld_x, 16)
                sp.dma_start(xs[HP:128, :, 0:WX - 1], src[:, :, 1:WX]).then_inc(ld_x, 16)

            def load(c):
                if later(c):
                    sp.wait_ge(patch_ps, c)
                    load_images(c)

            def store(c):
                sp.wait_ge(ot_done, c + 1)
                sp.dma_start(out[bass.ds(c * G, G)].rearrange("b t d -> t b d"), ot[:, :, :]).then_inc(stored, 16)

            sp.dma_start(cs[:, :], consts).then_inc(ld_w[1], 16)
            sp.dma_start(sm[:, :], small).then_inc(ld_w[2], 16)
            sp.dma_start(ch[:, :], chan).then_inc(ld_w[3], 16)
            sp.dma_start(wp[:, :, :], w_patch).then_inc(ld_w[0], 16)
            load_images(0)
            sp.dma_start(ws[:, :], w_split).then_inc(ld_w[4], 16)
            sp.dma_start(wf[:, :], w_full).then_inc(ld_w[5], 16)
            sp.dma_start(w2s[:, :, :], w2).then_inc(ld_w[6], 16)
            pipeline(sp, SYNC_ORDER, {"load": load, "store": store})
            sp.wait_ge(stored, 16 * NCH)

        @block.tensor
        def _(pe):
            def mm(o, l, r, start=True, stop=True):
                return nc.tensor.matmul(o, l, r, start=start, stop=stop)

            def split_mm(o, cols, r):
                mm(o, wh[:, cols], r, stop=False)
                return mm(o, wl[:, cols], r, start=False)

            def split_mm_t(o, stacked, cols):
                mm(o, stacked, wh[:, cols], stop=False)
                return mm(o, stacked, wl[:, cols], start=False)

            pm_readers = {
                "values1": (v1_done, 1, 1), "position": (pv_done, 1, 1), "patch": (emb_done, 1, 1),
                "tokens": (res_done, 1, 1), "xt1": (n1["xt_done"], 1, 1), "proj1a": (yta_done, 1, 1),
                "proj1b": (h1_done, 1, 1), "xt2": (n2["xt_done"], 1, 1), "p2a": (v2n_done, 1, 1),
                "p2b": (rpb_done, 1, 1), "proj2a": (ytb_done, 1, 1),
                "proj2b": (x1_done, 1, 1), "xt3": (n3["xt_done"], 1, 1), "logits": (rt_dve, RT, 2),
                "fwt0": (fwt_done, 4, 1), "fwt1": (fwt_done, 4, 2), "fwt2": (fwt_done, 4, 3),
                "fwt3": (fwt_done, 4, 4),
            }

            def pm_free(use, c, waited=None):
                for before, other in PM_BEFORE[use]:
                    if (before, other) == (waited, 0):
                        return
                    if exists(c + other):
                        signal, per, n = pm_readers[before]
                        pe.wait_ge(signal, (c + other) * per + n)
                        return

            def patch(c, part):
                if part == 0:
                    if isinstance(c, int) and c == 0:
                        pe.wait_ge(ld_w[0], 16)
                    pe.wait_ge(ld_x, 32 * c + 32)
                    pm_free("patch", c)
                for m in range(4 * part, min(4 * part + 4, PAIRS)):
                    r0 = C * (m % 2)
                    last = nc.tensor.matmul(pM[r0:r0 + C, 0:G * NP], wp[:, m, :],
                                            xs[:, :, 2 * m:2 * m + SW * (NP - 1) + 1:SW], start=m < 2,
                                            stop=m >= PAIRS - 2, skip_group_check=True)
                if part == 3:
                    last.then_inc(patch_ps, 1)

            def tokens(c):
                pe.wait_ge(emb_done, c + 1)
                pm_free("tokens", c, waited="patch")
                if isinstance(c, int) and c == 0:
                    pe.wait_ge(casts, 1)
                for b in range(G):
                    last = mm(pM[0:T, b * C:b * C + C], emb[:, b, :], fold)
                last.then_inc(tok_ps, 1)
                if isinstance(c, int) and c == 0:
                    positional()

            def positional():
                pe.wait_ge(pos_dve, 7)
                for h in range(H1):
                    last = nc.tensor.transpose(pS[0:T, h // 4, h % 4 * T:h % 4 * T + T], pos_b[:, h, :],
                                               ident[0:T, 0:T])
                last.then_inc(pos_pe, 1)

            def to_channels(name, n):
                def step(c):
                    pm_free(name, c)
                    pe.wait_ge(n["ysp_done"], c + 1)
                    for b in range(G):
                        last = nc.tensor.transpose(pM[:, b * TP:b * TP + T],
                                                   n["ysp"][:, b].rearrange("p a c -> p (a c)").bitcast(F),
                                                   ident[0:T, 0:T])
                    last.then_inc(n["xt_ps"], 1)
                return step

            def queries(c, t):
                pe.wait_ge(n1["xt_done"], c + 1)
                if t >= 2:
                    pe.wait_ge(qk1_done, c * 4 + t - 1)
                elif later(c):
                    pe.wait_ge(mix, c * MIX - MIX + 4)
                split_mm(pS[:, t % 2, 0:GT], slice(QK1 + t * 128, QK1 + t * 128 + 128),
                         xt1[:, :, :].rearrange("p b t -> p (b t)")).then_inc(qk1_ps, 1)

            def values1(c):
                pm_free("values1", c)
                for b in range(G):
                    last = split_mm_t(pM[0:T, b * C:b * C + C], xt1[:, b, 0:T], slice(V1C, V1C + C))
                last.then_inc(v1_ps, 1)

            def position(c):
                pm_free("position", c)
                pe.wait_ge(v1_done, c + 1)
                for h in range(H1):
                    last = mm(pM[0:T, h * 32:h * 32 + 32], pos_t[:, h, :], v1[:, :, h, 0:D1])
                last.then_inc(pv_ps, 1)

            def s1(c, b, half):
                if half == 0:
                    if b == 0:
                        pe.wait_ge(qk1_done, c * 4 + 4)
                    else:
                        pe.wait_ge(a1["avt_done"], c * G + b)
                else:
                    pe.wait_ge(s1_half, c * G + b + 1)
                for j in (2 * half, 2 * half + 1):
                    for t in range(2):
                        at = (j // 2 * 2 + t) * TP
                        last = mm(pS[0:T, j % 2, at:at + TP], qk1[32 * j:32 * j + 32, t, b * TP:b * TP + T],
                                  qk1[32 * j:32 * j + 32, 2 + t, b * TP:b * TP + TP])
                last.then_inc(a1["s_ps"] if half else s1_half, 1)

            def st1(c, b, half):
                if half == 0:
                    pe.wait_ge(a1["qm_done"], c * G + b + 1)
                else:
                    pe.wait_ge(st1_half, c * G + b + 1)
                for j in (2 * half, 2 * half + 1):
                    for t in range(2):
                        at = (j // 2 * 2 + t) * TP
                        last = mm(pS[0:T, j % 2, at:at + TP], qk1[32 * j:32 * j + 32, 2 + t, b * TP:b * TP + T],
                                  qm1[32 * j:32 * j + 32, t, :])
                last.then_inc(a1["st_ps"] if half else st1_half, 1)

            def maxima_t(a, mx, bank):
                def step(c, b):
                    pe.wait_ge(a["mx_done"], c * G + b + 1)
                    for t in range(2):
                        last = nc.tensor.transpose(bank[:, 0, t * TP:t * TP + T], mx[:, t].bitcast(F), ident[0:T, 0:T])
                    last.then_inc(a["mt_ps"], 1)
                return step

            def av1(c, b):
                pe.wait_ge(a1["ex_done"], c * G + b + 1)
                for t in range(2):
                    for j in range(4):
                        at = (j // 2 * 2 + t) * TP
                        last = mm(pS[32 * j:32 * j + 32, 0, t * TP:t * TP + TP], v1[:, b, 4 * t + j, :],
                                  ex1[:, b % 2, j % 2, at:at + TP])
                last.then_inc(a1["av_ps"], 1)

            def yt1(c):
                pe.wait_ge(a1["avt_done"], c * G + G)
                for b in range(G):
                    for t in range(2):
                        at = (b % 2) * 256 + t * 128
                        last = nc.tensor.transpose(pS[0:T, b // 2, at:at + 128], avt1[:, b, t * TP:t * TP + T], ident)
                last.then_inc(yt1_ps, 1)

            def projection(name, y_done, y, yt_ps, yt, yt_done, pr_ps, w):
                def to_rows(c):
                    pm_free(name + "a", c)
                    pe.wait_ge(y_done, c + 1)
                    for q in range(2):
                        last = nc.tensor.transpose(pM[:, q * TP:q * TP + T],
                                                   y[:, 2 * q:2 * q + 2].rearrange("p b c -> p (b c)"), ident[0:T, 0:T])
                    last.then_inc(yt_ps, 1)

                def project(c):
                    pe.wait_ge(yt_done, c + 1)
                    pm_free(name + "b", c, waited=name + "a")
                    if isinstance(c, int) and c == 0:
                        pe.wait_ge(ld_w[5], 16)
                    for q in range(2):
                        last = mm(pM[0:T, q * 128:q * 128 + 128], yt[:, q, 0:T], wf[:, w:w + 128])
                    last.then_inc(pr_ps, 1)
                return to_rows, project

            proj1a, proj1b = projection("proj1", y2a_done, y2a, yta_ps, yta, yta_done, pra_ps, WPROJ)
            proj2a, proj2b = projection("proj2", y2b_done, y2b, ytb_ps, ytb, ytb_done, prb_ps, WOUT)

            def p2a(c):
                pe.wait_ge(n2["xt_done"], c + 1)
                pm_free("p2a", c)
                for b in range(G):
                    last = split_mm_t(pM[0:T, b * 128:b * 128 + 128], xt2[:, b, 0:T], slice(QKV2, QKV2 + 128))
                last.then_inc(p2a_ps, 1)

            def p2b(c):
                pm_free("p2b", c)
                for b in range(G):
                    last = split_mm_t(pM[0:T, b * 96:b * 96 + 96], xt2[:, b, 0:T], slice(ROT2, ROT2 + 96))
                last.then_inc(p2b_ps, 1)

            def rst(c, t):
                if t == 0:
                    pe.wait_ge(rs_act, c + 1)
                    pe.wait_ge(rs_pool, c + 1)
                    if later(c):
                        pe.wait_ge(y2b_done, c)
                if t == 2:
                    pe.wait_ge(rst_done, c * 3 + 1)
                for b in range(G):
                    last = nc.tensor.transpose(pT[:, t % 2, b * TP:b * TP + T],
                                               rs[:, b, 2 * t:2 * t + 2].rearrange("p a c -> p (a c)").bitcast(F),
                                               ident[0:T, 0:T])
                last.then_inc(rst_ps, 1)

            def s2(c, b):
                if b == 0:
                    pe.wait_ge(rst_done, c * 3 + 3)
                else:
                    pe.wait_ge(a2["avt_done"], c * G + b)
                for i in range(2):
                    nc.tensor.matmul(pT[0:T, i, 0:2 * TP], identb[0:T, 0:T], maskb[0:T, 0, :], start=True, stop=False,
                                     skip_group_check=True)
                for i in range(2):
                    for t in range(2):
                        last = nc.tensor.matmul(pT[0:T, i, t * TP:t * TP + TP],
                                                qk2[64 * i:64 * i + 64, t, b * TP:b * TP + T],
                                                qk2[64 * i:64 * i + 64, 2, b * TP:b * TP + TP], start=False,
                                                stop=t == 1, skip_group_check=True)
                last.then_inc(a2["s_ps"], 1)

            def st2(c, b):
                pe.wait_ge(a2["qm_done"], c * G + b + 1)
                for i in range(2):
                    nc.tensor.matmul(pT[0:T, i, 0:2 * TP], identb[0:T, 0:T], maskb[0:T, 1, :], start=True, stop=False,
                                     skip_group_check=True)
                for i in range(2):
                    for t in range(2):
                        last = nc.tensor.matmul(pT[0:T, i, t * TP:t * TP + TP],
                                                qk2[64 * i:64 * i + 64, 2, b * TP:b * TP + T],
                                                qm2[64 * i:64 * i + 64, t, :], start=False, stop=t == 1,
                                                skip_group_check=True)
                last.then_inc(a2["st_ps"], 1)

            def av2(c, b):
                pe.wait_ge(a2["ex_done"], c * G + b + 1)
                if b == 0:
                    pe.wait_ge(v2_done, c + 1)
                for h in range(H2):
                    i, t = h // 2, h % 2
                    last = mm(pT[32 * h:32 * h + 32, 0, 0:TP], v2[:, b, i, :], ex2[:, b % 2, i, t * TP:t * TP + TP])
                last.then_inc(a2["av_ps"], 1)

            def yt2(c):
                pe.wait_ge(a2["avt_done"], c * G + G)
                for b in range(G):
                    last = nc.tensor.transpose(pT[0:T, 0, b * 128:b * 128 + 128], avt2[:, b, 0:T], ident)
                last.then_inc(yt2_ps, 1)

            def logits(c):
                pe.wait_ge(n3["xt_done"], c + 1)
                pm_free("logits", c, waited="xt3")
                for b in range(G):
                    last = split_mm_t(pM[0:T, b * NE:b * NE + NE], xt3[:, b, 0:T], slice(ROUT, ROUT + NE))
                last.then_inc(lg_ps, 1)

            def fwt_step(c, p):
                pm_free(f"fwt{p}", c)
                pe.wait_ge(fw_done, c + 1)
                for b in range(G):
                    last = nc.tensor.transpose(pM[:, b * TP:b * TP + T],
                                               fw[:, b, 2 * p:2 * p + 2].rearrange("p e c -> p (e c)"), ident[0:T, 0:T])
                last.then_inc(fwt_ps, 1)

            def down(c, k):
                pe.wait_ge(hid_done, c * TILES + k + 2)
                if k == 0 and later(c):
                    pe.wait_ge(yd_done, c)
                for n in (k, k + 1):
                    r0 = 64 * (n % 2)
                    last = nc.tensor.matmul(pY[r0:r0 + C, 0:GT], w2s[:, n, :], hid[:, n % 4, :],
                                            start=k == 0, stop=k == TILES - 2, skip_group_check=True)
                last.then_inc(down_done, 1)

            def gate(c, k):
                if k == 0:
                    pe.wait_ge(kept, c + 1)
                    if later(c):
                        pe.wait_ge(ot_done, c)
                    else:
                        pe.wait_ge(w_half_done, 2)
                else:
                    pe.wait_ge(gb_done, c * TILES + k)
                cols = slice(W1C + k * HT_ROWS, W1C + k * HT_ROWS + HT_ROWS)
                split_mm(pG[0:HT_ROWS, 0:GT], cols, xte[:, :, :].rearrange("p b t -> p (b t)")).then_inc(g_ps, 1)

            def up(c, k):
                if k % 3 == 0:
                    pe.wait_ge(fwt_done, c * 4 + k // 3 + 1)
                if k > 0 or later(c):
                    pe.wait_ge(hid_done, c * TILES + k)
                mm(pU[0:HT_ROWS, 0:GT], wf[:, W3C + k * HT_ROWS:W3C + k * HT_ROWS + HT_ROWS],
                   fwt[:, k // 3].rearrange("p b t -> p (b t)")).then_inc(u_ps, 1)

            def expert_sum(c):
                pe.wait_ge(yd_done, c + 1)
                for b in range(G):
                    last = mm(pG[0:T, b * C:b * C + C], yd[:, b * TP:b * TP + T], fold)
                last.then_inc(o_ps, 1)

            def start():
                pe.wait_ge(w_low_done, 3)
                pe.wait_ge(pos_act, 3)

            pipeline(pe, TENSOR_ORDER, {
                "patch": patch, "tokens": tokens, "xt1": to_channels("xt1", n1), "queries": queries,
                "values1": values1, "position": position, "s1": s1, "st1": st1, "mt1": maxima_t(a1, mx1, pS),
                "av1": av1, "yt1": yt1, "proj1a": proj1a, "proj1b": proj1b, "xt2": to_channels("xt2", n2),
                "p2a": p2a, "p2b": p2b, "rst": rst, "s2": s2, "st2": st2, "mt2": maxima_t(a2, mx2, pT), "av2": av2,
                "yt2": yt2, "proj2a": proj2a, "proj2b": proj2b, "xt3": to_channels("xt3", n3), "logits": logits,
                "fwt": fwt_step, "gate": gate, "up": up, "down": down, "sum": expert_sum}, start)

        @block.scalar
        def _(act):
            def copy(o, i):
                return nc.scalar.activation(o, i, ACT.Copy)

            def embed(c):
                act.wait_ge(patch_ps, c + 1)
                nc.scalar.activation(emb[:, :, 1:T], pM[:, 0:G * NP].rearrange("p (b n) -> p b n", b=G), ACT.Identity,
                                     bias=ch[:, BPATCH:BPATCH + 1]).then_inc(emb_done, 1)

            def highs(n, c):
                act.wait_ge(n["yn_done"], c + 1)
                copy(n["ysp"][:, :, 0], n["yn"][:, :, :]).then_inc(n["yh_done"], 1)

            def center(n, k, dst, src):
                for b in range(G):
                    last = nc.scalar.activation(dst[:, b, :], src[:, b, :], ACT.Identity,
                                                bias=n["nb"][:, k * G + b:k * G + b + 1],
                                                scale=n["y"][:, k * G + b:k * G + b + 1])
                return last

            def ln1_out(c):
                act.wait_ge(n1["root"], (c + 1) * n1["roots"])
                center(n1, 0, n1["yn"], res).then_inc(n1["yn_done"], 1)
                highs(n1, c)

            def ln2_out(c):
                act.wait_ge(n2["root"], (c + 1) * n2["roots"])
                center(n2, 1, n2["yn"], h1).then_inc(n2["yn_done"], 1)
                highs(n2, c)

            def zz_out(c):
                if later(c):
                    act.wait_ge(h1_kept, c)
                center(n2, 0, zz, h1).then_inc(zz_done, 1)

            def rms_out(c):
                highs(n3, c)

            def stacked(n, dst):
                def step(c):
                    act.wait_ge(n["xt_ps"], c + 1)
                    if dst is xt3 and later(c):
                        act.wait_ge(kept, c)
                    copy(dst[:, :, 0:T],
                         pM[:, 0:GT].rearrange("p (b t) -> p b t", b=G)[:, :, 0:T]).then_inc(n["xt_done"], 1)
                return step

            def queries(c, t):
                act.wait_ge(qk1_ps, c * 4 + t + 1)
                nc.scalar.activation(hi[:, t], pS[:, t % 2, 0:GT], ACT.Identity,
                                     bias=cs[:, HMASK + 2:HMASK + 3] if t >= 2 else 0.0).then_inc(hi_done, 1)

            def tokens(c):
                act.wait_ge(tok_ps, c + 1)
                if later(c):
                    act.wait_ge(resb_done, c)
                nc.scalar.activation(res[:, :, :].rearrange("p b c -> p (b c)"), pM[0:T, 0:G * C],
                                     ACT.Gelu).then_inc(gelu_done, 1)
                act.wait_ge(gelu_done, c + 1)
                copy(res[0:1, :, :], bc(sm[0:1, CLS:CLS + C].rearrange("p (b c) -> p b c", b=1),
                                        [1, G, C])).then_inc(res_done, 1)
                if isinstance(c, int) and c == 0:
                    positional()

            def positional():
                act.wait_ge(pos_pe, 1)
                copy(pos_t[0:T, :, :].rearrange("p (a h) t -> p a h t", a=2),
                     pS[0:T, :, 0:4 * T].rearrange("p a (h t) -> p a h t", h=4)).then_inc(pos_act, 1)

            def values1(c):
                act.wait_ge(v1_ps, c + 1)
                copy(v1[0:T, :, :, 0:D1],
                     pM[0:T, 0:G * C].rearrange("p (b h d) -> p b h d", b=G, h=H1)).then_inc(v1_done, 1)

            def position(c):
                act.wait_ge(pv_ps, c + 1)
                copy(pv[:, :, :, :].rearrange("p h b d -> p (h b d)"), pM[0:T, 0:G * C]).then_inc(pv_done, 1)

            def exps(a, ex, bank, width, scale, c, b):
                act.wait_ge(a["st_ps"], c * G + b + 1)
                if b >= 2 or later(c):
                    act.wait_ge(a["av_ps"], c * G + b - 1)
                nc.scalar.activation(ex[0:T, b % 2, :, 0:width], bank[0:T, :, 0:width], ACT.Exp,
                                     scale=scale).then_inc(a["ex_done"], 1)

            def exps1(c, b):
                exps(a1, ex1, pS, 4 * TP, D1 ** -0.5, c, b)

            def exps2(c, b):
                exps(a2, ex2, pT, 2 * TP, D2 ** -0.5, c, b)

            def values(a, avt, bank, width):
                def step(c, b):
                    act.wait_ge(a["av_ps"], c * G + b + 1)
                    copy(avt[:, b, 0:width], bank[:, 0, 0:width]).then_inc(a["avt_done"], 1)
                return step

            def mixed(ps, yt, done):
                def step(c):
                    act.wait_ge(ps, c + 1)
                    copy(yt[:, :, 0:T], pM[:, 0:2 * TP].rearrange("p (q t) -> p q t", q=2)[:, :, 0:T]).then_inc(done, 1)
                return step

            def p2a(c):
                act.wait_ge(rpa_done, c + 1)
                copy(v2n[:, :, :, :], pM[0:T].rearrange("p (b n) -> p b n", b=G)[:, :, 96:128]
                     .rearrange("p b (k d) -> p b k d", k=KV2)).then_inc(v2n_done, 1)

            def rope(c):
                act.wait_ge(rp_done, c + 1)
                if later(c):
                    act.wait_ge(rst_ps, c * 3)
                heads = rp[:, :, :].rearrange("p b (h d) -> p b h d", d=D2)
                copy(rph[:, :, :], rp[:, :, :]).then_inc(rph_done, 1)
                copy(rs[:, :, :, 0:16], heads)
                copy(rs[:, :, 0:4, 32:48], heads[:, :, 0:4])
                copy(rs[:, :, 4:6, 16:32], heads[:, :, 4:6]).then_inc(rs_act, 1)

            def v2_step(c):
                act.wait_ge(v2n_done, c + 1)
                copy(v2[0:T, :, :, 0:D2], v2n[:, :, :, :]).then_inc(v2_done, 1)

            def rst(c, t):
                act.wait_ge(rst_ps, c * 3 + t + 1)
                copy(qk2[:, t].rearrange("p (b t) -> p b t", b=G)[:, :, 0:T],
                     pT[:, t % 2, 0:GT].rearrange("p (b t) -> p b t", b=G)[:, :, 0:T]).then_inc(rst_done, 1)

            def router(c):
                act.wait_ge(rt_dve, c * RT + 2)
                nc.scalar.activation(rt[:, 1], rt[:, 0], ACT.Exp).then_inc(rt_exp, 1)

            def fwt_step(c, p):
                act.wait_ge(fwt_ps, c * 4 + p + 1)
                copy(fwt[:, p, :, 0:T],
                     pM[:, 0:GT].rearrange("p (b t) -> p b t", b=G)[:, :, 0:T]).then_inc(fwt_done, 1)

            def tile(c, k):
                act.wait_ge(g_ps, c * TILES + k + 1)
                if k > 0 or later(c):
                    act.wait_ge(gb_done, c * TILES + k)
                nc.scalar.activation(th[:, :], pG[0:HT_ROWS, 0:GT], ACT.Tanh, scale=0.5).then_inc(th_done, 1)

            def expert_sum(c):
                act.wait_ge(down_done, c * 6 + 6)
                copy(yd[:, :], pY[:, 0:GT]).then_inc(yd_done, 1)

            act.wait_ge(ld_w[2], 16)
            nc.scalar.activation(pos_s[:, 3], sm[0:T, GATE:GATE + H1], ACT.Exp, scale=-1.0).then_inc(pos_act, 1)
            act.wait_ge(pos_pool, 7)
            nc.scalar.activation(pos_a[:, :, :], pos_b[:, :, :], ACT.Exp).then_inc(pos_act, 1)
            act.wait_ge(zeroed, 1)
            act.wait_ge(ld_w[1], 16)
            act.wait_ge(ld_w[3], 16)

            pipeline(act, SCALAR_ORDER, {
                "embed": embed, "ln1_out": ln1_out, "xt1": stacked(n1, xt1), "queries": queries, "tokens": tokens,
                "values1": values1, "position": position, "st1": exps1, "av1": values(a1, avt1, pS, 2 * TP), "proj1a": mixed(yta_ps, yta, yta_done),
                "ln2_out": ln2_out, "zz": zz_out, "xt2": stacked(n2, xt2), "p2a": p2a, "rope": rope, "v2": v2_step, "rst": rst,
                "st2": exps2, "av2": values(a2, avt2, pT, TP), "proj2a": mixed(ytb_ps, ytb, ytb_done),
                "rms_out": rms_out, "xt3": stacked(n3, xt3), "router": router, "fwt": fwt_step, "tile": tile,
                "sum": expert_sum})

        @block.vector
        def _(dve):
            V = nc.vector

            def moments(n, c, src):
                bst, bsum, mv, stat, at = n["bst"], n["bsum"], n["mv"], n["stat"], c * n["per"]
                for b in range(G):
                    last = V.bn_stats(bst[:, b, :], src[:, b, :])
                last.then_inc(stat, 1)
                dve.wait_ge(stat, at + 1)
                V.tensor_tensor(bsum[:, :, 0:2], bst[:, :, 1:3], bst[:, :, 4:6], ALU.add)
                V.tensor_tensor(bsum[:, :, 2], bst[:, :, 1], bst[:, :, 4], ALU.subtract).then_inc(stat, 1)
                dve.wait_ge(stat, at + 2)
                V.scalar_tensor_tensor(bsum[:, :, 3], bsum[:, :, 2], 0.25, bsum[:, :, 2], ALU.mult, ALU.mult)
                V.tensor_scalar(mv[:, :, 0], bsum[:, :, 0], -0.5, None, ALU.mult).then_inc(stat, 1)
                dve.wait_ge(stat, at + 3)
                V.scalar_tensor_tensor(mv[:, :, 1], bsum[:, :, 1], 1.0 / C, bsum[:, :, 3], ALU.mult,
                                       ALU.add).then_inc(stat, 1)
                dve.wait_ge(stat, at + 4)

            def root_start(n, at):
                dve.wait_ge(n["stat"], at)
                V.tensor_scalar(n["w"][:, :], n["v"][:, :], -0.5, None, ALU.mult)
                V.tensor_scalar(n["y"][:, :].bitcast(I32), n["v"][:, :].bitcast(I32), -0.5, MAGIC, ALU.mult,
                                ALU.add).then_inc(n["stat"], 1)

            def ln1(c):
                dve.wait_ge(res_done, c + 1)
                moments(n1, c, res)
                V.tensor_scalar(n1["v"][:, :], n1["mv"][:, :, 1], LN_EPS, None, ALU.add).then_inc(n1["stat"], 1)
                root_start(n1, c * n1["per"] + 5)

            def queries(c, t):
                dve.wait_ge(hi_done, c * 4 + t + 1)
                V.scalar_tensor_tensor(qk1[:, t], hi[:, t].bitcast(F), cs[:, HMASK + t // 2:HMASK + t // 2 + 1],
                                       pS[:, t % 2, 0:GT], ALU.mult, ALU.add).then_inc(qk1_done, 1)

            def maxima(a, c, b, nm, scores):
                dve.wait_ge(a["s_ps"], c * G + b + 1)
                V.tensor_reduce(nm[:, :], scores, AX, ALU.max, negate=True).then_inc(a["nm_done"], 1)
            def maxima_parts(a, nm, heads_hi, heads_lo):
                def step(c, b):
                    dve.wait_ge(a["nm_done"], c * G + b + 1)
                    V.tensor_copy(heads_hi, nm[:, :].rearrange("p (a b t) -> p a b t", a=2, t=2)).then_inc(a["mh_done"], 1)
                    dve.wait_ge(a["mh_done"], c * G + b + 1)
                    V.tensor_tensor(heads_lo, nm[:, :].rearrange("p (a b t) -> p a b t", a=2, t=2),
                                    heads_hi.bitcast(F), ALU.subtract).then_inc(a["mx_done"], 1)
                return step

            m1 = mx1[:, :, :].rearrange("p t (j2 bk r) -> p bk j2 t r", j2=2, bk=2)
            m2 = mx2[:, :, :].rearrange("p t (a i r) -> p i a t r", i=2, a=1)

            def s1(c, b):
                maxima(a1, c, b, nm1, pS[0:T, :, 0:4 * TP].rearrange("p a (s t) -> p a s t", t=TP)[:, :, :, 0:T])

            def s2(c, b):
                maxima(a2, c, b, nm2, pT[0:T, :, 0:2 * TP].rearrange("p a (s t) -> p a s t", t=TP)[:, :, :, 0:T])

            def shifted(a, qm, qk, bank):
                def step(c, b):
                    dve.wait_ge(a["mt_ps"], c * G + b + 1)
                    if b > 0 or later(c):
                        dve.wait_ge(a["st_ps"], c * G + b)
                    V.tensor_tensor(qm[:, :, 0:T], bank[:, 0, 0:2 * TP].rearrange("p (a t) -> p a t", a=2)[:, :, 0:T],
                                    qk[:, 0:2, b * TP:b * TP + T].bitcast(F), ALU.add).then_inc(a["qm_done"], 1)
                return step

            def yt1(c):
                dve.wait_ge(yt1_ps, c + 1)
                tok = pS[0:T, :, :].rearrange("p a n -> p (a n)").rearrange("p (b h r) -> p b h r", b=G, h=H1)
                s = [den1[:, i] for i in range(4)]
                k = c * MIX
                y2h = y2a[:, :, :].rearrange("p b (h d) -> p b h d", h=H1)
                V.reciprocal(s[0], tok[:, :, :, D1]).then_inc(mix, 1)
                dve.wait_ge(mix, k + 1)
                V.tensor_tensor(s[1], s[0], bc(one_g.rearrange("p (a h) -> p a h", a=1), [T, G, H1]),
                                ALU.mult).then_inc(mix, 1)
                dve.wait_ge(mix, k + 2)
                V.tensor_tensor(s[2], tok[:, :, :, D1], s[1], ALU.mult).then_inc(mix, 1)
                V.tensor_tensor(y2h, tok[:, :, :, 0:D1], bc(s[1].rearrange("p b (h d) -> p b h d", d=1), [T, G, H1, D1]),
                                ALU.mult).then_inc(mix, 1)

            def mixture(c):
                s = [den1[:, i] for i in range(4)]
                k = c * MIX
                y2h = y2a[:, :, :].rearrange("p b (h d) -> p b h d", h=H1)
                dve.wait_ge(mix, k + 4)
                V.tensor_tensor(s[3], s[2], bc(pos_sum.rearrange("p (a h) -> p a h", a=1), [T, G, H1]),
                                ALU.add).then_inc(mix, 1)
                dve.wait_ge(pv_done, c + 1)
                V.tensor_tensor(y2h, y2h, pv[:, :, :, :].rearrange("p h b d -> p b h d"), ALU.add).then_inc(mix, 1)
                dve.wait_ge(mix, k + 6)
                V.reciprocal(s[2], s[3]).then_inc(mix, 1)
                dve.wait_ge(mix, k + 7)
                V.tensor_tensor(y2h, y2h, bc(s[2].rearrange("p b (h d) -> p b h d", d=1), [T, G, H1, D1]),
                                ALU.mult).then_inc(y2a_done, 1)

            def proj1b(c):
                dve.wait_ge(pra_ps, c + 1)
                dve.wait_ge(resb_done, c + 1)
                if later(c):
                    dve.wait_ge(h1_kept, c)
                V.tensor_tensor(h1[:, :, :].rearrange("p b c -> p (b c)"), pM[0:T, 0:G * C],
                                resb[:, :, :].rearrange("p b c -> p (b c)"), ALU.add).then_inc(h1_done, 1)

            def ln2(c):
                dve.wait_ge(h1_done, c + 1)
                moments(n2, c, h1)
                mv, v = n2["mv"], n2["v"]
                V.tensor_scalar(v[:, 0:G], mv[:, :, 1], LN_EPS, None, ALU.add)
                V.tensor_scalar(v[:, G:2 * G], mv[:, :, 1], 1.0 + RMS_EPS, RMS_EPS * LN_EPS, ALU.mult,
                                ALU.add).then_inc(n2["stat"], 1)
                root_start(n2, c * n2["per"] + 5)

            def rotate(ps, width, tab, dst, done):
                def step(c):
                    dve.wait_ge(ps, c + 1)
                    V.tensor_tensor(dst[:, :, :], pM[0:T, 0:G * width].rearrange("p (b n) -> p b n", b=G)[:, :, 0:96],
                                    bc(cs[0:T, tab:tab + 96].rearrange("p (a n) -> p a n", a=1), [T, G, 96]),
                                    ALU.mult).then_inc(done, 1)
                return step

            def yt2(c):
                dve.wait_ge(yt2_ps, c + 1)
                tok2 = pT[0:T, 0].rearrange("p (b h r) -> p b h r", b=G, h=H2)
                V.reciprocal(den2[:, :, :], tok2[:, :, :, D2]).then_inc(den2_done, 1)
                dve.wait_ge(den2_done, c + 1)
                V.tensor_tensor(y2b[:, :, :].rearrange("p b (h d) -> p b h d", h=H2), tok2[:, :, :, 0:D2],
                                bc(den2[:, :, :].rearrange("p b (h d) -> p b h d", d=1), [T, G, H2, D2]),
                                ALU.mult).then_inc(y2b_done, 1)

            def proj2b(c):
                dve.wait_ge(prb_ps, c + 1)
                dve.wait_ge(h1_kept, c + 1)
                V.tensor_tensor(x1[:, :, :].rearrange("p b c -> p (b c)"), pM[0:T, 0:G * C],
                                zzk[:, :, :].rearrange("p b c -> p (b c)"), ALU.add).then_inc(x1_done, 1)

            def rms(c):
                stat, at = n3["stat"], c * n3["per"]
                dve.wait_ge(sq_done, c + 1)
                V.tensor_reduce(n3["a"][:, :], sq[:, :, :], AX, ALU.add).then_inc(stat, 1)
                dve.wait_ge(stat, at + 1)
                V.tensor_scalar(n3["v"][:, :], n3["a"][:, :], 1.0 / C, RMS_EPS, ALU.mult, ALU.add).then_inc(stat, 1)
                root_start(n3, at + 2)

            def one(ap):
                return ap.rearrange("p (b e) -> p b e", e=1)

            def logits(c):
                lg = pM[0:T, 0:G * NE].rearrange("p (b e) -> p b e", b=G)
                dve.wait_ge(lg_ps, c + 1)
                V.tensor_reduce(rsm[:, 0], lg, AX, ALU.max).then_inc(rt_dve, 1)
                dve.wait_ge(rt_dve, c * RT + 1)
                V.tensor_tensor(rt[:, 0], lg, bc(one(rsm[:, 0]), [T, G, NE]), ALU.subtract).then_inc(rt_dve, 1)

            ff = lambda t: t[:, :, :, :].rearrange("p b e f -> p b (e f)")

            def probabilities(c):
                k = c * RT
                dve.wait_ge(rt_exp, c + 1)
                V.tensor_reduce(rsm[:, 1], rt[:, 1], AX, ALU.add).then_inc(rt_dve, 1)
                dve.wait_ge(rt_dve, k + 3)
                V.reciprocal(rsm[:, 2], rsm[:, 1]).then_inc(rt_dve, 1)
                dve.wait_ge(rt_dve, k + 4)
                V.tensor_tensor(rt[:, 2], rt[:, 1], bc(one(rsm[:, 2]), [T, G, NE]), ALU.mult).then_inc(rt_dve, 1)

            def compare(c):
                k = c * RT
                dve.wait_ge(rt_dve, k + 5)
                for b in range(G):
                    pe_ = bc(rt[:, 2, b].rearrange("p (e f) -> p e f", f=1), [T, NE, NE])
                    pf_ = bc(rt[:, 2, b].rearrange("p (e f) -> p e f", e=1), [T, NE, NE])
                    V.tensor_tensor(cmp1[:, b], pf_, pe_, ALU.is_gt)
                    last = V.tensor_tensor(cmp2[:, b], pf_, pe_, ALU.is_equal)
                last.then_inc(rt_dve, 1)
                dve.wait_ge(rt_dve, k + 6)
                V.tensor_tensor(ff(cmp2), ff(cmp2), bc(cs[0:T, TRI:TRI + 64].rearrange("p (b e) -> p b e", b=1),
                                                       [T, G, 64]), ALU.mult).then_inc(rt_dve, 1)
                dve.wait_ge(rt_dve, k + 7)
                V.tensor_tensor(ff(cmp1), ff(cmp1), ff(cmp2), ALU.add).then_inc(rt_dve, 1)
                dve.wait_ge(rt_dve, k + 8)
                V.tensor_reduce(rt[:, 3], cmp1[:, :, :, :], AX, ALU.add).then_inc(rt_dve, 1)

            def top2(c):
                k = c * RT
                dve.wait_ge(rt_dve, k + 9)
                V.scalar_tensor_tensor(rt[:, 4], rt[:, 3], 1.5, rt[:, 2], ALU.is_lt, ALU.mult).then_inc(rt_dve, 1)
                dve.wait_ge(rt_dve, k + 10)
                V.tensor_reduce(rsm[:, 3], rt[:, 4], AX, ALU.add).then_inc(rt_dve, 1)
                dve.wait_ge(rt_dve, k + 11)
                V.tensor_scalar(rsm[:, 0], rsm[:, 3], 1e-9, None, ALU.add).then_inc(rt_dve, 1)
                dve.wait_ge(rt_dve, k + 12)
                V.reciprocal(rsm[:, 1], rsm[:, 0]).then_inc(rt_dve, 1)
                dve.wait_ge(rt_dve, k + 13)
                V.tensor_tensor(rt[:, 5], rt[:, 4], bc(one(rsm[:, 1]), [T, G, NE]), ALU.mult).then_inc(wt_done, 1)

            def gated(c, k):
                dve.wait_ge(th_done, c * TILES + k + 1)
                V.scalar_tensor_tensor(gb[:, k % 2, :], th[:, :], 1.0, pG[0:HT_ROWS, 0:GT], ALU.add,
                                       ALU.mult).then_inc(gb_done, 1)

            def hidden(c, k):
                dve.wait_ge(gb_done, c * TILES + k + 1)
                dve.wait_ge(u_ps, c * TILES + k + 1)
                if k >= 4 or later(c):
                    dve.wait_ge(down_done, c * 6 + k // 2 - 1)
                V.tensor_tensor(hid[:, k % 4, :], gb[:, k % 2, :], pU[0:HT_ROWS, 0:GT], ALU.mult).then_inc(hid_done, 1)

            def expert_sum(c):
                dve.wait_ge(o_ps, c + 1)
                dve.wait_ge(rr_done, c + 1)
                if later(c):
                    dve.wait_ge(stored, 16 * c)
                V.tensor_tensor(ot[:, :, :].rearrange("p b c -> p (b c)"), pG[0:T, 0:G * C],
                                rr[:, :, :].rearrange("p b c -> p (b c)"), ALU.add).then_inc(ot_done, 1)

            for t in (xt1, xt2, xt3, qm1, qm2):
                V.memset(t[:, :, T:TP].bitcast(F), 0.0)
            for t in (qk1, qk2):
                V.memset(t[:, :, :].rearrange("p t (b s) -> p (t b) s", s=TP)[:, :, T:TP].bitcast(F), 0.0)
            V.memset(fwt[:, :, :, T:TP], 0.0)
            V.memset(emb[:, :, 0:1], 0.0)
            V.memset(pos_t[64:128, :, :], 0.0)
            V.memset(mx1[:, :, :].bitcast(F), 0.0)
            V.memset(mx2[:, :, :].bitcast(F), 0.0).then_inc(zeroed, 1)
            dve.wait_ge(zeroed, 1)
            dve.wait_ge(ld_w[1], 16)
            dve.wait_ge(ld_w[3], 16)
            V.tensor_copy(identb[:, :], ident)
            V.tensor_copy(maskb[:, :, :], cs[:, MROW:MROW + 4 * TP].rearrange("p (a t) -> p a t", a=2)).then_inc(casts, 1)
            dve.wait_ge(pos_act, 1)
            V.tensor_scalar(pos_s[:, 3], pos_s[:, 3], 1.0, None, ALU.add).then_inc(pos_dve, 1)
            dve.wait_ge(pos_dve, 1)
            V.reciprocal(pos_s[:, 3], pos_s[:, 3]).then_inc(pos_dve, 1)
            dve.wait_ge(pos_dve, 2)
            V.tensor_scalar(one_g, pos_s[:, 3], -1.0, 1.0, ALU.mult, ALU.add)
            dve.wait_ge(pos_pool, 6)
            V.tensor_reduce(pos_s[:, 0], pos_a[:, :, :], AX, ALU.max).then_inc(pos_dve, 1)
            dve.wait_ge(pos_act, 2)
            V.tensor_reduce(pos_s[:, 1], pos_a[:, :, :], AX, ALU.add).then_inc(pos_dve, 1)
            dve.wait_ge(pos_dve, 4)
            V.reciprocal(pos_s[:, 2], pos_s[:, 1]).then_inc(pos_dve, 1)
            dve.wait_ge(pos_dve, 5)
            V.tensor_tensor(pos_s[:, 2], pos_s[:, 2], pos_s[:, 3], ALU.mult).then_inc(pos_dve, 1)
            dve.wait_ge(pos_dve, 6)
            V.tensor_tensor(pos_b[:, :, :], pos_a[:, :, :],
                            bc(pos_s[:, 2].rearrange("p (h t) -> p h t", t=1), [T, H1, T]),
                            ALU.mult).then_inc(pos_dve, 1)
            dve.wait_ge(pos_dve, 7)
            V.tensor_reduce(pos_sum, pos_b[:, :, :], AX, ALU.add).then_inc(pos_dve, 1)
            dve.wait_ge(pos_dve, 8)
            def start():
                dve.wait_ge(ld_w[4], 16)
                for a, z, w in ((QK1, QKV2, None), (QKV2, ROUT, LN1W), (ROUT, NSPLIT, LN2W)):
                    scale = 1.0 if w is None else ch[:, w:w + 1]
                    last = V.tensor_scalar(wh[:, a:z], ws[:, a:z], scale, None, ALU.mult)
                last.then_inc(w_split_done, 1)
                dve.wait_ge(w_split_done, 1)
                for a, z, w in ((QK1, QKV2, None), (QKV2, ROUT, LN1W), (ROUT, NSPLIT, LN2W)):
                    scale = 1.0 if w is None else ch[:, w:w + 1]
                    V.scalar_tensor_tensor(wl[:, a:z], ws[:, a:z], scale, wh[:, a:z].bitcast(F), ALU.mult,
                                           ALU.subtract).then_inc(w_low_done, 1)
                dve.wait_ge(ld_w[5], 16)
                dve.wait_ge(ld_w[6], 16)
                V.tensor_scalar(w2s[:, :, :].rearrange("p k c -> p (k c)"), w2s[:, :, :].rearrange("p k c -> p (k c)"),
                                0.5, None, ALU.mult).then_inc(w_half_done, 1)
                V.tensor_scalar(wf[:, W3C:FEND], wf[:, W3C:FEND], ch[:, LN2W:LN2W + 1], None,
                                ALU.mult).then_inc(w_half_done, 1)

            pipeline(dve, VECTOR_ORDER, {
                "ln1": ln1, "queries": queries, "s1": s1,
                "mx1": maxima_parts(a1, nm1, m1[:, :, :, :, 24], m1[:, :, :, :, 25]),
                "mx2": maxima_parts(a2, nm2, m2[:, :, :, :, 48], m2[:, :, :, :, 49]),
                "mt1": shifted(a1, qm1, qk1, pS), "yt1": yt1, "mixture": mixture, "proj1b": proj1b, "ln2": ln2,
                "p2a": rotate(p2a_ps, 128, COSC, rp1, rpa_done), "p2b": rotate(p2b_ps, 96, SINC, rp2, rpb_done),
                "s2": s2, "mt2": shifted(a2, qm2, qk2, pT), "yt2": yt2, "proj2b": proj2b, "rms": rms,
                "logits": logits, "probabilities": probabilities,
                "compare": compare, "top2": top2, "gated": gated, "hidden": hidden, "sum": expert_sum}, start)

        @block.gpsimd
        def _(pool):
            P = nc.gpsimd

            def lows(n):
                def step(c):
                    pool.wait_ge(n["yh_done"], c + 1)
                    P.tensor_tensor(n["ysp"][:, :, 1], n["yn"][:, :, :], n["ysp"][:, :, 0].bitcast(F),
                                    ALU.subtract).then_inc(n["ysp_done"], 1)
                return step

            def root(n, c):
                (y, a, b, w), root, at = (n[t][:, :] for t in "yabw"), n["root"], c * n["roots"]
                half3 = bc(three_halves[:, :], [T, y.shape[1]])
                pool.wait_ge(n["stat"], c * n["per"] + n["per"])
                for i in range(3):
                    P.tensor_tensor(a, y, y, ALU.mult).then_inc(root, 1)
                    pool.wait_ge(root, at + 4 * i + 1)
                    P.tensor_tensor(b, a, w, ALU.mult).then_inc(root, 1)
                    pool.wait_ge(root, at + 4 * i + 2)
                    P.tensor_tensor(a, b, half3, ALU.add).then_inc(root, 1)
                    pool.wait_ge(root, at + 4 * i + 3)
                    P.tensor_tensor(y, a, y, ALU.mult).then_inc(root, 1)
                    pool.wait_ge(root, at + 4 * i + 4)

            def norm_root(n, k):
                def step(c):
                    root(n, c)
                    P.tensor_tensor(n["nb"][:, :].rearrange("p (k b) -> p k b", k=k),
                                    n["y"][:, :].rearrange("p (k b) -> p k b", k=k),
                                    bc(n["mv"][:, :, 0].rearrange("p (k b) -> p k b", k=1), [T, k, G]),
                                    ALU.mult).then_inc(n["root"], 1)
                return step

            def rms(c):
                root(n3, c)
                P.tensor_tensor(n3["yn"][:, :, :], x1[:, :, :],
                                bc(n3["y"][:, :].rearrange("p (b c) -> p b c", c=1), [T, G, C]),
                                ALU.mult).then_inc(n3["yn_done"], 1)

            def residual(c):
                pool.wait_ge(res_done, c + 1)
                if later(c):
                    pool.wait_ge(h1_done, c)
                P.tensor_tensor(resb[:, :, :], res[:, :, :],
                                bc(sm[0:T, BPROJ:BPROJ + C].rearrange("p (b c) -> p b c", b=1), [T, G, C]),
                                ALU.add).then_inc(resb_done, 1)

            def rope(c):
                pool.wait_ge(rpb_done, c + 1)
                P.tensor_tensor(rp[:, :, :], rp1[:, :, :], rp2[:, :, :], ALU.add).then_inc(rp_done, 1)
                pool.wait_ge(rph_done, c + 1)
                heads = rp[:, :, :].rearrange("p b (h d) -> p b h d", d=D2)
                highs = rph[:, :, :].rearrange("p b (h d) -> p b h d", d=D2).bitcast(F)
                P.tensor_tensor(rs[:, :, 0:4, 16:32], heads[:, :, 0:4], highs[:, :, 0:4], ALU.subtract)
                P.tensor_tensor(rs[:, :, 4:6, 32:48], heads[:, :, 4:6], highs[:, :, 4:6],
                                ALU.subtract).then_inc(rs_pool, 1)

            def squares(c):
                pool.wait_ge(x1_done, c + 1)
                P.tensor_tensor(sq[:, :, :], x1[:, :, :], x1[:, :, :], ALU.mult).then_inc(sq_done, 1)
                if later(c):
                    pool.wait_ge(rr_done, c)
                P.tensor_tensor(xh[:, :, :], x1[:, :, :], h1k[:, :, :], ALU.add).then_inc(xh_done, 1)

            def router(c):
                pool.wait_ge(wt_done, c + 1)
                for b in range(G):
                    last = P.tensor_tensor(fw[:, b], bc(n3["yn"][:, b].rearrange("p (e c) -> p e c", e=1), [T, NE, C]),
                                           bc(rt[:, 5, b].rearrange("p (e c) -> p e c", c=1), [T, NE, C]), ALU.mult)
                last.then_inc(fw_done, 1)

            def keep_sum(c):
                if later(c):
                    pool.wait_ge(ot_done, c)
                pool.wait_ge(xh_done, c + 1)
                pool.wait_ge(n3["xt_done"], c + 1)
                P.tensor_tensor(rr[:, :, :], xh[:, :, :], bc(zero[:, :, :], [T, G, C]), ALU.add).then_inc(rr_done, 1)
                P.tensor_copy(xte[:, :, :], xt3[:, :, :].bitcast(F)).then_inc(kept, 1)

            def keep_h1(c):
                pool.wait_ge(zz_done, c + 1)
                if later(c):
                    pool.wait_ge(x1_done, c)
                    pool.wait_ge(xh_done, c)
                P.tensor_tensor(zzk[:, :, :], zz[:, :, :], bc(zero[:, :, :], [T, G, C]), ALU.add)
                P.tensor_copy(h1k[:, :, :], h1[:, :, :]).then_inc(h1_kept, 1)

            for t in (v1, v2, ex1, ex2):
                P.memset(t[:, :, :, :], 0.0)
            P.memset(zero[:, :, :], 0.0)
            P.memset(three_halves[:, :], 1.5)
            P.memset(rs[:, :, :, :].bitcast(F), 0.0).then_inc(zeroed_pool, 1)
            pool.wait_ge(zeroed_pool, 1)
            P.memset(v1[0:T, :, :, D1:D1 + 1], 1.0)
            P.memset(v2[0:T, :, :, D2:D2 + 1], 1.0)
            P.memset(rs[:, :, 4:6, 48:50].bitcast(F), 1.0).then_inc(zeroed_pool, 1)
            pool.wait_ge(ld_w[1], 16)
            pool.wait_ge(ld_w[2], 16)
            wpos = sm[0:T, WPOS:WPOS + 24].rearrange("p (h k) -> p h k", k=3)
            dist = cs[0:T, DIST:DIST + 3 * T].rearrange("p (k t) -> p k t", k=3)
            n = 0
            for k in range(3):
                dst = pos_a if k == 0 else pos_b
                P.tensor_tensor(dst[:, :, :], bc(dist[:, k:k + 1], [T, H1, T]), bc(wpos[:, :, k:k + 1], [T, H1, T]),
                                ALU.mult).then_inc(pos_pool, 1)
                n += 1
                pool.wait_ge(pos_pool, n)
                if k > 0:
                    P.tensor_tensor(pos_a[:, :, :], pos_a[:, :, :], pos_b[:, :, :], ALU.add).then_inc(pos_pool, 1)
                    n += 1
                    pool.wait_ge(pos_pool, n)
            P.tensor_tensor(pos_a[:, :, :], pos_a[:, :, :],
                            bc(sm[0:T, BPOS:BPOS + H1].rearrange("p (h t) -> p h t", t=1), [T, H1, T]),
                            ALU.add).then_inc(pos_pool, 1)
            pool.wait_ge(pos_dve, 3)
            P.tensor_tensor(pos_b[:, :, :], pos_a[:, :, :],
                            bc(pos_s[:, 0].rearrange("p (h t) -> p h t", t=1), [T, H1, T]),
                            ALU.subtract).then_inc(pos_pool, 1)

            pipeline(pool, GPSIMD_ORDER, {
                "ln1": norm_root(n1, 1), "ln1_out": lows(n1), "position": residual, "ln2": norm_root(n2, 2),
                "ln2_out": lows(n2), "rope": rope, "proj2b": squares, "rms": rms, "rms_out": lows(n3),
                "router": router, "keep_sum": keep_sum, "keep_h1": keep_h1})


def _split_weights(Wqk, Wv, wq, wk, wv, router_w, w1):
    w = np.zeros((C, NSPLIT), np.float32)
    for t in range(4):
        for j in range(4):
            rows = Wqk[(t // 2) * C + (4 * (t % 2) + j) * D1:][:D1]
            for r in range(3):
                at = QK1 + t * 128 + 32 * j + 8 * r
                w[:, at:at + D1] = rows.T
    w[:, V1C:V1C + C] = Wv.T
    order = (0, 2, 1, 3)
    heads = [wq[h * D2:h * D2 + D2] for h in order] + [wk[:D2], wk[D2:]]
    for n, rows in enumerate(heads):
        w[:, QKV2 + n * D2:QKV2 + n * D2 + D2] = rows.T
        w[:, ROT2 + n * D2:ROT2 + n * D2 + D2] = np.roll(rows, D2 // 2, axis=0).T
    w[:, QKV2 + 96:QKV2 + 128] = wv.T
    w[:, ROUT:ROUT + NE] = router_w.T
    for e in range(NE):
        at = W1C + e // 2 * 3 * HT_ROWS + e % 2 * HID
        w[:, at:at + HID] = w1[e].T
    return np.concatenate([w, w])


def _whole_weights(Wproj, wo, w3):
    f = np.zeros((128, FEND), np.float32)
    for n in range(2):
        f[n * C:n * C + C, WPROJ + n * C:WPROJ + n * C + C] = Wproj.T
        f[n * C:n * C + C, WOUT + n * C:WOUT + n * C + C] = wo.T
    for e in range(NE):
        at = W3C + e // 2 * 3 * HT_ROWS + e % 2 * HID
        f[e % 2 * C:e % 2 * C + C, at:at + HID] = w3[e].T
    return f


def _down_weights(w2):
    d = np.zeros((NPAIR, 3 * HT_ROWS, C), np.float32)
    for e in range(NE):
        d[e // 2, e % 2 * HID:e % 2 * HID + HID] = w2[e].T
    return np.ascontiguousarray(d.reshape(TILES, HT_ROWS, C).transpose(1, 0, 2))


def _patch_weights(weight):
    w = np.zeros((2, HP, PAIRS, C), np.float32)
    taps = weight.reshape(HP, PW, C)
    w[0] = taps[:, 0::2]
    w[1, :, :PW // 2] = taps[:, 1::2]
    w = w.reshape(128, PAIRS, C)
    return w


def _constants():
    k = np.zeros((128, CEND), np.float32)
    k[:, IDENT:IDENT + 128] = np.eye(128)
    k[:, FOLD:FOLD + C] = np.concatenate([np.eye(C)] * 2)
    inv = 1.0 / 10000.0 ** (np.arange(0, D2, 2, dtype=np.float32) / D2)
    freqs = np.outer(np.arange(T, dtype=np.float32), inv)
    cos, sin = np.cos(freqs), np.sin(freqs)
    k[:T, COSC:COSC + 96] = np.tile(np.concatenate([cos, cos], 1), 6)
    k[:T, SINC:SINC + 96] = np.tile(np.concatenate([-sin, sin], 1), 6)
    i = np.arange(TP)
    by_row = np.where(i[None, :] > i[:T, None], -1e30, 0.0)
    by_col = np.pad(np.where(i[None, :T] < i[:T, None], -1e30, 0.0), ((0, 0), (0, 1)))
    k[:T, MROW:MROW + 2 * TP] = np.tile(by_row, 2)
    k[:T, MCOL:MCOL + 2 * TP] = np.tile(by_col, 2)
    e = np.arange(NE)
    k[:, TRI:TRI + NE * NE] = (e[None, :] < e[:, None]).ravel()
    d = (np.arange(T)[None, :] - np.arange(T)[:, None]).astype(np.float32)
    k[:T, DIST:DIST + 3 * T] = np.concatenate([d, np.zeros_like(d), d * d], 1)
    r = np.arange(128) % 32
    k[:, HMASK] = -1.0 * ((r >= 8) & (r < 16))
    k[:, HMASK + 1] = -1.0 * ((r >= 16) & (r < 24)) + ((r == 24) | (r == 25))
    k[:, HMASK + 2] = (r == 24) | (r == 25)
    return k


def kernel(x, cls_tok, L0_tok_weight, L0_tok_bias, L0_attn_Wqk, L0_attn_Wv, L0_attn_Wpos, L0_attn_bpos,
           L0_attn_Wproj, L0_attn_bproj, L0_attn_gating, L0_ffn_ln1_w, L0_ffn_ln2_w, L0_ffn_wq, L0_ffn_wk,
           L0_ffn_wv, L0_ffn_wo, L0_ffn_router_w, L0_ffn_w1, L0_ffn_w2, L0_ffn_w3):
    import concourse.bacc as bacc
    from concourse.bass_utils import run_bass_kernel_spmd

    a = np.asarray
    small = np.concatenate([a(L0_attn_Wpos).ravel(), a(L0_attn_bpos), a(L0_attn_gating), a(L0_attn_bproj),
                            a(cls_tok).ravel()])
    chan = np.stack([a(L0_tok_bias), a(L0_ffn_ln1_w), a(L0_ffn_ln2_w)], 1)
    chan = np.concatenate([chan, chan])
    chan[C:, BPATCH] = 0.0
    arrays = {
        "x": np.ascontiguousarray(a(x)),
        "w_patch": _patch_weights(a(L0_tok_weight)),
        "w_split": _split_weights(*map(a, (L0_attn_Wqk, L0_attn_Wv, L0_ffn_wq, L0_ffn_wk, L0_ffn_wv,
                                           L0_ffn_router_w, L0_ffn_w1))),
        "w_full": _whole_weights(a(L0_attn_Wproj), a(L0_ffn_wo), a(L0_ffn_w3)),
        "w2": _down_weights(a(L0_ffn_w2)),
        "consts": _constants(),
        "small": np.ascontiguousarray(np.broadcast_to(small, (128, SEND))),
        "chan": chan,
    }
    nc = bacc.Bacc("TRN2", target_bir_lowering=False, num_devices=1)
    args = [nc.dram_tensor(f"in_{n}", v.shape, mybir.dt.from_np(v.dtype), kind="ExternalInput").ap()
            for n, v in arrays.items()]
    out = nc.dram_tensor("out_0", (B, T, C), mybir.dt.float32, kind="ExternalOutput").ap()
    build_program(nc, *args, out)
    r = run_bass_kernel_spmd(nc, [{f"in_{n}": v for n, v in arrays.items()}], core_ids=[0])
    return r.results[0]["out_0"]
```
